# Optimizing a Trainium2 kernel written in Bass

```python
import numpy as np
import jax
import jax.numpy as jnp

def _softmax(x, axis=-1):
    return jax.nn.softmax(x, axis=axis)

def _gelu(x):
    return jax.nn.gelu(x, approximate=True)

def _silu(x):
    return jax.nn.silu(x)

def _sigmoid(x):
    return jax.nn.sigmoid(x)

def _layernorm(x, axis=-1, eps=1e-05):
    m = jnp.mean(x, axis=axis, keepdims=True)
    v = jnp.var(x, axis=axis, keepdims=True)
    return (x - m) / jnp.sqrt(v + eps)

def _scatter_add(tgt, idx, src, axis=0):
    return tgt.at[idx].add(src)

def _segment_sum(src, seg, n):
    return jax.ops.segment_sum(src, seg, n)
kernel_name = 'mk_sandwich_d1_jaxref_r8_5f4898'

def setup_inputs(seed: int=0):
    np.random.seed(seed)
    _w = jnp.asarray

    def _L0_attn_setup():
        import jax, jax.numpy as jnp
        import numpy as np
        H, P, G, N, K, CS = (64, 64, 8, 128, 4, 32)
        HID = 256
        INTER = H * P
        CONV_D = INTER + 2 * G * N
        PROJ = INTER + CONV_D + H
        EPS = 1e-05
        key = jax.random.key(seed)
        ks = jax.random.split(key, 4)
        B_, L_ = (2, 256)
        return {'hidden_states': jax.random.normal(ks[0], (B_, L_, HID), jnp.float32), 'in_proj_w': jax.random.normal(ks[1], (PROJ, HID), jnp.float32) * 0.02, 'conv_w': jax.random.normal(ks[2], (CONV_D, K), jnp.float32) * 0.2, 'conv_b': jnp.zeros((CONV_D,), jnp.float32), 'dt_bias': jnp.ones((H,), jnp.float32), 'A_log': jnp.log(jnp.arange(1, H + 1, dtype=jnp.float32)), 'D': jnp.ones((H,), jnp.float32), 'norm_w': jnp.ones((INTER,), jnp.float32), 'out_proj_w': jax.random.normal(ks[3], (HID, INTER), jnp.float32) * 0.02}
    _L0_attn_in = _L0_attn_setup()

    def _L0_ffn_setup():
        import jax, jax.numpy as jnp
        import numpy as np
        B, T, C = (2, 128, 256)
        E, TOPK = (8, 2)
        F_MOE = 176
        F_SHARED = 704
        key = jax.random.key(seed)
        ks = jax.random.split(key, 9)
        s = 0.02
        return {'x': jax.random.normal(ks[0], (B, T, C), dtype=jnp.float32), 'gate_w': jax.random.normal(ks[1], (E, C), dtype=jnp.float32) * s, 'expert_fc1': jax.random.normal(ks[2], (E, F_MOE, C), dtype=jnp.float32) * s, 'expert_fc2': jax.random.normal(ks[3], (E, F_MOE, C), dtype=jnp.float32) * s, 'expert_proj': jax.random.normal(ks[4], (E, C, F_MOE), dtype=jnp.float32) * s, 'shared_fc1': jax.random.normal(ks[5], (F_SHARED, C), dtype=jnp.float32) * s, 'shared_fc2': jax.random.normal(ks[6], (F_SHARED, C), dtype=jnp.float32) * s, 'shared_proj': jax.random.normal(ks[7], (C, F_SHARED), dtype=jnp.float32) * s, 'shared_gate_w': jax.random.normal(ks[8], (1, C), dtype=jnp.float32) * s}
    _L0_ffn_in = _L0_ffn_setup()
    _d = {'L0_attn_hidden_states': _L0_attn_in['hidden_states'], 'L0_attn_in_proj_w': _L0_attn_in['in_proj_w'], 'L0_attn_conv_w': _L0_attn_in['conv_w'], 'L0_attn_conv_b': _L0_attn_in['conv_b'], 'L0_attn_dt_bias': _L0_attn_in['dt_bias'], 'L0_attn_A_log': _L0_attn_in['A_log'], 'L0_attn_D': _L0_attn_in['D'], 'L0_attn_norm_w': _L0_attn_in['norm_w'], 'L0_attn_out_proj_w': _L0_attn_in['out_proj_w'], 'L0_ffn_gate_w': _L0_ffn_in['gate_w'], 'L0_ffn_expert_fc1': _L0_ffn_in['expert_fc1'], 'L0_ffn_expert_fc2': _L0_ffn_in['expert_fc2'], 'L0_ffn_expert_proj': _L0_ffn_in['expert_proj'], 'L0_ffn_shared_fc1': _L0_ffn_in['shared_fc1'], 'L0_ffn_shared_fc2': _L0_ffn_in['shared_fc2'], 'L0_ffn_shared_proj': _L0_ffn_in['shared_proj'], 'L0_ffn_shared_gate_w': _L0_ffn_in['shared_gate_w']}
    _x0 = _d['L0_attn_hidden_states']
    _d['L0_attn_hidden_states'] = jax.random.normal(jax.random.fold_in(jax.random.key(seed), 1), (8, 256, 256), dtype=_x0.dtype)
    del _x0
    return _d

def reference(L0_attn_hidden_states, L0_attn_in_proj_w, L0_attn_conv_w, L0_attn_conv_b, L0_attn_dt_bias, L0_attn_A_log, L0_attn_D, L0_attn_norm_w, L0_attn_out_proj_w, L0_ffn_gate_w, L0_ffn_expert_fc1, L0_ffn_expert_fc2, L0_ffn_expert_proj, L0_ffn_shared_fc1, L0_ffn_shared_fc2, L0_ffn_shared_proj, L0_ffn_shared_gate_w):

    def _L0_attn_ref(hidden_states, in_proj_w, conv_w, conv_b, dt_bias, A_log, D, norm_w, out_proj_w):
        import jax, jax.numpy as jnp
        import numpy as np
        H, P, G, N, K, CS = (64, 64, 8, 128, 4, 32)
        HID = 256
        INTER = H * P
        CONV_D = INTER + 2 * G * N
        PROJ = INTER + CONV_D + H
        EPS = 1e-05
        b, l, _ = hidden_states.shape
        r = H // G
        zxbcdt = hidden_states @ in_proj_w.T
        z = zxbcdt[..., :INTER]
        xBC = zxbcdt[..., INTER:INTER + CONV_D]
        dt = zxbcdt[..., INTER + CONV_D:]
        xp = jnp.pad(xBC, ((0, 0), (K - 1, 0), (0, 0)))
        conv = conv_b
        for i in range(K):
            conv = conv + conv_w[:, i] * xp[:, i:i + l, :]
        xBC = jax.nn.silu(conv)
        x = xBC[..., :INTER]
        Bm = xBC[..., INTER:INTER + G * N]
        Cm = xBC[..., INTER + G * N:]
        dt = jax.nn.softplus(dt + dt_bias)
        A = -jnp.exp(A_log)
        nc = l // CS
        x_c = x.reshape(b, nc, CS, G, r, P)
        dt_c = dt.reshape(b, nc, CS, G, r)
        B_c = Bm.reshape(b, nc, CS, G, N)
        C_c = Cm.reshape(b, nc, CS, G, N)
        dA = dt_c * A.reshape(G, r)
        dA_cs = jnp.cumsum(dA, axis=2)
        diff = dA_cs[:, :, :, None] - dA_cs[:, :, None]
        mask = jnp.tril(jnp.ones((CS, CS), bool))[None, None, :, :, None, None]
        Lmat = jnp.exp(jnp.where(mask, diff, -jnp.inf))
        CB = jnp.einsum('bzign,bzjgn->bzijg', C_c, B_c)
        M = CB[..., None] * Lmat * dt_c[:, :, None]
        Y_diag = jnp.einsum('bzijgr,bzjgrp->bzigrp', M, x_c)
        w = jnp.exp(dA_cs[:, :, -1:] - dA_cs) * dt_c
        states = jnp.einsum('bzjgn,bzjgr,bzjgrp->bzgrpn', B_c, w, x_c)
        chunk_decay = jnp.exp(dA_cs[:, :, -1])

        def step(S, inp):
            d, s = inp
            return (d[..., None, None] * S + s, S)
        init = jnp.zeros((b, G, r, P, N), x.dtype)
        _, prev = jax.lax.scan(step, init, (jnp.moveaxis(chunk_decay, 1, 0), jnp.moveaxis(states, 1, 0)))
        prev = jnp.moveaxis(prev, 0, 1)
        Y_off = jnp.einsum('bzign,bzgrpn->bzigrp', C_c, prev) * jnp.exp(dA_cs)[..., None]
        Y = (Y_diag + Y_off).reshape(b, l, H, P) + D[:, None] * x.reshape(b, l, H, P)
        y = Y.reshape(b, l, INTER)
        var = jnp.mean(y * y, axis=-1, keepdims=True)
        y = norm_w * (y * jax.lax.rsqrt(var + EPS)) * jax.nn.silu(z)
        return y @ out_proj_w.T

    def _L0_ffn_ref(x, gate_w, expert_fc1, expert_fc2, expert_proj, shared_fc1, shared_fc2, shared_proj, shared_gate_w):
        import jax, jax.numpy as jnp
        import numpy as np
        B, T, C = (2, 128, 256)
        E, TOPK = (8, 2)
        F_MOE = 176
        F_SHARED = 704
        b, t, c = x.shape
        xf = x.reshape(-1, c)
        n = xf.shape[0]
        router = xf @ gate_w.T
        probs = jax.nn.softmax(router.astype(jnp.float32), axis=1).astype(x.dtype)
        top_p, top_i = jax.lax.top_k(probs, TOPK)
        combine = jnp.zeros((n, E), dtype=x.dtype).at[jnp.arange(n)[:, None], top_i].set(top_p)
        h1 = jnp.einsum('nc,efc->enf', xf, expert_fc1)
        h2 = jnp.einsum('nc,efc->enf', xf, expert_fc2)
        h = jax.nn.silu(h1) * h2
        out_e = jnp.einsum('enf,ecf->enc', h, expert_proj)
        y = jnp.einsum('ne,enc->nc', combine, out_e)
        s1 = xf @ shared_fc1.T
        s2 = xf @ shared_fc2.T
        shared = jax.nn.silu(s1) * s2 @ shared_proj.T
        y = y + jax.nn.sigmoid(xf @ shared_gate_w.T) * shared
        return y.reshape(b, t, c)
    x = L0_attn_hidden_states
    x = x + _layernorm(_L0_attn_ref(_layernorm(x, axis=-1), L0_attn_in_proj_w, L0_attn_conv_w, L0_attn_conv_b, L0_attn_dt_bias, L0_attn_A_log, L0_attn_D, L0_attn_norm_w, L0_attn_out_proj_w), axis=-1)
    x = x + _layernorm(_L0_ffn_ref(_layernorm(x, axis=-1), L0_ffn_gate_w, L0_ffn_expert_fc1, L0_ffn_expert_fc2, L0_ffn_expert_proj, L0_ffn_shared_fc1, L0_ffn_shared_fc2, L0_ffn_shared_proj, L0_ffn_shared_gate_w), axis=-1)
    return x

_drawn_inputs = setup_inputs


def setup_inputs(seed=0):
    import zlib

    import numpy as np

    out = dict(_drawn_inputs(seed))
    spreads = {'L0_attn_conv_b': (0.0, 0.1),
     'L0_attn_dt_bias': (1.0, 0.6),
     'L0_attn_D': (1.0, 0.2),
     'L0_attn_norm_w': (1.0, 0.2)}
    factors = {'L0_attn_A_log': 8.0}
    for name, (base, spread) in spreads.items():
        noise = np.random.default_rng([zlib.crc32(name.encode()), seed]).standard_normal(out[name].shape)
        drawn = base * np.exp(spread * noise) if base else spread * noise
        out[name] = jnp.asarray(drawn.astype(out[name].dtype))
    for name, factor in factors.items():
        out[name] = (out[name] * factor).astype(out[name].dtype)
    return out
```

```python
import concourse.bass as bass
from concourse import mybir
from contextlib import ExitStack


def mamba_moe_sandwich_kernel(nc, x_d, wx_d, wz_d, wo_d, par_d, wdt_d, dtb_d, alog_d,
                              wf_d, wg_d, sq_const_d, mask_d, tie_d, neg_hot_d, f_hot_d, out_d):
    fp32, f32r, bf16 = mybir.dt.float32, mybir.dt.float32r, mybir.dt.bfloat16
    ALU = mybir.AluOpType
    ACT = mybir.ActivationFunctionType
    AX = mybir.AxisListType

    NBATCH, SEQ, HID = 8, 256, 256
    TOK = NBATCH * SEQ
    TILES = TOK // 128
    KH = HID // 128
    GROUPS, HPG, P = 8, 8, 64
    HEADS = GROUPS * HPG
    CT = HPG * P // 128
    CONVT = CT + 2
    TAPS = 4
    PAIRS = NBATCH // 2
    UT = 2 * SEQ
    PARTS = 3
    LROWS = PARTS * HPG
    DROWS = LROWS + PARTS
    INTER = HEADS * P
    E, ROUTES = 8, 9
    FT = 17
    CROWS = PARTS * ROUTES
    CHUNKS = TOK // UT
    EPS = 1e-5
    NPAR = CONVT * TAPS + CONVT + CT + CT
    PA = CONVT * TAPS + CONVT
    ZBANK = (1, 0, 1, 0)
    BLK = 3

    outer = ExitStack()
    with outer:
        def sem(name):
            return outer.enter_context(nc.semaphore(name))

        def need(eng, s, value):
            if isinstance(value, int) and value <= 0:
                return
            eng.wait_ge(s, value)

        cs_parts = nc.dram_tensor("cs_parts", (GROUPS, LROWS, NBATCH * BLK * 128), bf16, kind="Internal").ap()

        def make_sb(stack):
            return lambda name, shape, dt: stack.enter_context(nc.sbuf_tensor(name, shape, dt))

        sb = make_sb(outer)
        PS = outer.enter_context(nc.psum_tensor("PS", [128, 8, 512], fp32))

        xnT_hi = sb("xnT_hi", [128, KH, TOK], f32r)
        xnT_lo = sb("xnT_lo", [128, KH, TOK], f32r)
        outT = sb("outT", [128, KH, TOK], fp32)
        ident = sb("ident", [128, 128], fp32)
        ssq = sb("ssq", [128, TOK], fp32)
        epsc = sb("epsc", [128, 1], fp32)

        mamba = ExitStack()
        sb = make_sb(mamba)
        dt_sb = sb("dt_sb", [128, TILES, GROUPS, HPG], fp32)
        wraw = sb("wraw", [128, KH * CONVT * 128], fp32)
        praw = sb("praw", [128, NPAR], fp32)
        wx_hi = sb("wx_hi", [128, KH, CONVT * 128], f32r)
        wx_lo = sb("wx_lo", [128, KH, CONVT * 128], f32r)
        wz_hi = sb("wz_hi", [128, KH, CT * 128], f32r)
        wz_lo = sb("wz_lo", [128, KH, CT * 128], f32r)
        wo_hi = sb("wo_hi", [128, CT, HID], f32r)
        wo_lo = sb("wo_lo", [128, CT, HID], f32r)
        mask = sb("mask", [128, BLK * 128], fp32)
        L = sb("L", [DROWS, 2, BLK * 128], bf16)
        R = sb("R", [DROWS, 2, HPG, 256], bf16)
        neg_hot = sb("neg_hot", [DROWS, HPG], fp32)
        wraw_x = wraw[:, :].rearrange("p (k n) -> p k n", k=KH)
        wraw_z = wraw[:, 0:KH * CT * 128].rearrange("p (k n) -> p k n", k=KH)
        wraw_o = wraw[:, 0:CT * HID].rearrange("p (c n) -> p c n", c=CT)

        s0 = ExitStack()
        sb = make_sb(s0)
        umask = sb("umask", [128, 128], fp32)
        sufmask = sb("sufmask", [128, 128], fp32)
        wdt_raw = sb("wdt_raw", [128, KH, HEADS], fp32)
        wdt_hi = sb("wdt_hi", [128, KH, HEADS], f32r)
        wdt_lo = sb("wdt_lo", [128, KH, HEADS], f32r)
        dtb = sb("dtb", [128, HEADS], fp32)
        alog = sb("alog", [128, HEADS], fp32)
        expA = sb("expA", [128, HEADS], fp32)
        st = sb("st", [128, TILES, 6], fp32)
        mv = sb("mv", [128, TILES, 2], fp32)
        std = sb("std", [128, TILES], fp32)
        rstd = sb("rstd", [128, TILES], fp32)
        xn = sb("xn", [128, TILES, HID], fp32)
        dtw = [sb(f"dtw{i}", [128, TILES * HEADS], fp32) for i in range(6)]
        csr = [sb(f"csr{i}", [HEADS, NBATCH * BLK * 128], fp32) for i in range(2)]
        csp = [sb(f"csp{i}", [HEADS, NBATCH * BLK * 128], bf16) for i in range(PARTS)]
        x_v = outT[:, :, :].rearrange("p k t -> p (k t)").rearrange("p (t c) -> p t c", c=HID)
        xd_v = x_d.rearrange("(t p) c -> p t c", p=128)

        s_x0 = [sem(f"s0_x{i}") for i in range(4)]
        s_c0 = sem("s0_const_in")
        s_par = sem("params_in")
        s_raw = sem("weights_in")
        s_stat = sem("s0_stat")
        s_sqrt = sem("s0_sqrt")
        s_rstd = sem("s0_rstd")
        s_xn = sem("s0_xn")
        s_xt = sem("s0_xt")
        s_hi0 = sem("s0_hi")
        s_lo0 = sem("s0_lo")
        s_wdt = sem("s0_wdt")
        s_dtp = sem("s0_dt_psum")
        s_v = sem("s0_softplus_dve")
        s_a = sem("s0_softplus_act")
        s_cs = sem("s0_cs_psum")
        s_p = sem("s0_parts_act")
        s_r = sem("s0_rest_dve")
        s_scr = sem("s0_scratch_out")
        s_ms = sem("s0_memset")
        QT = TILES // 4

        with nc.Block() as block:
            @block.sync
            def _(sp):
                for i in range(4):
                    sp.dma_start(x_v[:, QT * i:QT * i + QT, :], xd_v[:, QT * i:QT * i + QT, :]).then_inc(s_x0[i], 16)
                for dst, src in ((ident, sq_const_d[:, 0:128]), (umask, sq_const_d[:, 128:256]),
                                 (sufmask, sq_const_d[:, 256:384]), (mask, mask_d), (dtb, dtb_d),
                                 (alog, alog_d), (neg_hot, neg_hot_d)):
                    sp.dma_start(dst[:, :], src).then_inc(s_c0, 16)
                sp.dma_start(wdt_raw[:, :, :], wdt_d.rearrange("p (k n) -> p k n", k=KH)).then_inc(s_c0, 16)
                sp.dma_start(praw[:, :], par_d[0, :, :]).then_inc(s_par, 16)
                sp.dma_start(wraw[:, :], wx_d[0, :, :]).then_inc(s_raw, 16)
                sp.wait_ge(s_p, PARTS)
                for i in range(PARTS):
                    for g in range(GROUPS):
                        sp.dma_start(cs_parts[g, HPG * i:HPG * i + HPG, :],
                                     csp[i][HPG * g:HPG * g + HPG, :]).then_inc(s_scr, 16)
                sp.wait_ge(s_scr, 16 * PARTS * GROUPS)

            @block.gpsimd
            def _(pool):
                pool.memset(epsc[:, :], EPS).then_inc(s_ms, 1)
                pool.memset(ssq[:, :], 0.0).then_inc(s_ms, 1)
                pool.memset(L[:, :, :], 1.0).then_inc(s_ms, 1)
                pool.wait_ge(s_xn, 4)
                pool.memset(outT[:, :, :], 0.0).then_inc(s_ms, 1)

            @block.vector
            def _(dve):
                for i in range(4):
                    dve.wait_ge(s_x0[i], 16)
                    for t in range(QT * i, QT * i + QT):
                        ins = dve.bn_stats(st[:, t, :], x_v[:, t, :])
                    ins.then_inc(s_stat, 1)
                    dve.wait_ge(s_stat, 2 * i + 1)
                    for t in range(QT * i, QT * i + QT):
                        ins = dve.bn_aggr(mv[:, t, :], st[:, t, :])
                    ins.then_inc(s_stat, 1)
                for i in range(4):
                    a, b = QT * i, QT * i + QT
                    dve.wait_ge(s_sqrt, i + 1)
                    dve.reciprocal(rstd[:, a:b], std[:, a:b]).then_inc(s_rstd, 1)
                    dve.wait_ge(s_rstd, i + 1)
                    for t in range(a, b):
                        ins = dve.tensor_scalar(xn[:, t, :], x_v[:, t, :], mv[:, t, 0:1], rstd[:, t:t + 1],
                                                ALU.subtract, ALU.mult)
                    ins.then_inc(s_xn, 1)
                dve.wait_ge(s_c0, 16 * 8)
                for i in range(2):
                    dve.tensor_copy(R[:, i, :, :], neg_hot[:, :].unsqueeze(2).to_broadcast([DROWS, HPG, 256]))
                dve.wait_ge(s_wdt, 1)
                dve.tensor_tensor(wdt_lo[:, :, :], wdt_raw[:, :, :], wdt_hi[:, :, :].bitcast(fp32),
                                  ALU.subtract).then_inc(s_wdt, 1)
                for n in range(4 * KH):
                    i, k = n // KH, n % KH
                    dve.wait_ge(s_hi0, n + 1)
                    dve.tensor_tensor(xnT_lo[:, k, 512 * i:512 * i + 512], PS[:, n, :],
                                      xnT_hi[:, k, 512 * i:512 * i + 512].bitcast(fp32),
                                      ALU.subtract).then_inc(s_lo0, 1)
                v, e, w, lnw, r, q = dtw
                dve.wait_ge(s_dtp, 1)
                dve.tensor_tensor(v[:, :].rearrange("p (t h) -> p t h", h=HEADS),
                                  PS[:, 0:2, :].rearrange("p b (t h) -> p (b t) h", h=HEADS),
                                  dtb[:, :].unsqueeze(1).to_broadcast([128, TILES, HEADS]), ALU.add).then_inc(s_v, 1)
                dve.wait_ge(s_a, 2)
                dve.tensor_scalar(w[:, :], e[:, :], 1.0, None, ALU.add).then_inc(s_v, 1)
                dve.wait_ge(s_v, 2)
                dve.scalar_tensor_tensor(r[:, :], w[:, :], -1.0, e[:, :], ALU.add, ALU.subtract).then_inc(s_v, 1)
                dve.reciprocal(q[:, :], w[:, :]).then_inc(s_v, 1)
                dve.wait_ge(s_v, 4)
                dve.tensor_tensor(q[:, :], r[:, :], q[:, :], ALU.mult).then_inc(s_v, 1)
                dve.wait_ge(s_a, 3)
                dve.wait_ge(s_v, 5)
                dve.tensor_tensor(lnw[:, :], lnw[:, :], q[:, :], ALU.subtract).then_inc(s_v, 1)
                dve.wait_ge(s_v, 6)
                dt_flat = dt_sb[:, :, :, :].rearrange("p t g h -> p (t g h)")
                dve.scalar_tensor_tensor(dt_flat, v[:, :], 0.0, lnw[:, :], ALU.max, ALU.add).then_inc(s_v, 1)
                dve.wait_ge(s_v, 7)
                dve.wait_ge(s_a, 4)
                dve.scalar_tensor_tensor(r[:, :].rearrange("p (t h) -> p t h", h=HEADS),
                                         dt_flat.rearrange("p (t h) -> p t h", h=HEADS), -1.0,
                                         expA[:, :].unsqueeze(1).to_broadcast([128, TILES, HEADS]),
                                         ALU.mult, ALU.mult).then_inc(s_v, 1)
                psum = PS[0:HEADS, :, 0:BLK * 128]
                for i in range(PARTS - 1):
                    src = psum if i == 0 else csr[0][:, :].rearrange("p (b n) -> p b n", b=NBATCH)
                    dve.wait_ge(s_p, i + 1)
                    dve.tensor_tensor(csr[i][:, :].rearrange("p (b n) -> p b n", b=NBATCH), src,
                                      csp[i][:, :].rearrange("p (b n) -> p b n", b=NBATCH),
                                      ALU.subtract).then_inc(s_r, 1)
                    if i + 1 < PARTS - 1:
                        dve.wait_ge(s_r, i + 1)

            @block.scalar
            def _(act):
                act.wait_ge(s_ms, 1)
                for i in range(4):
                    act.wait_ge(s_stat, 2 * i + 2)
                    act.activation(std[:, QT * i:QT * i + QT], mv[:, QT * i:QT * i + QT, 1], ACT.Sqrt,
                                   bias=epsc[:, 0:1]).then_inc(s_sqrt, 1)
                act.wait_ge(s_c0, 16 * 8)
                act.activation(wdt_hi[:, :, :], wdt_raw[:, :, :], ACT.Copy).then_inc(s_wdt, 1)
                for n in range(4 * KH):
                    i, k = n // KH, n % KH
                    act.wait_ge(s_xt, n + 1)
                    act.activation(xnT_hi[:, k, 512 * i:512 * i + 512], PS[:, n, :], ACT.Copy).then_inc(s_hi0, 1)
                v, e, w, lnw, r, q = dtw
                act.wait_ge(s_v, 1)
                act.activation(e[:, :], v[:, :], ACT.Abs).then_inc(s_a, 1)
                act.wait_ge(s_a, 1)
                act.activation(e[:, :], e[:, :], ACT.Exp, scale=-1.0).then_inc(s_a, 1)
                act.wait_ge(s_v, 2)
                act.activation(lnw[:, :], w[:, :], ACT.Ln).then_inc(s_a, 1)
                act.activation(expA[:, :], alog[:, :], ACT.Exp).then_inc(s_a, 1)
                act.wait_ge(s_cs, 1)
                act.activation(csp[0][:, :].rearrange("p (b n) -> p b n", b=NBATCH),
                               PS[0:HEADS, :, 0:BLK * 128], ACT.Copy).then_inc(s_p, 1)
                for i in range(1, PARTS):
                    act.wait_ge(s_r, i)
                    act.activation(csp[i][:, :], csr[i - 1][:, :], ACT.Copy).then_inc(s_p, 1)

            @block.tensor
            def _(pe):
                pe.wait_ge(s_c0, 16 * 8)
                for i in range(4):
                    pe.wait_ge(s_xn, i + 1)
                    for k in range(KH):
                        for t in range(QT):
                            mm = pe.transpose(PS[:, KH * i + k, 128 * t:128 * t + 128],
                                              xn[:, QT * i + t, 128 * k:128 * k + 128], ident[:, :])
                        mm.then_inc(s_xt, 1)
                pe.wait_ge(s_wdt, 2)
                pe.wait_ge(s_lo0, 4 * KH)
                for t in range(TILES):
                    n = 0
                    for lhs, rhs in ((xnT_hi, wdt_hi), (xnT_hi, wdt_lo), (xnT_lo, wdt_hi)):
                        for k in range(KH):
                            mm = pe.matmul(PS[:, t // 8, HEADS * (t % 8):HEADS * (t % 8) + HEADS],
                                           lhs[:, k, 128 * t:128 * t + 128], rhs[:, k, :],
                                           start=(n == 0), stop=(n == 3 * KH - 1))
                            n += 1
                mm.then_inc(s_dtp, 1)
                pe.wait_ge(s_v, 8)
                dA = dtw[4]
                for b in range(NBATCH):
                    for blk, (c, m) in enumerate(((0, umask), (0, sufmask), (1, umask))):
                        t = 2 * b + c
                        mm = pe.matmul(PS[0:HEADS, b, 128 * blk:128 * blk + 128],
                                       dA[:, HEADS * t:HEADS * t + HEADS], m[:, :], start=True, stop=True)
                mm.then_inc(s_cs, 1)
        s0.close()

        sb = make_sb(mamba)
        par_a = sb("par_a", [128, PA], fp32)
        par_d_sb = sb("par_d_sb", [128, CT], fp32)
        xT = sb("xT", [128, 2, CT, UT], fp32)
        BC = sb("BC", [128, 2, 2, UT], fp32)
        acc = sb("acc", [128, 3, UT], fp32)
        xdt = sb("xdt", [128, 2, 2, HPG, P], fp32)
        M = sb("M", [128, 2, BLK, HPG, 128], fp32)
        cbm = sb("cbm", [128, BLK * 128], fp32)
        sz = sb("sz", [128, CT, UT], fp32)
        y = sb("y", [128, 2, 2, SEQ], fp32)
        y2 = sb("y2", [128, 2, 2, SEQ], fp32)
        gy = sb("gy", [128, 2, 2, SEQ], fp32)
        g_hi = sb("g_hi", [128, CT, UT], f32r)
        g_lo = sb("g_lo", [128, CT, UT], f32r)

        a_done, z_done, t_done, cb_done = sem("a_done"), sem("z_done"), sem("t_done"), sem("cb_done")
        d_done, yt_done, o_done = sem("decay_done"), sem("yT_done"), sem("proj_done")
        t0_done, xs_done, zs_done = sem("tap3_done"), sem("conv_silu_done"), sem("z_silu_done")
        clamp_done, exp_done = sem("clamp_done"), sem("exp_done")
        sq_done, hi_done = sem("y_squared"), sem("g_hi_done")
        wx_hi_done, wz_hi_done, wo_hi_done, wo_scaled = sem("wx_hi_done"), sem("wz_hi_done"), sem("wo_hi_done"), sem("wo_scaled")
        cbm_done, conv_done, tap_link, m_done = sem("cb_masked"), sem("conv_done"), sem("tap_link"), sem("m_done")
        y_done, xdt_done, oacc_done = sem("y_done"), sem("xdt_done"), sem("proj_added")
        pa_done, pd_done = sem("conv_params_ready"), sem("skip_params_ready")
        ssq_link, gy_done, lo_done = sem("squares_added"), sem("gated_done"), sem("g_lo_done")
        wx_lo_done, wz_lo_done, wo_lo_done = sem("wx_lo_done"), sem("wz_lo_done"), sem("wo_lo_done")
        l_in = [sem(f"l_in{b}") for b in range(2)]
        r_in = [sem(f"r_in{b}") for b in range(2)]

        PT = PS[:, 4, :]
        PY = PS[:, 5, :].rearrange("p (c t) -> p c t", c=2)
        PD = PS[:, 2:4, :]

        def groups(eng, body):
            body(0, False)
            with eng.Fori(1, GROUPS - 1) as g:
                body(g, False)
            body(GROUPS - 1, True)

        with nc.Block() as block:
            @block.sync
            def _(sp):
                def load_lr(g, q, b, bt):
                    need(sp, d_done, BLK * (bt - 2) + BLK)
                    n = 2 * q + b
                    src = cs_parts[g, :, BLK * 128 * n:BLK * 128 * n + BLK * 128]
                    sp.dma_start(L[0:LROWS, b, :], src).then_inc(l_in[b], 16)
                    rows = src.rearrange("(p h) t -> p h t", h=HPG)
                    for c in range(2):
                        sp.dma_start(R[LROWS:DROWS, b, :, 128 * c:128 * c + 128],
                                     rows[:, :, 256 * c:256 * c + 128]).then_inc(r_in[b], 16)

                load_lr(0, 0, 0, 0)
                load_lr(0, 0, 1, 1)
                sp.wait_ge(wx_lo_done, CONVT)
                sp.dma_start(wraw[:, 0:KH * CT * 128], wz_d[0, :, :]).then_inc(s_raw, 16)
                sp.wait_ge(wz_lo_done, CT)
                sp.dma_start(wraw[:, 0:CT * HID], wo_d[0, :, :]).then_inc(s_raw, 16)

                def body(g, last):
                    for q in range(PAIRS):
                        u = PAIRS * g + q
                        for b in range(2):
                            if not (last and q == PAIRS - 1):
                                nq = (q + 1) % PAIRS
                                load_lr(g + 1 if q == PAIRS - 1 else g, nq, b, 2 * u + b + 2)
                            if last:
                                continue
                            if q == 1 and b == 0:
                                sp.wait_ge(wo_lo_done, CT * (g + 1))
                                sp.wait_ge(pd_done, g + 1)
                                sp.dma_start(praw[:, :], par_d[g + 1, :, :]).then_inc(s_par, 16)
                                sp.dma_start(wraw[:, :], wx_d[g + 1, :, :]).then_inc(s_raw, 16)
                            if q == 3 and b == 0:
                                sp.wait_ge(wx_lo_done, CONVT * (g + 2))
                                sp.dma_start(wraw[:, 0:KH * CT * 128], wz_d[g + 1, :, :]).then_inc(s_raw, 16)
                            if q == 3 and b == 1:
                                sp.wait_ge(wz_lo_done, CT * (g + 2))
                                sp.dma_start(wraw[:, 0:CT * HID], wo_d[g + 1, :, :]).then_inc(s_raw, 16)
                groups(sp, body)

            @block.tensor
            def _(pe):
                def in_proj(bank, whi, wlo, c0, q, s):
                    n = 0
                    for lhs, rhs in ((whi, xnT_hi), (whi, xnT_lo), (wlo, xnT_hi)):
                        for k in range(KH):
                            mm = pe.matmul(PS[:, bank, :], lhs[:, k, c0:c0 + 128], rhs[:, k, UT * q:UT * q + UT],
                                           start=(n == 0), stop=(n == 3 * KH - 1))
                            n += 1
                    mm.then_inc(s, 1)

                def conv_in(g, q, v, k, free):
                    need(pe, *free)
                    pe.wait_ge(wx_lo_done, CONVT * g + k + 1)
                    in_proj(k % 2, wx_hi, wx_lo, 128 * k, q, a_done)

                def z_in(g, q, u, ct, free):
                    need(pe, *free)
                    pe.wait_ge(wz_lo_done, CT * g + ct + 1)
                    in_proj(ZBANK[ct], wz_hi, wz_lo, 128 * ct, q, z_done)

                def c_by_b(u, up, b, bt):
                    pe.wait_ge(xs_done, CONVT * u + 2)
                    need(pe, xdt_done, 2 * bt)
                    t = SEQ * b
                    pe.matmul(PT[:, 0:256], BC[:, up, 0, t:t + 128], BC[:, up, 1, t:t + 256],
                              start=True, stop=True)
                    pe.matmul(PT[:, 256:384], BC[:, up, 0, t + 128:t + 256], BC[:, up, 1, t + 128:t + 256],
                              start=True, stop=True).then_inc(cb_done, 1)

                def decay(u, b, bt, blk):
                    if blk == 0:
                        pe.wait_ge(l_in[b], 16 * (u + 1))
                        pe.wait_ge(r_in[b], 32 * (u + 1))
                    need(pe, m_done, BLK * bt + blk)
                    c = min(blk, 1)
                    for hh in range(2):
                        mm = pe.matmul(PS[:, 2 + hh, :], L[:, b, 128 * blk:128 * blk + 128],
                                       R[:, b, 4 * hh:4 * hh + 4, 128 * c:128 * c + 128], start=True, stop=True)
                    mm.then_inc(d_done, 1)

                def turn_x(u, up, b, bt, c):
                    if c == 0:
                        pe.wait_ge(xs_done, CONVT * u + CONVT)
                        pe.wait_ge(cbm_done, bt + 1)
                    else:
                        pe.wait_ge(xdt_done, 2 * bt + 1)
                    t = SEQ * b + 128 * c
                    for ct in range(CT):
                        mm = pe.transpose(PT[:, 128 * ct:128 * ct + 128], xT[:, up, ct, t:t + 128], ident[:, :])
                    mm.then_inc(t_done, 1)

                def y_t(par, bt, half):
                    if half == 0:
                        pe.wait_ge(m_done, BLK * bt + BLK)
                        pe.wait_ge(xdt_done, 2 * bt + 2)
                    need(pe, y_done, 2 * bt + half)
                    for cc in range(2):
                        ct = 2 * half + cc
                        for c in range(2):
                            for s in range(2):
                                h = 2 * ct + s
                                lhs = xdt[:, par, c, h, :]
                                o = PS[P * s:P * s + P, 5, SEQ * cc + 128 * c:SEQ * cc + SEQ]
                                rhs = M[:, par, 0:2, h, :] if c == 0 else M[:, par, 2, h, :]
                                mm = pe.matmul(o, lhs, rhs, start=(c == 0), stop=(c == 1))
                    mm.then_inc(yt_done, 1)

                def project(g, u, ct0):
                    if ct0 == 0:
                        pe.wait_ge(lo_done, 4 * u + 4)
                        pe.wait_ge(wo_lo_done, CT * g + CT)
                        need(pe, oacc_done, u)
                    for ct in (ct0, ct0 + 1):
                        for m in range(KH):
                            for n, (lhs, rhs) in enumerate(((wo_hi, g_hi), (wo_hi, g_lo), (wo_lo, g_hi))):
                                mm = pe.matmul(PS[:, 6 + m, :], lhs[:, ct, 128 * m:128 * m + 128], rhs[:, ct, :],
                                               start=(ct == 0 and n == 0), stop=(ct == CT - 1 and n == 2))
                    if ct0 == 2:
                        mm.then_inc(o_done, 1)

                def body(g, last):
                    for q in range(PAIRS):
                        u = PAIRS * g + q
                        first = isinstance(u, int) and u == 0
                        ahead = not (last and q == PAIRS - 1)
                        gv, qv, v = (g + 1 if q == PAIRS - 1 else g), (q + 1) % PAIRS, u + 1
                        up = q % 2
                        bt = 2 * u
                        done = lambda k, w: (conv_done, CONVT * w + k + 1)
                        zdone = lambda ct: (zs_done, CT * u + ct + 1)
                        if ahead:
                            conv_in(gv, qv, v, 0, done(4, u))
                        c_by_b(u, up, 0, bt)
                        decay(u, 0, bt, 0)
                        if not first:
                            y_t(1, bt - 1, 0)
                        if ahead:
                            conv_in(gv, qv, v, 1, done(5, u))
                        decay(u, 0, bt, 1)
                        if not first:
                            y_t(1, bt - 1, 1)
                        turn_x(u, up, 0, bt, 0)
                        decay(u, 0, bt, 2)
                        if ahead:
                            conv_in(gv, qv, v, 2, done(0, v))
                        turn_x(u, up, 0, bt, 1)
                        z_in(g, q, u, 0, done(1, v) if ahead else done(5, u))
                        z_in(g, q, u, 1, done(2, v) if ahead else done(4, u))
                        z_in(g, q, u, 2, zdone(0))
                        z_in(g, q, u, 3, zdone(1))
                        bt = 2 * u + 1
                        if ahead:
                            conv_in(gv, qv, v, 3, zdone(2))
                        c_by_b(u, up, 1, bt)
                        decay(u, 1, bt, 0)
                        if not first:
                            project(g if q else g - 1, u - 1, 0)
                        if ahead:
                            conv_in(gv, qv, v, 4, zdone(3))
                        decay(u, 1, bt, 1)
                        if not first:
                            project(g if q else g - 1, u - 1, 2)
                        y_t(0, bt - 1, 0)
                        decay(u, 1, bt, 2)
                        if ahead:
                            conv_in(gv, qv, v, 5, done(3, v))
                        y_t(0, bt - 1, 1)
                        turn_x(u, up, 1, bt, 0)
                        turn_x(u, up, 1, bt, 1)

                for k in range(CONVT):
                    conv_in(0, 0, 0, k, (conv_done, k - 1))
                groups(pe, body)
                end = 2 * PAIRS * GROUPS
                y_t(1, end - 1, 0)
                y_t(1, end - 1, 1)
                project(GROUPS - 1, PAIRS * GROUPS - 1, 0)
                project(GROUPS - 1, PAIRS * GROUPS - 1, 2)

            @block.scalar
            def _(act):
                def tap3(g, v, k):
                    n = CONVT * v + k
                    act.wait_ge(a_done, n + 1)
                    act.wait_ge(pa_done, g + 1)
                    need(act, xs_done, n - 2)
                    act.activation(acc[:, k % 3, :], PS[:, k % 2, :], ACT.Identity,
                                   scale=par_a[:, TAPS * k + TAPS - 1:TAPS * k + TAPS],
                                   bias=par_a[:, TAPS * CONVT + k:TAPS * CONVT + k + 1]).then_inc(t0_done, 1)

                def conv_silu(vp, v, k):
                    act.wait_ge(conv_done, CONVT * v + k + 1)
                    if k < 2:
                        need(act, cb_done, 2 * v - 2)
                        dst = BC[:, vp, k, :]
                    else:
                        need(act, y_done, 4 * v - 5 + (k - 2) // 2)
                        dst = xT[:, vp, k - 2, :]
                    act.activation(dst, acc[:, k % 3, :], ACT.Silu).then_inc(xs_done, 1)

                def z_silu(u, ct):
                    act.wait_ge(z_done, CT * u + ct + 1)
                    need(act, gy_done, 4 * u - 1 + ct // 2)
                    act.activation(sz[:, ct, :], PS[:, ZBANK[ct], :], ACT.Silu).then_inc(zs_done, 1)

                def decay_exp(bt, blk):
                    n = BLK * bt + blk
                    act.wait_ge(d_done, n + 1)
                    act.activation(PD, PD, ACT.Relu, scale=-1.0).then_inc(clamp_done, 1)
                    act.wait_ge(clamp_done, n + 1)
                    act.activation(PD, PD, ACT.Exp, scale=-1.0).then_inc(exp_done, 1)

                def square(bt, half):
                    n = 2 * bt + half
                    act.wait_ge(y_done, n + 1)
                    need(act, ssq_link, 2 * n - 2)
                    act.activation(y2[:, half, :, :], y[:, half, :, :], ACT.Square).then_inc(sq_done, 1)

                def gated_hi(u, b, bt, half):
                    n = 2 * bt + half
                    act.wait_ge(gy_done, n + 1)
                    need(act, o_done, u)
                    act.activation(g_hi[:, 2 * half:2 * half + 2, SEQ * b:SEQ * b + SEQ], gy[:, half, :, :],
                                   ACT.Copy).then_inc(hi_done, 1)

                def split_x(g, k):
                    act.wait_ge(s_raw, 48 * g + 16)
                    need(act, a_done, CONVT * PAIRS * g - CONVT + k + 1)
                    act.activation(wx_hi[:, :, 128 * k:128 * k + 128], wraw_x[:, :, 128 * k:128 * k + 128],
                                   ACT.Copy).then_inc(wx_hi_done, 1)

                def split_z(g, ct):
                    act.wait_ge(s_raw, 48 * g + 32)
                    need(act, z_done, CT * PAIRS * g - CT + ct + 1)
                    act.activation(wz_hi[:, :, 128 * ct:128 * ct + 128], wraw_z[:, :, 128 * ct:128 * ct + 128],
                                   ACT.Copy).then_inc(wz_hi_done, 1)

                def split_o(g):
                    act.wait_ge(s_raw, 48 * g + 48)
                    act.wait_ge(s_par, 16 * g + 16)
                    need(act, o_done, PAIRS * g)
                    for ct in range(CT):
                        act.activation(wraw_o[:, ct, :], wraw_o[:, ct, :], ACT.Copy,
                                       scale=praw[:, PA + CT + ct:PA + CT + ct + 1]).then_inc(wo_scaled, 1)
                    for ct in range(CT):
                        act.wait_ge(wo_scaled, CT * g + ct + 1)
                        act.activation(wo_hi[:, ct, :], wraw_o[:, ct, :], ACT.Copy).then_inc(wo_hi_done, 1)

                for k in range(CONVT):
                    split_x(0, k)
                for k in range(CONVT):
                    tap3(0, 0, k)
                    if k >= 2:
                        conv_silu(0, 0, k - 2)
                conv_silu(0, 0, CONVT - 2)
                conv_silu(0, 0, CONVT - 1)
                for ct in range(CT):
                    split_z(0, ct)

                def body(g, last):
                    for q in range(PAIRS):
                        u = PAIRS * g + q
                        first = isinstance(u, int) and u == 0
                        ahead = not (last and q == PAIRS - 1)
                        gv, v, vp = (g + 1 if q == PAIRS - 1 else g), u + 1, (q + 1) % 2
                        bt = 2 * u
                        if ahead:
                            tap3(gv, v, 0)
                        decay_exp(bt, 0)
                        if ahead:
                            tap3(gv, v, 1)
                        decay_exp(bt, 1)
                        if not first:
                            square(bt - 1, 0)
                        decay_exp(bt, 2)
                        if not first:
                            gated_hi(u - 1, 1, bt - 1, 0)
                            square(bt - 1, 1)
                        if ahead:
                            tap3(gv, v, 2)
                        if not first:
                            gated_hi(u - 1, 1, bt - 1, 1)
                        if ahead:
                            conv_silu(vp, v, 0)
                            conv_silu(vp, v, 1)
                        z_silu(u, 0)
                        z_silu(u, 1)
                        if ahead:
                            conv_silu(vp, v, 2)
                        z_silu(u, 2)
                        z_silu(u, 3)
                        if q == 1:
                            split_o(g)
                        if q == 3 and not last:
                            for k in range(3, CONVT):
                                split_x(g + 1, k)
                        bt = 2 * u + 1
                        if ahead:
                            tap3(gv, v, 3)
                        decay_exp(bt, 0)
                        if ahead:
                            tap3(gv, v, 4)
                        decay_exp(bt, 1)
                        if q == 2 and not last:
                            for k in range(3):
                                split_x(g + 1, k)
                        decay_exp(bt, 2)
                        square(bt - 1, 0)
                        if ahead:
                            tap3(gv, v, 5)
                        gated_hi(u, 0, bt - 1, 0)
                        square(bt - 1, 1)
                        gated_hi(u, 0, bt - 1, 1)
                        if ahead:
                            for k in range(3, CONVT):
                                conv_silu(vp, v, k)
                        if q == 3 and not last:
                            for ct in range(CT):
                                split_z(g + 1, ct)
                groups(act, body)
                end = 2 * PAIRS * GROUPS
                for half in range(2):
                    square(end - 1, half)
                    gated_hi(PAIRS * GROUPS - 1, 1, end - 1, half)

            @block.vector
            def _(dve):
                def mask_cb(bt):
                    dve.wait_ge(cb_done, bt + 1)
                    need(dve, m_done, BLK * bt)
                    dve.tensor_tensor(cbm[:, :], PT[:, 0:BLK * 128], mask[:, :], ALU.mult).then_inc(cbm_done, 1)

                def conv(g, v, k):
                    n = CONVT * v + k
                    dve.wait_ge(t0_done, n + 1)
                    dve.wait_ge(pa_done, g + 1)
                    src = PS[:, k % 2, :].rearrange("p (b t) -> p b t", b=2)
                    dst = acc[:, k % 3, :].rearrange("p (b t) -> p b t", b=2)
                    for i, s in enumerate(range(1, TAPS)):
                        if i:
                            dve.wait_ge(tap_link, 2 * n + i)
                        dve.scalar_tensor_tensor(dst[:, :, s:SEQ], src[:, :, 0:SEQ - s],
                                                 par_a[:, TAPS * k + TAPS - 1 - s:TAPS * k + TAPS - s],
                                                 dst[:, :, s:SEQ], ALU.mult, ALU.add)\
                           .then_inc(conv_done if s == TAPS - 1 else tap_link, 1)

                def decay_cb(par, bt, blk):
                    if blk == 0:
                        dve.wait_ge(cbm_done, bt + 1)
                    dve.wait_ge(exp_done, BLK * bt + blk + 1)
                    need(dve, yt_done, 2 * bt - 2)
                    dve.tensor_tensor(M[:, par, blk, :, :], PD.rearrange("p b (h i) -> p (b h) i", i=128),
                                      cbm[:, 128 * blk:128 * blk + 128].unsqueeze(1).to_broadcast([128, HPG, 128]),
                                      ALU.mult).then_inc(m_done, 1)

                def add_skip(g, up, b, bt, half):
                    n = 2 * bt + half
                    dve.wait_ge(yt_done, n + 1)
                    dve.wait_ge(pd_done, g + 1)
                    need(dve, sq_done, n - 1)
                    need(dve, gy_done, n - 1)
                    for cc in range(2):
                        ct = 2 * half + cc
                        ins = dve.scalar_tensor_tensor(y[:, half, cc, :], xT[:, up, ct, SEQ * b:SEQ * b + SEQ],
                                                       par_d_sb[:, ct:ct + 1], PY[:, cc, :], ALU.mult, ALU.add)
                    ins.then_inc(y_done, 1)

                def scale_x(g, q, par, b, bt, c):
                    dve.wait_ge(t_done, 2 * bt + c + 1)
                    need(dve, yt_done, 2 * bt - 2)
                    t = 4 * q + 2 * b + c
                    dve.tensor_tensor(xdt[:, par, c, :, :], PT.rearrange("p (h e) -> p h e", h=HPG),
                                      dt_sb[:, t, g, :].unsqueeze(2).to_broadcast([128, HPG, P]),
                                      ALU.mult).then_inc(xdt_done, 1)

                def add_proj(q, u):
                    dve.wait_ge(o_done, u + 1)
                    for m in range(KH):
                        o = outT[:, m, UT * q:UT * q + UT]
                        ins = dve.tensor_tensor(o, PS[:, 6 + m, :], o, ALU.add)
                    ins.then_inc(oacc_done, 1)

                def conv_params(g):
                    dve.wait_ge(s_par, 16 * g + 16)
                    need(dve, t0_done, CONVT * PAIRS * g)
                    need(dve, conv_done, CONVT * PAIRS * g)
                    dve.tensor_copy(par_a[:, :], praw[:, 0:PA]).then_inc(pa_done, 1)

                def skip_params(g):
                    dve.wait_ge(s_par, 16 * g + 16)
                    need(dve, y_done, 4 * PAIRS * g)
                    dve.tensor_copy(par_d_sb[:, :], praw[:, PA:PA + CT]).then_inc(pd_done, 1)

                conv_params(0)
                for k in range(CONVT):
                    conv(0, 0, k)

                def body(g, last):
                    for q in range(PAIRS):
                        u = PAIRS * g + q
                        first = isinstance(u, int) and u == 0
                        ahead = not (last and q == PAIRS - 1)
                        gv, v = (g + 1 if q == PAIRS - 1 else g), u + 1
                        up = q % 2
                        gy_, upy = (g if q else g - 1), 1 - up
                        bt = 2 * u
                        if q == PAIRS - 1 and ahead:
                            conv_params(g + 1)
                        mask_cb(bt)
                        if ahead:
                            conv(gv, v, 0)
                        decay_cb(0, bt, 0)
                        if not first:
                            add_skip(gy_, upy, 1, bt - 1, 0)
                        if ahead:
                            conv(gv, v, 1)
                        decay_cb(0, bt, 1)
                        if not first:
                            add_skip(gy_, upy, 1, bt - 1, 1)
                        scale_x(g, q, 0, 0, bt, 0)
                        decay_cb(0, bt, 2)
                        if ahead:
                            conv(gv, v, 2)
                        scale_x(g, q, 0, 0, bt, 1)
                        bt = 2 * u + 1
                        if q == 0:
                            skip_params(g)
                        mask_cb(bt)
                        if ahead:
                            conv(gv, v, 3)
                        decay_cb(1, bt, 0)
                        if ahead:
                            conv(gv, v, 4)
                        decay_cb(1, bt, 1)
                        add_skip(g, up, 0, bt - 1, 0)
                        if not first:
                            add_proj((q - 1) % PAIRS, u - 1)
                        decay_cb(1, bt, 2)
                        if ahead:
                            conv(gv, v, 5)
                        add_skip(g, up, 0, bt - 1, 1)
                        scale_x(g, q, 1, 1, bt, 0)
                        scale_x(g, q, 1, 1, bt, 1)
                groups(dve, body)
                end = 2 * PAIRS * GROUPS
                add_skip(GROUPS - 1, 1, 1, end - 1, 0)
                add_skip(GROUPS - 1, 1, 1, end - 1, 1)
                add_proj(PAIRS - 1, PAIRS * GROUPS - 1)

            @block.gpsimd
            def _(pool):
                def gate(u, q, b, bt):
                    for half in range(2):
                        n = 2 * bt + half
                        cts = slice(2 * half, 2 * half + 2)
                        ts = slice(SEQ * b, SEQ * b + SEQ)
                        pool.wait_ge(y_done, n + 1)
                        pool.wait_ge(zs_done, CT * u + 2 * half + 2)
                        need(pool, hi_done, n - 1)
                        need(pool, lo_done, n - 1)
                        pool.tensor_tensor(gy[:, half, :, :], y[:, half, :, :], sz[:, cts, ts],
                                           ALU.mult).then_inc(gy_done, 1)
                        pool.wait_ge(sq_done, n + 1)
                        tok = ssq[:, UT * q + SEQ * b:UT * q + SEQ * b + SEQ]
                        for cc in range(2):
                            need(pool, ssq_link, 2 * n + cc)
                            pool.tensor_tensor(tok, tok, y2[:, half, cc, :], ALU.add).then_inc(ssq_link, 1)
                        pool.wait_ge(hi_done, n + 1)
                        pool.tensor_tensor(g_lo[:, cts, ts], gy[:, half, :, :], g_hi[:, cts, ts].bitcast(fp32),
                                           ALU.subtract).then_inc(lo_done, 1)

                def split_x(g, k):
                    pool.wait_ge(wx_hi_done, CONVT * g + k + 1)
                    n = slice(128 * k, 128 * k + 128)
                    pool.tensor_tensor(wx_lo[:, :, n], wraw_x[:, :, n], wx_hi[:, :, n].bitcast(fp32),
                                       ALU.subtract).then_inc(wx_lo_done, 1)

                def split_z(g, ct):
                    pool.wait_ge(wz_hi_done, CT * g + ct + 1)
                    n = slice(128 * ct, 128 * ct + 128)
                    pool.tensor_tensor(wz_lo[:, :, n], wraw_z[:, :, n], wz_hi[:, :, n].bitcast(fp32),
                                       ALU.subtract).then_inc(wz_lo_done, 1)

                def split_o(g):
                    for ct in range(CT):
                        pool.wait_ge(wo_hi_done, CT * g + ct + 1)
                        pool.tensor_tensor(wo_lo[:, ct, :], wraw_o[:, ct, :], wo_hi[:, ct, :].bitcast(fp32),
                                           ALU.subtract).then_inc(wo_lo_done, 1)

                for k in range(CONVT):
                    split_x(0, k)
                for ct in range(CT):
                    split_z(0, ct)

                def body(g, last):
                    for q in range(PAIRS):
                        u = PAIRS * g + q
                        if not (isinstance(u, int) and u == 0):
                            gate(u - 1, (q - 1) % PAIRS, 1, 2 * u - 1)
                        if q == 1:
                            split_o(g)
                        if q == 3 and not last:
                            for k in range(3, CONVT):
                                split_x(g + 1, k)
                        if q == 2 and not last:
                            for k in range(3):
                                split_x(g + 1, k)
                        gate(u, q, 0, 2 * u)
                        if q == 3 and not last:
                            for ct in range(CT):
                                split_z(g + 1, ct)
                groups(pool, body)
                gate(PAIRS * GROUPS - 1, PAIRS - 1, 1, 2 * PAIRS * GROUPS - 1)

        mamba.close()

        sb = make_sb(outer)
        x1 = sb("x1", [128, TILES, HID], fp32)
        wf_raw = sb("wf_raw", [128, 2, 768], fp32)
        combT = sb("combT", [CROWS, TOK], bf16)
        f_hot = sb("f_hot", [CROWS, FT * 128], bf16)
        st = sb("st_b", [128, TILES, 6], fp32)
        mv = sb("mv_b", [128, TILES, 2], fp32)
        std = sb("std_b", [128, TILES], fp32)
        rstd = sb("rstd_b", [128, TILES], fp32)
        scl = sb("scl", [128, TILES], fp32)
        shf = sb("shf", [128, TILES], fp32)
        s2 = ExitStack()
        sb = make_sb(s2)
        xo = sb("xo", [128, TILES, HID], fp32)
        ones = sb("ones", [128, 1], fp32)
        rn = sb("rn", [128, TILES], fp32)
        v2 = sb("v2", [128, TILES], fp32)
        wg_raw = sb("wg_raw", [128, KH, ROUTES + 1], fp32)
        wg_hi = sb("wg_hi", [128, KH, ROUTES + 1], f32r)
        wg_lo = sb("wg_lo", [128, KH, ROUTES + 1], f32r)
        tie = sb("tie", [128, E * E], fp32)
        hot_raw = sb("hot_raw", [CROWS, FT * 128], fp32)
        ident_b = sb("ident_b", [128, 128], bf16)
        lg = sb("lg", [128, TILES, ROUTES + 1], fp32)
        mx = sb("mx", [128, TILES], fp32)
        pr = sb("pr", [128, TILES, E], fp32)
        sm = sb("sm", [128, TILES], fp32)
        gts = sb("gts", [128, TILES, E, E], fp32)
        eqs = sb("eqs", [128, TILES, E, E], fp32)
        rank = sb("rank", [128, TILES, E], fp32)
        comb = sb("comb", [128, TILES, ROUTES], fp32)
        comb_r = sb("comb_r", [128, TILES, ROUTES], fp32)
        cparts = sb("cparts", [128, TILES, PARTS, ROUTES], bf16)

        def tile_ps(t):
            return PS[:, t // 2, HID * (t % 2):HID * (t % 2) + HID]

        s_in = sem("s2_in")
        s_f = [sem(f"moe_weights_in{i}") for i in range(2)]
        s_on, s_idb, s_var, s_rn = sem("s2_ones"), sem("s2_ident_bf16"), sem("s2_var_psum"), sem("s2_std")
        s_tr, s_d, s_ac = sem("s2_outT_turned"), sem("s2_dve"), sem("s2_act")
        s_xo, s_x1 = sem("s2_scaled"), sem("s2_residual")
        s_st, s_sq, s_n = sem("s2_stat"), sem("s2_sqrt"), sem("s2_normed")
        s_t2, s_h2, s_l2 = sem("s2_xT"), sem("s2_hi"), sem("s2_lo")
        s_g, s_lg, s_e, s_ct, s_cc = sem("s2_gate_w"), sem("s2_logits"), sem("s2_exp"), sem("s2_combT"), sem("s2_combT_copy")
        s_q, s_cp = sem("s2_route_dve"), sem("s2_route_parts")
        s_xn2, s_rs2 = sem("s2_norm_squared"), sem("s2_rstd")

        with nc.Block() as block:
            @block.sync
            def _(sp):
                for dst, src in ((x1[:, :, :], xd_v), (wg_raw[:, :, :], wg_d.rearrange("p (k n) -> p k n", k=KH)),
                                 (tie[:, :], tie_d), (hot_raw[:, :], f_hot_d)):
                    sp.dma_start(dst, src).then_inc(s_in, 16)
                for f in range(2):
                    sp.dma_start(wf_raw[:, f, :], wf_d[f, :, :]).then_inc(s_f[f], 16)

            @block.gpsimd
            def _(pool):
                pool.memset(ones[:, :], 1.0).then_inc(s_on, 1)
                pool.wait_ge(s_tr, TILES // 2)
                pool.memset(outT[:, :, :], 0.0)

            @block.tensor
            def _(pe):
                pe.wait_ge(s_on, 1)
                for t in range(TILES):
                    mm = pe.matmul(PS[:, 7, t:t + 1], ssq[:, 128 * t:128 * t + 128], ones[:, :], start=True, stop=True)
                mm.then_inc(s_var, 1)
                for t in range(TILES):
                    if t == 14:
                        pe.wait_ge(s_rn, 1)
                    for k in range(KH):
                        mm = pe.transpose(PS[:, t // 2, HID * (t % 2) + 128 * k:HID * (t % 2) + 128 * k + 128],
                                          outT[:, k, 128 * t:128 * t + 128], ident[:, :])
                    if t % 2:
                        mm.then_inc(s_tr, 1)
                pe.wait_ge(s_xo, TILES)
                for i in range(4):
                    pe.wait_ge(s_n, i + 1)
                    for k in range(KH):
                        for t in range(QT):
                            mm = pe.transpose(PS[:, KH * i + k, 128 * t:128 * t + 128],
                                              xo[:, QT * i + t, 128 * k:128 * k + 128], ident[:, :])
                        mm.then_inc(s_t2, 1)
                pe.wait_ge(s_g, 2)
                pe.wait_ge(s_l2, 4 * KH)
                for t in range(TILES):
                    n = 0
                    for lhs, rhs in ((xnT_hi, wg_hi), (xnT_hi, wg_lo), (xnT_lo, wg_hi)):
                        for k in range(KH):
                            mm = pe.matmul(PS[:, 0, (ROUTES + 1) * t:(ROUTES + 1) * (t + 1)],
                                           lhs[:, k, 128 * t:128 * t + 128], rhs[:, k, :],
                                           start=(n == 0), stop=(n == 3 * KH - 1))
                            n += 1
                mm.then_inc(s_lg, 1)
                pe.wait_ge(s_cp, PARTS)
                pe.wait_ge(s_idb, 1)
                cps = PS[0:CROWS, 1:3, :].bitcast(bf16).rearrange("p b t -> p (b t)")
                for t in range(TILES):
                    mm = pe.transpose(cps[:, 128 * t:128 * t + 128],
                                      cparts[:, t, :, :].rearrange("p a r -> p (a r)"), ident_b[:, :])
                mm.then_inc(s_ct, 1)

            @block.scalar
            def _(act):
                act.wait_ge(s_var, 1)
                act.activation(std[:, :], PS[:, 7, 0:TILES], ACT.Sqrt, scale=1.0 / INTER, bias=epsc[:, 0:1]).then_inc(s_rn, 1)
                act.wait_ge(s_d, 3)
                act.activation(std[:, :], v2[:, :], ACT.Sqrt, bias=epsc[:, 0:1]).then_inc(s_ac, 1)
                act.wait_ge(s_d, 6)
                for t in range(TILES):
                    act.activation(xo[:, t, :], tile_ps(t), ACT.Identity, scale=scl[:, t:t + 1],
                                   bias=shf[:, t:t + 1]).then_inc(s_xo, 1)
                for i in range(4):
                    act.wait_ge(s_st, 2 * i + 2)
                    act.activation(std[:, QT * i:QT * i + QT], mv[:, QT * i:QT * i + QT, 1], ACT.Sqrt,
                                   bias=epsc[:, 0:1]).then_inc(s_sq, 1)
                act.wait_ge(s_in, 16 * 4)
                act.activation(wg_hi[:, :, :], wg_raw[:, :, :], ACT.Copy).then_inc(s_g, 1)
                for n in range(4 * KH):
                    i, k = n // KH, n % KH
                    act.wait_ge(s_t2, n + 1)
                    act.activation(xnT_hi[:, k, 512 * i:512 * i + 512], PS[:, n, :], ACT.Copy).then_inc(s_h2, 1)
                act.wait_ge(s_q, 3)
                act.activation(pr[:, :, :], pr[:, :, :], ACT.Exp).then_inc(s_e, 1)
                act.activation(sm[:, :], lg[:, :, E], ACT.Exp, scale=-1.0).then_inc(s_e, 1)

            @block.vector
            def _(dve):
                dve.tensor_copy(ident_b[:, :], ident[:, :]).then_inc(s_idb, 1)
                dve.wait_ge(s_rn, 1)
                dve.reciprocal(rn[:, :], std[:, :]).then_inc(s_d, 1)
                for i in range(TILES // 2):
                    dve.wait_ge(s_tr, i + 1)
                    for t in (2 * i, 2 * i + 1):
                        ins = dve.bn_stats(st[:, t, :], tile_ps(t))
                ins.then_inc(s_d, 1)
                dve.wait_ge(s_d, 2)
                for t in range(TILES):
                    ins = dve.bn_aggr(mv[:, t, :], st[:, t, :])
                dve.tensor_tensor(v2[:, :], rn[:, :], rn[:, :], ALU.mult).then_inc(s_xn2, 1)
                dve.wait_ge(s_xn2, 1)
                dve.tensor_tensor(v2[:, :], v2[:, :], mv[:, :, 1], ALU.mult).then_inc(s_d, 1)
                dve.wait_ge(s_ac, 1)
                dve.reciprocal(rstd[:, :], std[:, :]).then_inc(s_d, 1)
                dve.wait_ge(s_d, 4)
                dve.tensor_tensor(scl[:, :], rstd[:, :], rn[:, :], ALU.mult).then_inc(s_d, 1)
                dve.wait_ge(s_d, 5)
                dve.scalar_tensor_tensor(shf[:, :], mv[:, :, 0], -1.0, scl[:, :], ALU.mult, ALU.mult).then_inc(s_d, 1)
                dve.wait_ge(s_in, 16 * 4)
                for i in range(4):
                    a, b = QT * i, QT * i + QT
                    dve.wait_ge(s_xo, b)
                    dve.tensor_tensor(x1[:, a:b, :], x1[:, a:b, :], xo[:, a:b, :], ALU.add).then_inc(s_x1, 1)
                    dve.wait_ge(s_x1, i + 1)
                    for t in range(a, b):
                        ins = dve.bn_stats(st[:, t, :], x1[:, t, :])
                    ins.then_inc(s_st, 1)
                    dve.wait_ge(s_st, 2 * i + 1)
                    for t in range(a, b):
                        ins = dve.bn_aggr(mv[:, t, :], st[:, t, :])
                    ins.then_inc(s_st, 1)
                for i in range(4):
                    a, b = QT * i, QT * i + QT
                    dve.wait_ge(s_sq, i + 1)
                    dve.reciprocal(rstd[:, a:b], std[:, a:b]).then_inc(s_rs2, 1)
                    dve.wait_ge(s_rs2, i + 1)
                    for t in range(a, b):
                        ins = dve.tensor_scalar(xo[:, t, :], x1[:, t, :], mv[:, t, 0:1], rstd[:, t:t + 1],
                                                ALU.subtract, ALU.mult)
                    ins.then_inc(s_n, 1)
                dve.wait_ge(s_g, 1)
                dve.tensor_tensor(wg_lo[:, :, :], wg_raw[:, :, :], wg_hi[:, :, :].bitcast(fp32),
                                  ALU.subtract).then_inc(s_g, 1)
                dve.tensor_copy(f_hot[:, :], hot_raw[:, :])
                for n in range(4 * KH):
                    i, k = n // KH, n % KH
                    dve.wait_ge(s_h2, n + 1)
                    dve.tensor_tensor(xnT_lo[:, k, 512 * i:512 * i + 512], PS[:, n, :],
                                      xnT_hi[:, k, 512 * i:512 * i + 512].bitcast(fp32),
                                      ALU.subtract).then_inc(s_l2, 1)
                dve.wait_ge(s_lg, 1)
                dve.tensor_copy(lg[:, :, :], PS[:, 0, 0:TILES * (ROUTES + 1)].rearrange("p (t r) -> p t r", t=TILES)).then_inc(s_q, 1)
                dve.wait_ge(s_q, 1)
                dve.tensor_reduce(mx[:, :], lg[:, :, 0:E], AX.X, ALU.max).then_inc(s_q, 1)
                dve.wait_ge(s_q, 2)
                dve.tensor_tensor(pr[:, :, :], lg[:, :, 0:E], mx[:, :].unsqueeze(2).to_broadcast([128, TILES, E]),
                                  ALU.subtract).then_inc(s_q, 1)
                dve.wait_ge(s_e, 1)
                dve.tensor_reduce(mx[:, :], pr[:, :, :], AX.X, ALU.add).then_inc(s_q, 1)
                dve.wait_ge(s_e, 2)
                dve.tensor_scalar(sm[:, :], sm[:, :], 1.0, None, ALU.add).then_inc(s_q, 1)
                dve.wait_ge(s_q, 5)
                dve.reciprocal(mx[:, :], mx[:, :]).then_inc(s_q, 1)
                dve.reciprocal(comb[:, :, E], sm[:, :]).then_inc(s_q, 1)
                dve.wait_ge(s_q, 7)
                dve.tensor_tensor(pr[:, :, :], pr[:, :, :], mx[:, :].unsqueeze(2).to_broadcast([128, TILES, E]),
                                  ALU.mult).then_inc(s_q, 1)
                dve.wait_ge(s_q, 8)
                full = [128, TILES, E, E]
                other = pr[:, :, :].unsqueeze(2).to_broadcast(full)
                own = pr[:, :, :].unsqueeze(3).to_broadcast(full)
                before = tie[:, :].rearrange("p (e o) -> p e o", e=E).unsqueeze(1).to_broadcast(full)
                dve.tensor_tensor(gts[:, :, :, :], other, own, ALU.is_gt).then_inc(s_q, 1)
                dve.tensor_tensor(eqs[:, :, :, :], other, own, ALU.is_equal).then_inc(s_q, 1)
                dve.wait_ge(s_q, 10)
                dve.tensor_tensor(eqs[:, :, :, :], eqs[:, :, :, :], before, ALU.mult).then_inc(s_q, 1)
                dve.wait_ge(s_q, 11)
                dve.tensor_tensor(gts[:, :, :, :], gts[:, :, :, :], eqs[:, :, :, :], ALU.add).then_inc(s_q, 1)
                dve.wait_ge(s_q, 12)
                dve.tensor_reduce(rank[:, :, :], gts[:, :, :, :], AX.X, ALU.add).then_inc(s_q, 1)
                dve.wait_ge(s_q, 13)
                dve.scalar_tensor_tensor(comb[:, :, 0:E], rank[:, :, :], 2.0, pr[:, :, :], ALU.is_lt,
                                         ALU.mult).then_inc(s_q, 1)
                dve.wait_ge(s_q, 14)
                src = comb
                for i in range(PARTS):
                    dve.tensor_copy(cparts[:, :, i, :], src[:, :, :]).then_inc(s_cp, 1)
                    if i < PARTS - 1:
                        dve.wait_ge(s_cp, i + 1)
                        dve.tensor_tensor(comb_r[:, :, :], src[:, :, :], cparts[:, :, i, :], ALU.subtract).then_inc(s_q, 1)
                        dve.wait_ge(s_q, 15 + i)
                        src = comb_r
                dve.wait_ge(s_ct, 1)
                dve.tensor_copy(combT[:, :], PS[0:CROWS, 1:3, :].bitcast(bf16).rearrange("p b t -> p (b t)"))
        s2.close()

        s3 = ExitStack()
        sb = make_sb(s3)
        wf_hi = sb("wf_hi", [128, 2, 768], f32r)
        wf_lo = sb("wf_lo", [128, 2, 768], f32r)
        sl = sb("sl", [128, 2, UT], fp32)
        hm = sb("hm", [128, 2, UT], fp32)
        hc = sb("hc", [128, 2, UT], fp32)
        h_hi = sb("h_hi", [128, CHUNKS, UT], f32r)
        h_lo = sb("h_lo", [128, CHUNKS, UT], f32r)
        f1_done, f2_done, p_done = sem("fc1_done"), sem("fc2_done"), sem("moe_proj_done")
        sl_done, hhi_done, wfh_done = sem("fc1_silu_done"), sem("h_hi_done"), sem("moe_w_hi_done")
        hm_done, hc_done, fa_done = sem("h_done"), sem("h_scaled"), sem("moe_proj_added")
        hlo_done, wfl_done = sem("h_lo_done"), sem("moe_w_lo_done")

        def hidden_tiles(eng, body):
            body(0, 0, 0, False)
            with eng.Fori(0, (FT - 3) // 2) as i:
                body(2 * i + 1, i, 1, False)
                body(2 * i + 2, i + 1, 0, False)
            body(FT - 2, (FT - 2) // 2, 1, False)
            body(FT - 1, (FT - 1) // 2, 0, True)

        with nc.Block() as block:
            @block.sync
            def _(sp):
                def body(f, pair, par, last):
                    if last or (isinstance(f, int) and f == FT - 2):
                        return
                    sp.wait_ge(wfl_done, f + 1)
                    sp.dma_start(wf_raw[:, par, :], wf_d[f + 2, :, :]).then_inc(s_f[par], 16)
                hidden_tiles(sp, body)

            @block.tensor
            def _(pe):
                def hidden(f, par, c, which, bank, s):
                    n = 0
                    for whl, xhl in ((wf_hi, xnT_hi), (wf_hi, xnT_lo), (wf_lo, xnT_hi)):
                        for k in range(KH):
                            w0 = 256 * k + 128 * which
                            mm = pe.matmul(PS[:, bank, :], whl[:, par, w0:w0 + 128], xhl[:, k, UT * c:UT * c + UT],
                                           start=(n == 0), stop=(n == 3 * KH - 1))
                            n += 1
                    if s is not None:
                        mm.then_inc(s, 1)

                def project(j, par, c):
                    pe.wait_ge(hlo_done, j + 1)
                    need(pe, fa_done, j)
                    for m in range(KH):
                        w0 = 512 + 128 * m
                        for n, (whl, hhl) in enumerate(((wf_hi, h_hi), (wf_hi, h_lo), (wf_lo, h_hi))):
                            mm = pe.matmul(PS[:, 6 + m, :], whl[:, par, w0:w0 + 128], hhl[:, c, :],
                                           start=(n == 0), stop=(n == 2))
                    mm.then_inc(p_done, 1)

                def body(f, pair, par, last):
                    pe.wait_ge(wfl_done, f + 1)
                    for c in range(CHUNKS):
                        j = CHUNKS * f + c
                        need(pe, hc_done, j - 1)
                        hidden(f, par, c, 0, c % 2, f1_done)
                        hidden(f, par, c, 1, 2 + c % 2, None)
                        if isinstance(f, int):
                            hot = f_hot[:, 128 * f:128 * f + 128]
                        else:
                            hot = f_hot[:, bass.ds(128 * f, 128)]
                        pe.matmul(PS[:, 4 + c % 2, :], hot, combT[:, UT * c:UT * c + UT],
                                  start=True, stop=True).then_inc(f2_done, 1)
                        if not (isinstance(j, int) and j < 2):
                            project(j - 2, par if c >= 2 else 1 - par, (c - 2) % CHUNKS)
                hidden_tiles(pe, body)
                end = CHUNKS * FT
                project(end - 2, 0, CHUNKS - 2)
                project(end - 1, 0, CHUNKS - 1)

            @block.scalar
            def _(act):
                def split(f, pair, par):
                    act.wait_ge(s_f[par], 16 * (pair + 1))
                    need(act, p_done, CHUNKS * (f - 1))
                    act.activation(wf_hi[:, par, :], wf_raw[:, par, :], ACT.Copy).then_inc(wfh_done, 1)

                split(0, 0, 0)

                def high(j, c):
                    act.wait_ge(hc_done, j + 1)
                    need(act, p_done, j - 3)
                    act.activation(h_hi[:, c, :], hc[:, c % 2, :], ACT.Copy).then_inc(hhi_done, 1)

                def body(f, pair, par, last):
                    for c in range(CHUNKS):
                        j = CHUNKS * f + c
                        act.wait_ge(f1_done, j + 1)
                        need(act, hm_done, j - 1)
                        act.activation(sl[:, c % 2, :], PS[:, c % 2, :], ACT.Silu).then_inc(sl_done, 1)
                        high(j, c)
                        if c == 2 and not last:
                            split(f + 1, pair + par, 1 - par)
                hidden_tiles(act, body)

            @block.vector
            def _(dve):
                def add_up(j, c):
                    dve.wait_ge(p_done, j + 1)
                    o = outT[:, :, UT * c:UT * c + UT]
                    dve.tensor_tensor(o, PS[:, 6:8, :], o, ALU.add).then_inc(fa_done, 1)

                def body(f, pair, par, last):
                    for c in range(CHUNKS):
                        j = CHUNKS * f + c
                        dve.wait_ge(sl_done, j + 1)
                        dve.wait_ge(f2_done, j + 1)
                        dve.tensor_tensor(hm[:, c % 2, :], PS[:, 2 + c % 2, :], sl[:, c % 2, :], ALU.mult).then_inc(hm_done, 1)
                        dve.wait_ge(hm_done, j + 1)
                        need(dve, hlo_done, j - 1)
                        dve.tensor_tensor(hc[:, c % 2, :], PS[:, 4 + c % 2, :], hm[:, c % 2, :], ALU.mult).then_inc(hc_done, 1)
                        if not (isinstance(j, int) and j < 2):
                            add_up(j - 2, (c - 2) % CHUNKS)
                hidden_tiles(dve, body)
                end = CHUNKS * FT
                add_up(end - 2, CHUNKS - 2)
                add_up(end - 1, CHUNKS - 1)

            @block.gpsimd
            def _(pool):
                def split(f, pair, par):
                    pool.wait_ge(wfh_done, f + 1)
                    pool.tensor_tensor(wf_lo[:, par, :], wf_raw[:, par, :], wf_hi[:, par, :].bitcast(fp32),
                                       ALU.subtract).then_inc(wfl_done, 1)

                split(0, 0, 0)

                def body(f, pair, par, last):
                    for c in range(CHUNKS):
                        j = CHUNKS * f + c
                        pool.wait_ge(hhi_done, j + 1)
                        pool.tensor_tensor(h_lo[:, c, :], hc[:, c % 2, :], h_hi[:, c, :].bitcast(fp32),
                                           ALU.subtract).then_inc(hlo_done, 1)
                        if c == 2 and not last:
                            split(f + 1, pair + par, 1 - par)
                hidden_tiles(pool, body)
        s3.close()

        sb = make_sb(outer)
        res = sb("res", [128, TILES, HID], fp32)
        s_tr4, s_d4, s_a4, s_o4, s_out = sem("s4_turned"), sem("s4_dve"), sem("s4_act"), sem("s4_sum"), sem("s4_out")
        s_sc4 = sem("s4_scaled")
        out_v = out_d.rearrange("(t p) c -> p t c", p=128)

        with nc.Block() as block:
            @block.tensor
            def _(pe):
                for t in range(TILES):
                    for k in range(KH):
                        mm = pe.transpose(PS[:, t // 2, HID * (t % 2) + 128 * k:HID * (t % 2) + 128 * k + 128],
                                          outT[:, k, 128 * t:128 * t + 128], ident[:, :])
                    if t % 2:
                        mm.then_inc(s_tr4, 1)

            @block.vector
            def _(dve):
                for i in range(4):
                    a, b = QT * i, QT * i + QT
                    for t in range(a, b):
                        dve.wait_ge(s_tr4, t // 2 + 1)
                        ins = dve.bn_stats(st[:, t, :], tile_ps(t))
                    ins.then_inc(s_d4, 1)
                    dve.wait_ge(s_d4, 4 * i + 1)
                    for t in range(a, b):
                        ins = dve.bn_aggr(mv[:, t, :], st[:, t, :])
                    ins.then_inc(s_d4, 1)
                    dve.wait_ge(s_a4, i + 1)
                    dve.reciprocal(rstd[:, a:b], std[:, a:b]).then_inc(s_d4, 1)
                    dve.wait_ge(s_d4, 4 * i + 3)
                    dve.scalar_tensor_tensor(shf[:, a:b], mv[:, a:b, 0], -1.0, rstd[:, a:b], ALU.mult,
                                             ALU.mult).then_inc(s_d4, 1)
                    dve.wait_ge(s_sc4, b)
                    dve.tensor_tensor(res[:, a:b, :], res[:, a:b, :], x1[:, a:b, :], ALU.add).then_inc(s_o4, 1)

            @block.scalar
            def _(act):
                for i in range(4):
                    a, b = QT * i, QT * i + QT
                    act.wait_ge(s_d4, 4 * i + 2)
                    act.activation(std[:, a:b], mv[:, a:b, 1], ACT.Sqrt, bias=epsc[:, 0:1]).then_inc(s_a4, 1)
                    act.wait_ge(s_d4, 4 * i + 4)
                    for t in range(a, b):
                        act.activation(res[:, t, :], tile_ps(t), ACT.Identity, scale=rstd[:, t:t + 1],
                                       bias=shf[:, t:t + 1]).then_inc(s_sc4, 1)

            @block.sync
            def _(sp):
                for i in range(4):
                    a, b = QT * i, QT * i + QT
                    sp.wait_ge(s_o4, i + 1)
                    sp.dma_start(out_v[:, a:b, :], res[:, a:b, :]).then_inc(s_out, 16)
                sp.wait_ge(s_out, 16 * 4)


def kernel(L0_attn_hidden_states, L0_attn_in_proj_w, L0_attn_conv_w, L0_attn_conv_b, L0_attn_dt_bias,
           L0_attn_A_log, L0_attn_D, L0_attn_norm_w, L0_attn_out_proj_w, L0_ffn_gate_w, L0_ffn_expert_fc1,
           L0_ffn_expert_fc2, L0_ffn_expert_proj, L0_ffn_shared_fc1, L0_ffn_shared_fc2, L0_ffn_shared_proj,
           L0_ffn_shared_gate_w):
    import numpy as np
    import concourse.bacc as bacc
    from concourse import mybir as mb
    from concourse.bass_utils import run_bass_kernel_spmd

    G, CT, HID, INTER, GN, H = 8, 4, 256, 4096, 1024, 64
    E, F, FS, FT = 8, 176, 704, 17
    a = np.asarray
    x = a(L0_attn_hidden_states).reshape(-1, HID)
    w = a(L0_attn_in_proj_w)
    wz, wx, wB, wC, wdt = (w[i:j] for i, j in ((0, INTER), (INTER, 2 * INTER), (2 * INTER, 2 * INTER + GN),
                                               (2 * INTER + GN, 2 * INTER + 2 * GN), (2 * INTER + 2 * GN, w.shape[0])))

    def by_group(bcx, *rest):
        B, C, X = bcx
        return np.concatenate([v.reshape(G, -1, *rest) for v in (B, C, X)], axis=1)

    def k_major(v):
        n = v.shape[1]
        return v.transpose(0, 2, 1).reshape(v.shape[0], 2, 128, n).transpose(0, 2, 1, 3).reshape(v.shape[0], 128, 2 * n)

    cw, cb = a(L0_attn_conv_w), a(L0_attn_conv_b)
    bcx = lambda v: (v[INTER:INTER + GN], v[INTER + GN:], v[:INTER])
    tiles = lambda v, n: v.reshape(G, n, 128, -1).transpose(0, 2, 1, 3).reshape(G, 128, -1)
    par = np.concatenate([tiles(by_group(bcx(cw), 4), CT + 2), tiles(by_group(bcx(cb)), CT + 2),
                          tiles(np.repeat(a(L0_attn_D), INTER // H), CT), tiles(a(L0_attn_norm_w), CT)], axis=2)
    wo = a(L0_attn_out_proj_w).T.reshape(G, CT, 128, HID).transpose(0, 2, 1, 3).reshape(G, 128, CT * HID)
    pad = np.zeros((FT * 128 - E * F - FS, HID), np.float32)
    fc = [np.concatenate([a(e).reshape(E * F, HID), a(s), pad]).reshape(FT, 128, 2, 128) for e, s in
          ((L0_ffn_expert_fc1, L0_ffn_shared_fc1), (L0_ffn_expert_fc2, L0_ffn_shared_fc2))]
    w12 = np.stack(fc, axis=3).transpose(0, 4, 2, 3, 1).reshape(FT, 128, 512)
    wp = np.concatenate([a(L0_ffn_expert_proj).transpose(0, 2, 1).reshape(E * F, HID), a(L0_ffn_shared_proj).T, pad])
    wf = np.concatenate([w12, wp.reshape(FT, 128, HID)], axis=2)
    wg = np.concatenate([a(L0_ffn_gate_w), a(L0_ffn_shared_gate_w), np.zeros((1, HID), np.float32)])

    one = lambda v: np.asarray(v, np.float32)
    i, j = np.arange(128)[None, :], np.arange(128)[:, None]
    upper = one(j <= i)
    squares = np.concatenate([one(i == j), upper, -one(j > i)], axis=1)
    mask = np.concatenate([upper, np.ones((128, 128), np.float32), upper], axis=1)
    tie = np.tile(one(np.arange(E)[None, :] < np.arange(E)[:, None]).reshape(1, -1), (128, 1))
    neg_hot = np.concatenate([np.tile(-np.eye(8, dtype=np.float32), (3, 1)), np.zeros((3, 8), np.float32)])
    route = np.concatenate([np.repeat(np.arange(E), F), np.full(FT * 128 - E * F, E)])
    f_hot = np.tile(one(np.arange(E + 1)[:, None] == route[None, :]), (3, 1))

    ins = dict(x=x, wx=k_major(by_group(bcx(np.concatenate([wx, wB, wC])), HID)), wz=k_major(wz.reshape(G, -1, HID)),
               wo=wo, par=par, wdt=k_major(wdt[None])[0], dtb=np.tile(a(L0_attn_dt_bias), (128, 1)),
               alog=np.tile(a(L0_attn_A_log), (128, 1)), wf=wf, wg=k_major(wg[None])[0], squares=squares, mask=mask,
               tie=tie, neg_hot=neg_hot, f_hot=f_hot)
    nc = bacc.Bacc("TRN2", target_bir_lowering=False, num_devices=1)
    arrays, aps = {}, []
    for name, v in ins.items():
        v = np.ascontiguousarray(v)
        arrays[f"in_{name}"] = v
        aps.append(nc.dram_tensor(f"in_{name}", v.shape, mb.dt.from_np(v.dtype), kind="ExternalInput").ap())
    aps.append(nc.dram_tensor("out", x.shape, mb.dt.float32, kind="ExternalOutput").ap())
    mamba_moe_sandwich_kernel(nc, *aps)
    r = run_bass_kernel_spmd(nc, [arrays], core_ids=[0])
    return r.results[0]["out"].reshape(a(L0_attn_hidden_states).shape)
```

```python
import concourse.bass as bass
from concourse import mybir
from contextlib import ExitStack


def mamba_moe_sandwich_kernel(nc, x_d, wx_d, wz_d, wo_d, par_d, wdt_d, dtb_d, alog_d,
                              wf_d, wg_d, sq_const_d, mask_d, tie_d, l_const_d, r_const_d, f_hot_d, out_d):
    fp32, f32r, bf16 = mybir.dt.float32, mybir.dt.float32r, mybir.dt.bfloat16
    ALU = mybir.AluOpType
    ACT = mybir.ActivationFunctionType
    AX = mybir.AxisListType

    NBATCH, SEQ, HID = 8, 256, 256
    TOK = NBATCH * SEQ
    TILES = TOK // 128
    KH = HID // 128
    GROUPS, HPG, P = 8, 8, 64
    HEADS = GROUPS * HPG
    CT = HPG * P // 128
    CONVT = CT + 2
    TAPS = 4
    PAIRS = NBATCH // 2
    UT = 2 * SEQ
    PARTS = 3
    LROWS = PARTS * HPG
    SUMS = LROWS + PARTS
    DROWS = SUMS + 64
    INTER = HEADS * P
    E, ROUTES = 8, 9
    FT = 17
    CROWS = PARTS * ROUTES
    CHUNKS = TOK // UT
    EPS = 1e-5
    NPAR = CONVT * TAPS + CONVT + CT + CT
    PA = CONVT * TAPS + CONVT
    XBANK = (0, 1, 0, 7, 0, 1)
    ZBANK = (7, 1, 7, 1)
    BLK = 3
    BORDER = (0, 2, 1)

    outer = ExitStack()
    with outer:
        def sem(name):
            return outer.enter_context(nc.semaphore(name))

        def need(eng, s, value):
            if isinstance(value, int) and value <= 0:
                return
            eng.wait_ge(s, value)

        cs_parts = nc.dram_tensor("cs_parts", (GROUPS, LROWS, NBATCH * BLK * 128), bf16, kind="Internal").ap()

        def make_sb(stack):
            return lambda name, shape, dt: stack.enter_context(nc.sbuf_tensor(name, shape, dt))

        sb = make_sb(outer)
        PS = outer.enter_context(nc.psum_tensor("PS", [128, 8, 512], fp32))

        xnT_hi = sb("xnT_hi", [128, KH, TOK], f32r)
        xnT_lo = sb("xnT_lo", [128, KH, TOK], f32r)
        outT = sb("outT", [128, KH, TOK], fp32)
        ident = sb("ident", [128, 128], fp32)
        ssq = sb("ssq", [128, TOK], fp32)
        epsc = sb("epsc", [128, 1], fp32)

        mamba = ExitStack()
        sb = make_sb(mamba)
        dt_sb = sb("dt_sb", [128, TILES, GROUPS, HPG], fp32)
        wraw = sb("wraw", [128, KH * CONVT * 128], fp32)
        praw = sb("praw", [128, NPAR], fp32)
        wx_hi = sb("wx_hi", [128, KH, CONVT * 128], f32r)
        wx_lo = sb("wx_lo", [128, KH, CONVT * 128], f32r)
        wz_hi = sb("wz_hi", [128, KH, CT * 128], f32r)
        wz_lo = sb("wz_lo", [128, KH, CT * 128], f32r)
        wo_hi = sb("wo_hi", [128, CT, HID], f32r)
        wo_lo = sb("wo_lo", [128, CT, HID], f32r)
        mask = sb("mask", [128, BLK * 128], fp32)
        L = sb("L", [DROWS, 2, 2, BLK * 128], bf16)
        R = sb("R", [DROWS, 2, 2, 2, HPG, 64], bf16)
        wraw_x = wraw[:, :].rearrange("p (k n) -> p k n", k=KH)
        wraw_z = wraw[:, 0:KH * CT * 128].rearrange("p (k n) -> p k n", k=KH)
        wraw_o = wraw[:, 0:CT * HID].rearrange("p (c n) -> p c n", c=CT)

        s0 = ExitStack()
        sb = make_sb(s0)
        umask = sb("umask", [128, 128], fp32)
        sufmask = sb("sufmask", [128, 128], fp32)
        wdt_raw = sb("wdt_raw", [128, KH, HEADS], fp32)
        wdt_hi = sb("wdt_hi", [128, KH, HEADS], f32r)
        wdt_lo = sb("wdt_lo", [128, KH, HEADS], f32r)
        dtb = sb("dtb", [128, HEADS], fp32)
        alog = sb("alog", [128, HEADS], fp32)
        expA = sb("expA", [128, HEADS], fp32)
        st = sb("st", [128, TILES, 6], fp32)
        mv = sb("mv", [128, TILES, 2], fp32)
        std = sb("std", [128, TILES], fp32)
        rstd = sb("rstd", [128, TILES], fp32)
        xn = sb("xn", [128, TILES, HID], fp32)
        dtw = [sb(f"dtw{i}", [128, TILES * HEADS], fp32) for i in range(6)]
        csr = [sb(f"csr{i}", [HEADS, NBATCH * BLK * 128], fp32) for i in range(2)]
        l_const = sb("l_const", [DROWS, 2 * BLK * 128], fp32)
        r_const = sb("r_const", [DROWS, HPG * 64], fp32)
        csp = [sb(f"csp{i}", [HEADS, NBATCH * BLK * 128], bf16) for i in range(PARTS)]
        x_v = outT[:, :, :].rearrange("p k t -> p (k t)").rearrange("p (t c) -> p t c", c=HID)
        xd_v = x_d.rearrange("(t p) c -> p t c", p=128)

        s_x0 = [sem(f"s0_x{i}") for i in range(4)]
        s_c0 = sem("s0_const_in")
        s_par = sem("params_in")
        s_raw = sem("weights_in")
        s_stat = sem("s0_stat")
        s_sqrt = sem("s0_sqrt")
        s_rstd = sem("s0_rstd")
        s_xn = sem("s0_xn")
        s_xt = sem("s0_xt")
        s_hi0 = sem("s0_hi")
        s_lo0 = sem("s0_lo")
        s_wdt = sem("s0_wdt")
        s_dtp = sem("s0_dt_psum")
        s_v = sem("s0_softplus_dve")
        s_a = sem("s0_softplus_act")
        s_cs = sem("s0_cs_psum")
        s_p = sem("s0_parts_act")
        s_r = sem("s0_rest_dve")
        s_scr = sem("s0_scratch_out")
        s_ms = sem("s0_memset")
        QT = TILES // 4

        with nc.Block() as block:
            @block.sync
            def _(sp):
                for i in range(4):
                    sp.dma_start(x_v[:, QT * i:QT * i + QT, :], xd_v[:, QT * i:QT * i + QT, :]).then_inc(s_x0[i], 16)
                for dst, src in ((ident, sq_const_d[:, 0:128]), (umask, sq_const_d[:, 128:256]),
                                 (sufmask, sq_const_d[:, 256:384]), (mask, mask_d), (dtb, dtb_d),
                                 (alog, alog_d), (l_const, l_const_d), (r_const, r_const_d)):
                    sp.dma_start(dst[:, :], src).then_inc(s_c0, 16)
                sp.dma_start(wdt_raw[:, :, :], wdt_d.rearrange("p (k n) -> p k n", k=KH)).then_inc(s_c0, 16)
                sp.dma_start(praw[:, :], par_d[0, :, :]).then_inc(s_par, 16)
                sp.dma_start(wraw[:, :], wx_d[0, :, :]).then_inc(s_raw, 16)
                sp.wait_ge(s_p, PARTS)
                for i in range(PARTS):
                    for g in range(GROUPS):
                        sp.dma_start(cs_parts[g, HPG * i:HPG * i + HPG, :],
                                     csp[i][HPG * g:HPG * g + HPG, :]).then_inc(s_scr, 16)
                sp.wait_ge(s_scr, 16 * PARTS * GROUPS)

            @block.gpsimd
            def _(pool):
                pool.memset(epsc[:, :], EPS).then_inc(s_ms, 1)
                pool.memset(ssq[:, :], 0.0).then_inc(s_ms, 1)
                pool.wait_ge(s_c0, 16 * 9)
                for b in range(2):
                    pool.tensor_copy(L[:, b, :, :], l_const[:, :].rearrange("p (s n) -> p s n", s=2))
                    for c in range(2):
                        pool.tensor_copy(R[:, b, c, :, :, :].rearrange("p s h i -> p s (h i)"),
                                         r_const[:, :].unsqueeze(1).to_broadcast([DROWS, 2, HPG * 64]))
                pool.wait_ge(s_xn, 4)
                pool.memset(outT[:, :, :], 0.0).then_inc(s_ms, 1)

            @block.vector
            def _(dve):
                for i in range(4):
                    dve.wait_ge(s_x0[i], 16)
                    for t in range(QT * i, QT * i + QT):
                        ins = dve.bn_stats(st[:, t, :], x_v[:, t, :])
                    ins.then_inc(s_stat, 1)
                    dve.wait_ge(s_stat, 2 * i + 1)
                    for t in range(QT * i, QT * i + QT):
                        ins = dve.bn_aggr(mv[:, t, :], st[:, t, :])
                    ins.then_inc(s_stat, 1)
                for i in range(4):
                    a, b = QT * i, QT * i + QT
                    dve.wait_ge(s_sqrt, i + 1)
                    dve.reciprocal(rstd[:, a:b], std[:, a:b]).then_inc(s_rstd, 1)
                    dve.wait_ge(s_rstd, i + 1)
                    for t in range(a, b):
                        ins = dve.tensor_scalar(xn[:, t, :], x_v[:, t, :], mv[:, t, 0:1], rstd[:, t:t + 1],
                                                ALU.subtract, ALU.mult)
                    ins.then_inc(s_xn, 1)
                dve.wait_ge(s_wdt, 1)
                dve.tensor_tensor(wdt_lo[:, :, :], wdt_raw[:, :, :], wdt_hi[:, :, :].bitcast(fp32),
                                  ALU.subtract).then_inc(s_wdt, 1)
                for n in range(4 * KH):
                    i, k = n // KH, n % KH
                    dve.wait_ge(s_hi0, n + 1)
                    dve.tensor_tensor(xnT_lo[:, k, 512 * i:512 * i + 512], PS[:, n, :],
                                      xnT_hi[:, k, 512 * i:512 * i + 512].bitcast(fp32),
                                      ALU.subtract).then_inc(s_lo0, 1)
                v, e, w, lnw, r, q = dtw
                dve.wait_ge(s_dtp, 1)
                dve.tensor_tensor(v[:, :].rearrange("p (t h) -> p t h", h=HEADS),
                                  PS[:, 0:2, :].rearrange("p b (t h) -> p (b t) h", h=HEADS),
                                  dtb[:, :].unsqueeze(1).to_broadcast([128, TILES, HEADS]), ALU.add).then_inc(s_v, 1)
                dve.wait_ge(s_a, 2)
                dve.tensor_scalar(w[:, :], e[:, :], 1.0, None, ALU.add).then_inc(s_v, 1)
                dve.wait_ge(s_v, 2)
                dve.scalar_tensor_tensor(r[:, :], w[:, :], -1.0, e[:, :], ALU.add, ALU.subtract).then_inc(s_v, 1)
                dve.reciprocal(q[:, :], w[:, :]).then_inc(s_v, 1)
                dve.wait_ge(s_v, 4)
                dve.tensor_tensor(q[:, :], r[:, :], q[:, :], ALU.mult).then_inc(s_v, 1)
                dve.wait_ge(s_a, 3)
                dve.wait_ge(s_v, 5)
                dve.tensor_tensor(lnw[:, :], lnw[:, :], q[:, :], ALU.subtract).then_inc(s_v, 1)
                dve.wait_ge(s_v, 6)
                dt_flat = dt_sb[:, :, :, :].rearrange("p t g h -> p (t g h)")
                dve.scalar_tensor_tensor(dt_flat, v[:, :], 0.0, lnw[:, :], ALU.max, ALU.add).then_inc(s_v, 1)
                dve.wait_ge(s_v, 7)
                dve.wait_ge(s_a, 4)
                dve.scalar_tensor_tensor(r[:, :].rearrange("p (t h) -> p t h", h=HEADS),
                                         dt_flat.rearrange("p (t h) -> p t h", h=HEADS), -1.0,
                                         expA[:, :].unsqueeze(1).to_broadcast([128, TILES, HEADS]),
                                         ALU.mult, ALU.mult).then_inc(s_v, 1)
                psum = PS[0:HEADS, :, 0:BLK * 128]
                for i in range(PARTS - 1):
                    src = psum if i == 0 else csr[0][:, :].rearrange("p (b n) -> p b n", b=NBATCH)
                    dve.wait_ge(s_p, i + 1)
                    dve.tensor_tensor(csr[i][:, :].rearrange("p (b n) -> p b n", b=NBATCH), src,
                                      csp[i][:, :].rearrange("p (b n) -> p b n", b=NBATCH),
                                      ALU.subtract).then_inc(s_r, 1)
                    if i + 1 < PARTS - 1:
                        dve.wait_ge(s_r, i + 1)

            @block.scalar
            def _(act):
                act.wait_ge(s_ms, 1)
                for i in range(4):
                    act.wait_ge(s_stat, 2 * i + 2)
                    act.activation(std[:, QT * i:QT * i + QT], mv[:, QT * i:QT * i + QT, 1], ACT.Sqrt,
                                   bias=epsc[:, 0:1]).then_inc(s_sqrt, 1)
                act.wait_ge(s_c0, 16 * 9)
                act.activation(wdt_hi[:, :, :], wdt_raw[:, :, :], ACT.Copy).then_inc(s_wdt, 1)
                for n in range(4 * KH):
                    i, k = n // KH, n % KH
                    act.wait_ge(s_xt, n + 1)
                    act.activation(xnT_hi[:, k, 512 * i:512 * i + 512], PS[:, n, :], ACT.Copy).then_inc(s_hi0, 1)
                v, e, w, lnw, r, q = dtw
                act.wait_ge(s_v, 1)
                act.activation(e[:, :], v[:, :], ACT.Abs).then_inc(s_a, 1)
                act.wait_ge(s_a, 1)
                act.activation(e[:, :], e[:, :], ACT.Exp, scale=-1.0).then_inc(s_a, 1)
                act.wait_ge(s_v, 2)
                act.activation(lnw[:, :], w[:, :], ACT.Ln).then_inc(s_a, 1)
                act.activation(expA[:, :], alog[:, :], ACT.Exp).then_inc(s_a, 1)
                act.wait_ge(s_cs, 1)
                act.activation(csp[0][:, :].rearrange("p (b n) -> p b n", b=NBATCH),
                               PS[0:HEADS, :, 0:BLK * 128], ACT.Copy).then_inc(s_p, 1)
                for i in range(1, PARTS):
                    act.wait_ge(s_r, i)
                    act.activation(csp[i][:, :], csr[i - 1][:, :], ACT.Copy).then_inc(s_p, 1)

            @block.tensor
            def _(pe):
                pe.wait_ge(s_c0, 16 * 9)
                for i in range(4):
                    pe.wait_ge(s_xn, i + 1)
                    for k in range(KH):
                        for t in range(QT):
                            mm = pe.transpose(PS[:, KH * i + k, 128 * t:128 * t + 128],
                                              xn[:, QT * i + t, 128 * k:128 * k + 128], ident[:, :])
                        mm.then_inc(s_xt, 1)
                pe.wait_ge(s_wdt, 2)
                pe.wait_ge(s_lo0, 4 * KH)
                for t in range(TILES):
                    n = 0
                    for lhs, rhs in ((xnT_hi, wdt_hi), (xnT_hi, wdt_lo), (xnT_lo, wdt_hi)):
                        for k in range(KH):
                            mm = pe.matmul(PS[:, t // 8, HEADS * (t % 8):HEADS * (t % 8) + HEADS],
                                           lhs[:, k, 128 * t:128 * t + 128], rhs[:, k, :],
                                           start=(n == 0), stop=(n == 3 * KH - 1))
                            n += 1
                mm.then_inc(s_dtp, 1)
                pe.wait_ge(s_v, 8)
                dA = dtw[4]
                for b in range(NBATCH):
                    for blk, (c, m) in enumerate(((0, umask), (0, sufmask), (1, umask))):
                        t = 2 * b + c
                        mm = pe.matmul(PS[0:HEADS, b, 128 * blk:128 * blk + 128],
                                       dA[:, HEADS * t:HEADS * t + HEADS], m[:, :], start=True, stop=True)
                mm.then_inc(s_cs, 1)
        s0.close()

        sb = make_sb(mamba)
        par_a = sb("par_a", [128, PA], fp32)
        par_d_sb = sb("par_d_sb", [128, CT], fp32)
        xT = sb("xT", [128, 2, CT, UT], fp32)
        BC = sb("BC", [128, 2, 2, UT], fp32)
        acc = sb("acc", [128, 3, UT], fp32)
        xdt = sb("xdt", [128, 2, 2, HPG, P], fp32)
        M = sb("M", [128, 2, BLK, HPG, 128], fp32)
        cbm = sb("cbm", [128, BLK * 128], fp32)
        sz = sb("sz", [128, CT, UT], fp32)
        y = sb("y", [128, 2, 2, SEQ], fp32)
        y2 = sb("y2", [128, 2, 2, SEQ], fp32)
        gy = sb("gy", [128, 2, 2, SEQ], fp32)
        g_hi = sb("g_hi", [128, CT, UT], f32r)
        g_lo = sb("g_lo", [128, CT, UT], f32r)

        a_done, z_done, t_done, cb_done = sem("a_done"), sem("z_done"), sem("t_done"), sem("cb_done")
        d_done, yt_done, o_done = sem("decay_done"), sem("yT_done"), sem("proj_done")
        t0_done, xs_done, zs_done = sem("tap3_done"), sem("conv_silu_done"), sem("z_silu_done")
        exp_done = sem("exp_done")
        sq_done, hi_done = sem("y_squared"), sem("g_hi_done")
        wx_hi_done, wz_hi_done, wo_hi_done, wo_scaled = sem("wx_hi_done"), sem("wz_hi_done"), sem("wo_hi_done"), sem("wo_scaled")
        cbm_done, conv_done, tap_link, m_done = sem("cb_masked"), sem("conv_done"), sem("tap_link"), sem("m_done")
        y_done, xdt_done, oacc_done = sem("y_done"), sem("xdt_done"), sem("proj_added")
        pa_done, pd_done = sem("conv_params_ready"), sem("skip_params_ready")
        ssq_link, gy_done, lo_done = sem("squares_added"), sem("gated_done"), sem("g_lo_done")
        wx_lo_done, wz_lo_done, wo_lo_done = sem("wx_lo_done"), sem("wz_lo_done"), sem("wo_lo_done")
        l_in = [sem(f"l_in{b}") for b in range(2)]
        r_in = [sem(f"r_in{b}") for b in range(2)]

        PT = PS[:, 4, :]
        PO = PS[:, 6, :]
        PY = PS[:, 5, :].rearrange("p (c t) -> p c t", c=2)
        PD = PS[:, 2:4, :]

        def groups(eng, body):
            body(0, False)
            with eng.Fori(1, GROUPS - 1) as g:
                body(g, False)
            body(GROUPS - 1, True)

        with nc.Block() as block:
            @block.sync
            def _(sp):
                def load_lr(g, q, b, bt):
                    need(sp, d_done, BLK * (bt - 2) + BLK)
                    n = 2 * q + b
                    src = cs_parts[g, :, BLK * 128 * n:BLK * 128 * n + BLK * 128]
                    sp.dma_start(L[0:LROWS, b, :, :], src.unsqueeze(1).to_broadcast([LROWS, 2, BLK * 128])).then_inc(l_in[b], 16)
                    rows = src.rearrange("(p h) t -> p h t", h=HPG)
                    for c in range(2):
                        for s in range(2):
                            t = 256 * c + 64 * s
                            sp.dma_start(R[LROWS:SUMS, b, c, s, :, :], rows[:, :, t:t + 64]).then_inc(r_in[b], 16)

                load_lr(0, 0, 0, 0)
                load_lr(0, 0, 1, 1)
                sp.wait_ge(wx_lo_done, CONVT)
                sp.dma_start(wraw[:, 0:KH * CT * 128], wz_d[0, :, :]).then_inc(s_raw, 16)

                def body(g, last):
                    for q in range(PAIRS):
                        u = PAIRS * g + q
                        if q == 0:
                            sp.wait_ge(wz_lo_done, CT * g + CT)
                            sp.dma_start(wraw[:, 0:CT * HID], wo_d[g, :, :]).then_inc(s_raw, 16)
                        for b in range(2):
                            if not (last and q == PAIRS - 1):
                                nq = (q + 1) % PAIRS
                                load_lr(g + 1 if q == PAIRS - 1 else g, nq, b, 2 * u + b + 2)
                            if last:
                                continue
                            if q == 1 and b == 0:
                                sp.wait_ge(wo_lo_done, CT * (g + 1))
                                sp.wait_ge(pd_done, g + 1)
                                sp.dma_start(praw[:, :], par_d[g + 1, :, :]).then_inc(s_par, 16)
                                sp.dma_start(wraw[:, :], wx_d[g + 1, :, :]).then_inc(s_raw, 16)
                            if q == 3 and b == 0:
                                sp.wait_ge(wx_lo_done, CONVT * (g + 2))
                                sp.dma_start(wraw[:, 0:KH * CT * 128], wz_d[g + 1, :, :]).then_inc(s_raw, 16)
                groups(sp, body)

            @block.tensor
            def _(pe):
                def in_proj(bank, whi, wlo, c0, q, s):
                    n = 0
                    for lhs, rhs in ((whi, xnT_hi), (whi, xnT_lo), (wlo, xnT_hi)):
                        for k in range(KH):
                            mm = pe.matmul(PS[:, bank, :], lhs[:, k, c0:c0 + 128], rhs[:, k, UT * q:UT * q + UT],
                                           start=(n == 0), stop=(n == 3 * KH - 1))
                            n += 1
                    mm.then_inc(s, 1)

                def conv_in(g, q, v, k, free):
                    need(pe, *free)
                    pe.wait_ge(wx_lo_done, CONVT * g + k + 1)
                    in_proj(XBANK[k], wx_hi, wx_lo, 128 * k, q, a_done)

                def z_in(g, q, u, ct, free):
                    need(pe, *free)
                    pe.wait_ge(wz_lo_done, CT * g + ct + 1)
                    in_proj(ZBANK[ct], wz_hi, wz_lo, 128 * ct, q, z_done)

                def c_by_b(u, up, b, bt):
                    pe.wait_ge(xs_done, CONVT * u + 2)
                    if b == 0:
                        need(pe, oacc_done, KH * (u - 1))
                    else:
                        pe.wait_ge(cbm_done, bt)
                    t = SEQ * b
                    pe.matmul(PO[:, 0:256], BC[:, up, 0, t:t + 128], BC[:, up, 1, t:t + 256],
                              start=True, stop=True)
                    pe.matmul(PO[:, 256:384], BC[:, up, 0, t + 128:t + 256], BC[:, up, 1, t + 128:t + 256],
                              start=True, stop=True).then_inc(cb_done, 1)

                def decay(u, b, bt, n):
                    if n == 0:
                        pe.wait_ge(l_in[b], 16 * (u + 1))
                        pe.wait_ge(r_in[b], 64 * (u + 1))
                    need(pe, exp_done, BLK * bt + n)
                    blk = BORDER[n]
                    for s in range(2):
                        mm = pe.matmul(PS[:, 2 + s, :], L[:, b, s, 128 * blk:128 * blk + 128],
                                       R[:, b, min(blk, 1), s, :, :], start=True, stop=True)
                    mm.then_inc(d_done, 1)

                def turn_x(u, up, b, bt, c):
                    if c == 0:
                        pe.wait_ge(xs_done, CONVT * u + CONVT)
                    need(pe, xdt_done, 2 * bt + c)
                    t = SEQ * b + 128 * c
                    for ct in range(CT):
                        mm = pe.transpose(PT[:, 128 * ct:128 * ct + 128], xT[:, up, ct, t:t + 128], ident[:, :])
                    mm.then_inc(t_done, 1)

                def y_t(par, bt, half):
                    if half == 0:
                        pe.wait_ge(m_done, BLK * bt + BLK)
                        pe.wait_ge(xdt_done, 2 * bt + 2)
                    need(pe, y_done, 2 * bt + half)
                    for cc in range(2):
                        ct = 2 * half + cc
                        for c in range(2):
                            for s in range(2):
                                h = 2 * ct + s
                                lhs = xdt[:, par, c, h, :]
                                o = PS[P * s:P * s + P, 5, SEQ * cc + 128 * c:SEQ * cc + SEQ]
                                rhs = M[:, par, 0:2, h, :] if c == 0 else M[:, par, 2, h, :]
                                mm = pe.matmul(o, lhs, rhs, start=(c == 0), stop=(c == 1))
                    mm.then_inc(yt_done, 1)

                def project(g, u, m):
                    if m == 0:
                        pe.wait_ge(lo_done, 4 * u + 4)
                        pe.wait_ge(wo_lo_done, CT * g + CT)
                        pe.wait_ge(cbm_done, min(2 * u + 4, 2 * PAIRS * GROUPS) if isinstance(u, int) else 2 * u + 4)
                    else:
                        pe.wait_ge(oacc_done, KH * u + m)
                    for ct in range(CT):
                        for n, (lhs, rhs) in enumerate(((wo_hi, g_hi), (wo_hi, g_lo), (wo_lo, g_hi))):
                            mm = pe.matmul(PO, lhs[:, ct, 128 * m:128 * m + 128], rhs[:, ct, :],
                                           start=(ct == 0 and n == 0), stop=(ct == CT - 1 and n == 2))
                    mm.then_inc(o_done, 1)

                def body(g, last):
                    for q in range(PAIRS):
                        u = PAIRS * g + q
                        first = isinstance(u, int) and u == 0
                        ahead = not (last and q == PAIRS - 1)
                        gv, qv, v = (g + 1 if q == PAIRS - 1 else g), (q + 1) % PAIRS, u + 1
                        gu = g if q else g - 1
                        up = q % 2
                        bt = 2 * u
                        done = lambda w, k: (conv_done, CONVT * w + k + 1)
                        zdone = lambda w, ct: (zs_done, CT * w + ct + 1)
                        if ahead:
                            conv_in(gv, qv, v, 0, done(u, 4))
                        if not first:
                            y_t(1, bt - 1, 0)
                        decay(u, 0, bt, 1)
                        if ahead:
                            conv_in(gv, qv, v, 1, done(u, 5) if first else zdone(u - 1, 3))
                        decay(u, 0, bt, 2)
                        turn_x(u, up, 0, bt, 0)
                        z_in(g, q, u, 0, done(u, 3) if first else zdone(u - 1, 2))
                        if not first:
                            y_t(1, bt - 1, 1)
                        if ahead:
                            conv_in(gv, qv, v, 2, done(v, 0))
                        decay(u, 1, bt + 1, 0)
                        turn_x(u, up, 0, bt, 1)
                        z_in(g, q, u, 1, done(v, 1) if ahead else zdone(u - 1, 3))
                        c_by_b(u, up, 1, bt + 1)
                        bt = 2 * u + 1
                        if ahead:
                            conv_in(gv, qv, v, 3, zdone(u, 0))
                            conv_in(gv, qv, v, 4, done(v, 2))
                        decay(u, 1, bt, 1)
                        y_t(0, bt - 1, 0)
                        if not first:
                            project(gu, u - 1, 0)
                        decay(u, 1, bt, 2)
                        if ahead:
                            conv_in(gv, qv, v, 5, zdone(u, 1))
                        if not first:
                            project(gu, u - 1, 1)
                        turn_x(u, up, 1, bt, 0)
                        y_t(0, bt - 1, 1)
                        z_in(g, q, u, 2, done(v, 3) if ahead else zdone(u, 0))
                        if ahead:
                            decay(v, 0, 2 * v, 0)
                        turn_x(u, up, 1, bt, 1)
                        z_in(g, q, u, 3, done(v, 5) if ahead else zdone(u, 1))
                        if ahead:
                            c_by_b(v, 1 - up, 0, 2 * v)

                for k in range(CONVT):
                    conv_in(0, 0, 0, k, (conv_done, (0, 0, 1, 0, 3, 2)[k]))
                c_by_b(0, 0, 0, 0)
                decay(0, 0, 0, 0)
                groups(pe, body)
                end = 2 * PAIRS * GROUPS
                y_t(1, end - 1, 0)
                y_t(1, end - 1, 1)
                project(GROUPS - 1, PAIRS * GROUPS - 1, 0)
                project(GROUPS - 1, PAIRS * GROUPS - 1, 1)

            @block.scalar
            def _(act):
                def tap3(g, v, k):
                    n = CONVT * v + k
                    act.wait_ge(a_done, n + 1)
                    act.wait_ge(pa_done, g + 1)
                    need(act, xs_done, n - 2)
                    act.activation(acc[:, k % 3, :], PS[:, XBANK[k], :], ACT.Identity,
                                   scale=par_a[:, TAPS * k + TAPS - 1:TAPS * k + TAPS],
                                   bias=par_a[:, TAPS * CONVT + k:TAPS * CONVT + k + 1]).then_inc(t0_done, 1)

                def conv_silu(vp, v, k):
                    act.wait_ge(conv_done, CONVT * v + k + 1)
                    if k < 2:
                        need(act, cb_done, 2 * v - 2)
                        dst = BC[:, vp, k, :]
                    else:
                        need(act, y_done, 4 * v - 5 + (k - 2) // 2)
                        dst = xT[:, vp, k - 2, :]
                    act.activation(dst, acc[:, k % 3, :], ACT.Silu).then_inc(xs_done, 1)

                def z_silu(u, ct):
                    act.wait_ge(z_done, CT * u + ct + 1)
                    need(act, gy_done, 4 * u - 1 + ct // 2)
                    act.activation(sz[:, ct, :], PS[:, ZBANK[ct], :], ACT.Silu).then_inc(zs_done, 1)

                def decay_exp(par, bt, n):
                    act.wait_ge(d_done, BLK * bt + n + 1)
                    need(act, yt_done, 2 * bt - 2)
                    act.activation(M[:, par, BORDER[n], :, :].rearrange("p h (s i) -> p s h i", s=2),
                                   PD.rearrange("p s (h i) -> p s h i", i=64), ACT.Exp).then_inc(exp_done, 1)

                def square(bt, half):
                    n = 2 * bt + half
                    act.wait_ge(y_done, n + 1)
                    need(act, ssq_link, 2 * n - 2)
                    act.activation(y2[:, half, :, :], y[:, half, :, :], ACT.Square).then_inc(sq_done, 1)

                def gated_hi(u, b, bt, half):
                    n = 2 * bt + half
                    act.wait_ge(gy_done, n + 1)
                    need(act, o_done, KH * u)
                    act.activation(g_hi[:, 2 * half:2 * half + 2, SEQ * b:SEQ * b + SEQ], gy[:, half, :, :],
                                   ACT.Copy).then_inc(hi_done, 1)

                def split_x(g, k):
                    act.wait_ge(s_raw, 48 * g + 16)
                    need(act, a_done, CONVT * PAIRS * g - CONVT + k + 1)
                    act.activation(wx_hi[:, :, 128 * k:128 * k + 128], wraw_x[:, :, 128 * k:128 * k + 128],
                                   ACT.Copy).then_inc(wx_hi_done, 1)

                def split_z(g, ct):
                    act.wait_ge(s_raw, 48 * g + 32)
                    need(act, z_done, CT * PAIRS * g - CT + ct + 1)
                    act.activation(wz_hi[:, :, 128 * ct:128 * ct + 128], wraw_z[:, :, 128 * ct:128 * ct + 128],
                                   ACT.Copy).then_inc(wz_hi_done, 1)

                def split_o(g, ct):
                    act.wait_ge(wo_scaled, CT * g + ct + 1)
                    need(act, o_done, KH * PAIRS * g)
                    act.activation(wo_hi[:, ct, :], wraw_o[:, ct, :], ACT.Copy).then_inc(wo_hi_done, 1)

                for k in range(CONVT):
                    split_x(0, k)
                for k in range(CONVT):
                    tap3(0, 0, k)
                    if k >= 2:
                        conv_silu(0, 0, k - 2)
                conv_silu(0, 0, CONVT - 2)
                conv_silu(0, 0, CONVT - 1)
                for ct in range(CT):
                    split_z(0, ct)

                def body(g, last):
                    for q in range(PAIRS):
                        u = PAIRS * g + q
                        first = isinstance(u, int) and u == 0
                        ahead = not (last and q == PAIRS - 1)
                        gv, v, vp = (g + 1 if q == PAIRS - 1 else g), u + 1, (q + 1) % 2
                        bt = 2 * u
                        decay_exp(0, bt, 0)
                        if ahead:
                            tap3(gv, v, 0)
                        decay_exp(0, bt, 1)
                        if not first:
                            gated_hi(u - 1, 0, bt - 2, 1)
                        if q == 0 and not first:
                            for ct in range(CT):
                                split_z(g, ct)
                        if ahead:
                            tap3(gv, v, 1)
                        if not first:
                            square(bt - 2, 1)
                        if q == 1:
                            for ct in (2, 3):
                                split_o(g, ct)
                        decay_exp(0, bt, 2)
                        z_silu(u, 0)
                        if ahead:
                            tap3(gv, v, 2)
                            conv_silu(vp, v, 0)
                        if not first:
                            gated_hi(u - 1, 1, bt - 1, 0)
                        if ahead:
                            conv_silu(vp, v, 1)
                        if not first:
                            square(bt - 1, 0)
                        z_silu(u, 1)
                        bt = 2 * u + 1
                        decay_exp(1, bt, 0)
                        if not first:
                            gated_hi(u - 1, 1, bt - 2, 1)
                        if ahead:
                            tap3(gv, v, 3)
                        decay_exp(1, bt, 1)
                        if ahead:
                            tap3(gv, v, 4)
                        if not first:
                            square(bt - 2, 1)
                        decay_exp(1, bt, 2)
                        if q == 2 and not last:
                            for k in range(3):
                                split_x(g + 1, k)
                        if ahead:
                            conv_silu(vp, v, 2)
                            tap3(gv, v, 5)
                            conv_silu(vp, v, 3)
                        square(bt - 1, 0)
                        if ahead:
                            conv_silu(vp, v, 4)
                        gated_hi(u, 0, bt - 1, 0)
                        if q == 0:
                            for ct in (0, 1):
                                split_o(g, ct)
                        z_silu(u, 2)
                        if ahead:
                            conv_silu(vp, v, 5)
                        if q == 2 and not last:
                            for k in range(3, CONVT):
                                split_x(g + 1, k)
                        z_silu(u, 3)
                groups(act, body)
                end = 2 * PAIRS * GROUPS
                gated_hi(PAIRS * GROUPS - 1, 0, end - 2, 1)
                square(end - 2, 1)
                for half in range(2):
                    gated_hi(PAIRS * GROUPS - 1, 1, end - 1, half)
                    square(end - 1, half)

            @block.vector
            def _(dve):
                def mask_cb(bt):
                    dve.wait_ge(cb_done, bt + 1)
                    need(dve, m_done, BLK * bt)
                    dve.tensor_tensor(cbm[:, :], PO[:, 0:BLK * 128], mask[:, :], ALU.mult).then_inc(cbm_done, 1)

                def conv(g, v, k, s):
                    n = CONVT * v + k
                    if s == 1:
                        dve.wait_ge(t0_done, n + 1)
                        dve.wait_ge(pa_done, g + 1)
                    else:
                        dve.wait_ge(tap_link, 2 * n + s - 1)
                    src = PS[:, XBANK[k], :].rearrange("p (b t) -> p b t", b=2)
                    dst = acc[:, k % 3, :].rearrange("p (b t) -> p b t", b=2)
                    dve.scalar_tensor_tensor(dst[:, :, s:SEQ], src[:, :, 0:SEQ - s],
                                             par_a[:, TAPS * k + TAPS - 1 - s:TAPS * k + TAPS - s],
                                             dst[:, :, s:SEQ], ALU.mult, ALU.add)\
                       .then_inc(conv_done if s == TAPS - 1 else tap_link, 1)

                def decay_cb(par, bt, n):
                    if n == 0:
                        dve.wait_ge(cbm_done, bt + 1)
                    dve.wait_ge(exp_done, BLK * bt + n + 1)
                    blk = BORDER[n]
                    dve.scalar_tensor_tensor(M[:, par, blk, :, :], M[:, par, blk, :, :], 1.0,
                                             cbm[:, 128 * blk:128 * blk + 128].unsqueeze(1).to_broadcast([128, HPG, 128]),
                                             ALU.min, ALU.mult).then_inc(m_done, 1)

                def add_skip(g, up, b, bt, half):
                    n = 2 * bt + half
                    dve.wait_ge(yt_done, n + 1)
                    dve.wait_ge(pd_done, g + 1)
                    need(dve, sq_done, n - 1)
                    need(dve, gy_done, n - 1)
                    for cc in range(2):
                        ct = 2 * half + cc
                        ins = dve.scalar_tensor_tensor(y[:, half, cc, :], xT[:, up, ct, SEQ * b:SEQ * b + SEQ],
                                                       par_d_sb[:, ct:ct + 1], PY[:, cc, :], ALU.mult, ALU.add)
                    ins.then_inc(y_done, 1)

                def scale_x(g, q, par, b, bt, c):
                    dve.wait_ge(t_done, 2 * bt + c + 1)
                    need(dve, yt_done, 2 * bt - 2)
                    t = 4 * q + 2 * b + c
                    dve.tensor_tensor(xdt[:, par, c, :, :], PT.rearrange("p (h e) -> p h e", h=HPG),
                                      dt_sb[:, t, g, :].unsqueeze(2).to_broadcast([128, HPG, P]),
                                      ALU.mult).then_inc(xdt_done, 1)

                def add_proj(q, u, m):
                    dve.wait_ge(o_done, KH * u + m + 1)
                    o = outT[:, m, UT * q:UT * q + UT]
                    dve.tensor_tensor(o, PO, o, ALU.add).then_inc(oacc_done, 1)

                def conv_params(g):
                    dve.wait_ge(s_par, 16 * g + 16)
                    need(dve, t0_done, CONVT * PAIRS * g)
                    need(dve, conv_done, CONVT * PAIRS * g)
                    dve.tensor_copy(par_a[:, :], praw[:, 0:PA]).then_inc(pa_done, 1)

                def skip_params(g):
                    dve.wait_ge(s_par, 16 * g + 16)
                    need(dve, y_done, 4 * PAIRS * g)
                    dve.tensor_copy(par_d_sb[:, :], praw[:, PA:PA + CT]).then_inc(pd_done, 1)

                conv_params(0)
                for k in range(CONVT):
                    for s in range(1, TAPS):
                        conv(0, 0, k, s)

                def body(g, last):
                    for q in range(PAIRS):
                        u = PAIRS * g + q
                        first = isinstance(u, int) and u == 0
                        ahead = not (last and q == PAIRS - 1)
                        gv, v = (g + 1 if q == PAIRS - 1 else g), u + 1
                        up = q % 2
                        gy_, upy = (g if q else g - 1), 1 - up
                        bt = 2 * u
                        if q == PAIRS - 1 and ahead:
                            conv_params(g + 1)
                        mask_cb(bt)
                        if not first:
                            scale_x(gy_, (q - 1) % PAIRS, 1, 1, bt - 1, 1)
                        decay_cb(0, bt, 0)
                        if ahead:
                            conv(gv, v, 0, 1)
                        if not first:
                            add_skip(gy_, upy, 1, bt - 1, 0)
                        if ahead:
                            conv(gv, v, 0, 2)
                        decay_cb(0, bt, 1)
                        if ahead:
                            conv(gv, v, 0, 3)
                            conv(gv, v, 1, 1)
                        scale_x(g, q, 0, 0, bt, 0)
                        if ahead:
                            conv(gv, v, 1, 2)
                        decay_cb(0, bt, 2)
                        if ahead:
                            conv(gv, v, 1, 3)
                            conv(gv, v, 2, 1)
                        if not first:
                            add_skip(gy_, upy, 1, bt - 1, 1)
                        if ahead:
                            conv(gv, v, 2, 2)
                        scale_x(g, q, 0, 0, bt, 1)
                        if ahead:
                            conv(gv, v, 2, 3)
                        bt = 2 * u + 1
                        if q == 0:
                            skip_params(g)
                        mask_cb(bt)
                        decay_cb(1, bt, 0)
                        if ahead:
                            conv(gv, v, 3, 1)
                        decay_cb(1, bt, 1)
                        if ahead:
                            conv(gv, v, 3, 2)
                        add_skip(g, up, 0, bt - 1, 0)
                        if ahead:
                            conv(gv, v, 3, 3)
                            conv(gv, v, 4, 1)
                        if not first:
                            add_proj((q - 1) % PAIRS, u - 1, 0)
                        if ahead:
                            conv(gv, v, 4, 2)
                        if ahead:
                            conv(gv, v, 4, 3)
                            conv(gv, v, 5, 1)
                        if not first:
                            add_proj((q - 1) % PAIRS, u - 1, 1)
                        if ahead:
                            conv(gv, v, 5, 2)
                        scale_x(g, q, 1, 1, bt, 0)
                        if ahead:
                            conv(gv, v, 5, 3)
                        add_skip(g, up, 0, bt - 1, 1)
                        decay_cb(1, bt, 2)
                groups(dve, body)
                end = 2 * PAIRS * GROUPS
                scale_x(GROUPS - 1, PAIRS - 1, 1, 1, end - 1, 1)
                add_skip(GROUPS - 1, 1, 1, end - 1, 0)
                add_skip(GROUPS - 1, 1, 1, end - 1, 1)
                for m in range(KH):
                    add_proj(PAIRS - 1, PAIRS * GROUPS - 1, m)

            @block.gpsimd
            def _(pool):
                def gate(u, b, bt, half):
                    n = 2 * bt + half
                    pool.wait_ge(y_done, n + 1)
                    pool.wait_ge(zs_done, CT * u + 2 * half + 2)
                    need(pool, hi_done, n - 1)
                    need(pool, lo_done, n - 1)
                    pool.tensor_tensor(gy[:, half, :, :], y[:, half, :, :],
                                       sz[:, 2 * half:2 * half + 2, SEQ * b:SEQ * b + SEQ], ALU.mult).then_inc(gy_done, 1)

                def gated_lo(b, bt, half):
                    cts, ts = slice(2 * half, 2 * half + 2), slice(SEQ * b, SEQ * b + SEQ)
                    pool.wait_ge(hi_done, 2 * bt + half + 1)
                    pool.tensor_tensor(g_lo[:, cts, ts], gy[:, half, :, :], g_hi[:, cts, ts].bitcast(fp32),
                                       ALU.subtract).then_inc(lo_done, 1)

                def add_squares(q, b, bt, half):
                    n = 2 * bt + half
                    pool.wait_ge(sq_done, n + 1)
                    tok = ssq[:, UT * q + SEQ * b:UT * q + SEQ * b + SEQ]
                    for cc in range(2):
                        need(pool, ssq_link, 2 * n + cc)
                        pool.tensor_tensor(tok, tok, y2[:, half, cc, :], ALU.add).then_inc(ssq_link, 1)

                def split_x(g, k):
                    pool.wait_ge(wx_hi_done, CONVT * g + k + 1)
                    n = slice(128 * k, 128 * k + 128)
                    pool.tensor_tensor(wx_lo[:, :, n], wraw_x[:, :, n], wx_hi[:, :, n].bitcast(fp32),
                                       ALU.subtract).then_inc(wx_lo_done, 1)

                def split_z(g, ct):
                    pool.wait_ge(wz_hi_done, CT * g + ct + 1)
                    n = slice(128 * ct, 128 * ct + 128)
                    pool.tensor_tensor(wz_lo[:, :, n], wraw_z[:, :, n], wz_hi[:, :, n].bitcast(fp32),
                                       ALU.subtract).then_inc(wz_lo_done, 1)

                def scale_o(g):
                    pool.wait_ge(s_raw, 48 * g + 48)
                    pool.wait_ge(s_par, 16 * g + 16)
                    for ct in range(CT):
                        pool.tensor_tensor(wraw_o[:, ct, :], wraw_o[:, ct, :],
                                           praw[:, PA + CT + ct:PA + CT + ct + 1].to_broadcast([128, HID]),
                                           ALU.mult).then_inc(wo_scaled, 1)

                def split_o(g, cts):
                    for ct in cts:
                        pool.wait_ge(wo_hi_done, CT * g + ct + 1)
                        pool.tensor_tensor(wo_lo[:, ct, :], wraw_o[:, ct, :], wo_hi[:, ct, :].bitcast(fp32),
                                           ALU.subtract).then_inc(wo_lo_done, 1)

                for k in range(CONVT):
                    split_x(0, k)
                for ct in range(CT):
                    split_z(0, ct)

                def body(g, last):
                    for q in range(PAIRS):
                        u = PAIRS * g + q
                        first = isinstance(u, int) and u == 0
                        bt, pq = 2 * u, (q - 1) % PAIRS
                        if not first:
                            gated_lo(0, bt - 2, 1)
                        if q == 0 and not first:
                            for ct in range(CT):
                                split_z(g, ct)
                        if not first:
                            gate(u - 1, 1, bt - 1, 0)
                            add_squares(pq, 0, bt - 2, 1)
                            gated_lo(1, bt - 1, 0)
                            add_squares(pq, 1, bt - 1, 0)
                        if q == 1:
                            split_o(g, (2, 3))
                        if not first:
                            gate(u - 1, 1, bt - 1, 1)
                            gated_lo(1, bt - 1, 1)
                            add_squares(pq, 1, bt - 1, 1)
                        if q == 2 and not last:
                            for k in range(3):
                                split_x(g + 1, k)
                        if q == 0:
                            scale_o(g)
                        gate(u, 0, bt, 0)
                        gated_lo(0, bt, 0)
                        if q == 0:
                            split_o(g, (0, 1))
                        add_squares(q, 0, bt, 0)
                        if q == 2 and not last:
                            for k in range(3, CONVT):
                                split_x(g + 1, k)
                        gate(u, 0, bt, 1)
                groups(pool, body)
                u, q = PAIRS * GROUPS - 1, PAIRS - 1
                gated_lo(0, 2 * u, 1)
                add_squares(q, 0, 2 * u, 1)
                for half in range(2):
                    gate(u, 1, 2 * u + 1, half)
                    gated_lo(1, 2 * u + 1, half)
                    add_squares(q, 1, 2 * u + 1, half)

        mamba.close()

        sb = make_sb(outer)
        x1 = sb("x1", [128, TILES, HID], fp32)
        wf_raw = sb("wf_raw", [128, 2, 768], fp32)
        combT = sb("combT", [CROWS, TOK], bf16)
        f_hot = sb("f_hot", [CROWS, FT * 128], bf16)
        st = sb("st_b", [128, TILES, 6], fp32)
        mv = sb("mv_b", [128, TILES, 2], fp32)
        std = sb("std_b", [128, TILES], fp32)
        rstd = sb("rstd_b", [128, TILES], fp32)
        scl = sb("scl", [128, TILES], fp32)
        shf = sb("shf", [128, TILES], fp32)
        s2 = ExitStack()
        sb = make_sb(s2)
        xo = sb("xo", [128, TILES, HID], fp32)
        ones = sb("ones", [128, 1], fp32)
        rn = sb("rn", [128, TILES], fp32)
        v2 = sb("v2", [128, TILES], fp32)
        wg_raw = sb("wg_raw", [128, KH, ROUTES + 1], fp32)
        wg_hi = sb("wg_hi", [128, KH, ROUTES + 1], f32r)
        wg_lo = sb("wg_lo", [128, KH, ROUTES + 1], f32r)
        tie = sb("tie", [128, E * E], fp32)
        hot_raw = sb("hot_raw", [CROWS, FT * 128], fp32)
        ident_b = sb("ident_b", [128, 128], bf16)
        lg = sb("lg", [128, TILES, ROUTES + 1], fp32)
        mx = sb("mx", [128, TILES], fp32)
        pr = sb("pr", [128, TILES, E], fp32)
        sm = sb("sm", [128, TILES], fp32)
        gts = sb("gts", [128, TILES, E, E], fp32)
        eqs = sb("eqs", [128, TILES, E, E], fp32)
        rank = sb("rank", [128, TILES, E], fp32)
        comb = sb("comb", [128, TILES, ROUTES], fp32)
        comb_r = sb("comb_r", [128, TILES, ROUTES], fp32)
        cparts = sb("cparts", [128, TILES, PARTS, ROUTES], bf16)

        def tile_ps(t):
            return PS[:, t // 2, HID * (t % 2):HID * (t % 2) + HID]

        s_in = sem("s2_in")
        s_f = [sem(f"moe_weights_in{i}") for i in range(2)]
        s_on, s_idb, s_var, s_rn = sem("s2_ones"), sem("s2_ident_bf16"), sem("s2_var_psum"), sem("s2_std")
        s_tr, s_d, s_ac = sem("s2_outT_turned"), sem("s2_dve"), sem("s2_act")
        s_xo, s_x1 = sem("s2_scaled"), sem("s2_residual")
        s_st, s_sq, s_n = sem("s2_stat"), sem("s2_sqrt"), sem("s2_normed")
        s_t2, s_h2, s_l2 = sem("s2_xT"), sem("s2_hi"), sem("s2_lo")
        s_g, s_lg, s_e, s_ct, s_cc = sem("s2_gate_w"), sem("s2_logits"), sem("s2_exp"), sem("s2_combT"), sem("s2_combT_copy")
        s_q, s_cp = sem("s2_route_dve"), sem("s2_route_parts")
        s_xn2, s_rs2 = sem("s2_norm_squared"), sem("s2_rstd")

        with nc.Block() as block:
            @block.sync
            def _(sp):
                for dst, src in ((x1[:, :, :], xd_v), (wg_raw[:, :, :], wg_d.rearrange("p (k n) -> p k n", k=KH)),
                                 (tie[:, :], tie_d), (hot_raw[:, :], f_hot_d)):
                    sp.dma_start(dst, src).then_inc(s_in, 16)
                for f in range(2):
                    sp.dma_start(wf_raw[:, f, :], wf_d[f, :, :]).then_inc(s_f[f], 16)

            @block.gpsimd
            def _(pool):
                pool.memset(ones[:, :], 1.0).then_inc(s_on, 1)
                pool.wait_ge(s_tr, TILES // 2)
                pool.memset(outT[:, :, :], 0.0)

            @block.tensor
            def _(pe):
                pe.wait_ge(s_on, 1)
                for t in range(TILES):
                    mm = pe.matmul(PS[:, 7, t:t + 1], ssq[:, 128 * t:128 * t + 128], ones[:, :], start=True, stop=True)
                mm.then_inc(s_var, 1)
                for t in range(TILES):
                    if t == 14:
                        pe.wait_ge(s_rn, 1)
                    for k in range(KH):
                        mm = pe.transpose(PS[:, t // 2, HID * (t % 2) + 128 * k:HID * (t % 2) + 128 * k + 128],
                                          outT[:, k, 128 * t:128 * t + 128], ident[:, :])
                    if t % 2:
                        mm.then_inc(s_tr, 1)
                pe.wait_ge(s_xo, TILES)
                for i in range(4):
                    pe.wait_ge(s_n, i + 1)
                    for k in range(KH):
                        for t in range(QT):
                            mm = pe.transpose(PS[:, KH * i + k, 128 * t:128 * t + 128],
                                              xo[:, QT * i + t, 128 * k:128 * k + 128], ident[:, :])
                        mm.then_inc(s_t2, 1)
                pe.wait_ge(s_g, 2)
                pe.wait_ge(s_l2, 4 * KH)
                for t in range(TILES):
                    n = 0
                    for lhs, rhs in ((xnT_hi, wg_hi), (xnT_hi, wg_lo), (xnT_lo, wg_hi)):
                        for k in range(KH):
                            mm = pe.matmul(PS[:, 0, (ROUTES + 1) * t:(ROUTES + 1) * (t + 1)],
                                           lhs[:, k, 128 * t:128 * t + 128], rhs[:, k, :],
                                           start=(n == 0), stop=(n == 3 * KH - 1))
                            n += 1
                mm.then_inc(s_lg, 1)
                pe.wait_ge(s_cp, PARTS)
                pe.wait_ge(s_idb, 1)
                cps = PS[0:CROWS, 1:3, :].bitcast(bf16).rearrange("p b t -> p (b t)")
                for t in range(TILES):
                    mm = pe.transpose(cps[:, 128 * t:128 * t + 128],
                                      cparts[:, t, :, :].rearrange("p a r -> p (a r)"), ident_b[:, :])
                mm.then_inc(s_ct, 1)

            @block.scalar
            def _(act):
                act.wait_ge(s_var, 1)
                act.activation(std[:, :], PS[:, 7, 0:TILES], ACT.Sqrt, scale=1.0 / INTER, bias=epsc[:, 0:1]).then_inc(s_rn, 1)
                act.wait_ge(s_d, 3)
                act.activation(std[:, :], v2[:, :], ACT.Sqrt, bias=epsc[:, 0:1]).then_inc(s_ac, 1)
                act.wait_ge(s_d, 6)
                for t in range(TILES):
                    act.activation(xo[:, t, :], tile_ps(t), ACT.Identity, scale=scl[:, t:t + 1],
                                   bias=shf[:, t:t + 1]).then_inc(s_xo, 1)
                for i in range(4):
                    act.wait_ge(s_st, 2 * i + 2)
                    act.activation(std[:, QT * i:QT * i + QT], mv[:, QT * i:QT * i + QT, 1], ACT.Sqrt,
                                   bias=epsc[:, 0:1]).then_inc(s_sq, 1)
                act.wait_ge(s_in, 16 * 4)
                act.activation(wg_hi[:, :, :], wg_raw[:, :, :], ACT.Copy).then_inc(s_g, 1)
                for n in range(4 * KH):
                    i, k = n // KH, n % KH
                    act.wait_ge(s_t2, n + 1)
                    act.activation(xnT_hi[:, k, 512 * i:512 * i + 512], PS[:, n, :], ACT.Copy).then_inc(s_h2, 1)
                act.wait_ge(s_q, 3)
                act.activation(pr[:, :, :], pr[:, :, :], ACT.Exp).then_inc(s_e, 1)
                act.activation(sm[:, :], lg[:, :, E], ACT.Exp, scale=-1.0).then_inc(s_e, 1)

            @block.vector
            def _(dve):
                dve.tensor_copy(ident_b[:, :], ident[:, :]).then_inc(s_idb, 1)
                dve.wait_ge(s_rn, 1)
                dve.reciprocal(rn[:, :], std[:, :]).then_inc(s_d, 1)
                for i in range(TILES // 2):
                    dve.wait_ge(s_tr, i + 1)
                    for t in (2 * i, 2 * i + 1):
                        ins = dve.bn_stats(st[:, t, :], tile_ps(t))
                ins.then_inc(s_d, 1)
                dve.wait_ge(s_d, 2)
                for t in range(TILES):
                    ins = dve.bn_aggr(mv[:, t, :], st[:, t, :])
                dve.tensor_tensor(v2[:, :], rn[:, :], rn[:, :], ALU.mult).then_inc(s_xn2, 1)
                dve.wait_ge(s_xn2, 1)
                dve.tensor_tensor(v2[:, :], v2[:, :], mv[:, :, 1], ALU.mult).then_inc(s_d, 1)
                dve.wait_ge(s_ac, 1)
                dve.reciprocal(rstd[:, :], std[:, :]).then_inc(s_d, 1)
                dve.wait_ge(s_d, 4)
                dve.tensor_tensor(scl[:, :], rstd[:, :], rn[:, :], ALU.mult).then_inc(s_d, 1)
                dve.wait_ge(s_d, 5)
                dve.scalar_tensor_tensor(shf[:, :], mv[:, :, 0], -1.0, scl[:, :], ALU.mult, ALU.mult).then_inc(s_d, 1)
                dve.wait_ge(s_in, 16 * 4)
                for i in range(4):
                    a, b = QT * i, QT * i + QT
                    dve.wait_ge(s_xo, b)
                    dve.tensor_tensor(x1[:, a:b, :], x1[:, a:b, :], xo[:, a:b, :], ALU.add).then_inc(s_x1, 1)
                    dve.wait_ge(s_x1, i + 1)
                    for t in range(a, b):
                        ins = dve.bn_stats(st[:, t, :], x1[:, t, :])
                    ins.then_inc(s_st, 1)
                    dve.wait_ge(s_st, 2 * i + 1)
                    for t in range(a, b):
                        ins = dve.bn_aggr(mv[:, t, :], st[:, t, :])
                    ins.then_inc(s_st, 1)
                for i in range(4):
                    a, b = QT * i, QT * i + QT
                    dve.wait_ge(s_sq, i + 1)
                    dve.reciprocal(rstd[:, a:b], std[:, a:b]).then_inc(s_rs2, 1)
                    dve.wait_ge(s_rs2, i + 1)
                    for t in range(a, b):
                        ins = dve.tensor_scalar(xo[:, t, :], x1[:, t, :], mv[:, t, 0:1], rstd[:, t:t + 1],
                                                ALU.subtract, ALU.mult)
                    ins.then_inc(s_n, 1)
                dve.wait_ge(s_g, 1)
                dve.tensor_tensor(wg_lo[:, :, :], wg_raw[:, :, :], wg_hi[:, :, :].bitcast(fp32),
                                  ALU.subtract).then_inc(s_g, 1)
                dve.tensor_copy(f_hot[:, :], hot_raw[:, :])
                for n in range(4 * KH):
                    i, k = n // KH, n % KH
                    dve.wait_ge(s_h2, n + 1)
                    dve.tensor_tensor(xnT_lo[:, k, 512 * i:512 * i + 512], PS[:, n, :],
                                      xnT_hi[:, k, 512 * i:512 * i + 512].bitcast(fp32),
                                      ALU.subtract).then_inc(s_l2, 1)
                dve.wait_ge(s_lg, 1)
                dve.tensor_copy(lg[:, :, :], PS[:, 0, 0:TILES * (ROUTES + 1)].rearrange("p (t r) -> p t r", t=TILES)).then_inc(s_q, 1)
                dve.wait_ge(s_q, 1)
                dve.tensor_reduce(mx[:, :], lg[:, :, 0:E], AX.X, ALU.max).then_inc(s_q, 1)
                dve.wait_ge(s_q, 2)
                dve.tensor_tensor(pr[:, :, :], lg[:, :, 0:E], mx[:, :].unsqueeze(2).to_broadcast([128, TILES, E]),
                                  ALU.subtract).then_inc(s_q, 1)
                dve.wait_ge(s_e, 1)
                dve.tensor_reduce(mx[:, :], pr[:, :, :], AX.X, ALU.add).then_inc(s_q, 1)
                dve.wait_ge(s_e, 2)
                dve.tensor_scalar(sm[:, :], sm[:, :], 1.0, None, ALU.add).then_inc(s_q, 1)
                dve.wait_ge(s_q, 5)
                dve.reciprocal(mx[:, :], mx[:, :]).then_inc(s_q, 1)
                dve.reciprocal(comb[:, :, E], sm[:, :]).then_inc(s_q, 1)
                dve.wait_ge(s_q, 7)
                dve.tensor_tensor(pr[:, :, :], pr[:, :, :], mx[:, :].unsqueeze(2).to_broadcast([128, TILES, E]),
                                  ALU.mult).then_inc(s_q, 1)
                dve.wait_ge(s_q, 8)
                full = [128, TILES, E, E]
                other = pr[:, :, :].unsqueeze(2).to_broadcast(full)
                own = pr[:, :, :].unsqueeze(3).to_broadcast(full)
                before = tie[:, :].rearrange("p (e o) -> p e o", e=E).unsqueeze(1).to_broadcast(full)
                dve.tensor_tensor(gts[:, :, :, :], other, own, ALU.is_gt).then_inc(s_q, 1)
                dve.tensor_tensor(eqs[:, :, :, :], other, own, ALU.is_equal).then_inc(s_q, 1)
                dve.wait_ge(s_q, 10)
                dve.tensor_tensor(eqs[:, :, :, :], eqs[:, :, :, :], before, ALU.mult).then_inc(s_q, 1)
                dve.wait_ge(s_q, 11)
                dve.tensor_tensor(gts[:, :, :, :], gts[:, :, :, :], eqs[:, :, :, :], ALU.add).then_inc(s_q, 1)
                dve.wait_ge(s_q, 12)
                dve.tensor_reduce(rank[:, :, :], gts[:, :, :, :], AX.X, ALU.add).then_inc(s_q, 1)
                dve.wait_ge(s_q, 13)
                dve.scalar_tensor_tensor(comb[:, :, 0:E], rank[:, :, :], 2.0, pr[:, :, :], ALU.is_lt,
                                         ALU.mult).then_inc(s_q, 1)
                dve.wait_ge(s_q, 14)
                src = comb
                for i in range(PARTS):
                    dve.tensor_copy(cparts[:, :, i, :], src[:, :, :]).then_inc(s_cp, 1)
                    if i < PARTS - 1:
                        dve.wait_ge(s_cp, i + 1)
                        dve.tensor_tensor(comb_r[:, :, :], src[:, :, :], cparts[:, :, i, :], ALU.subtract).then_inc(s_q, 1)
                        dve.wait_ge(s_q, 15 + i)
                        src = comb_r
                dve.wait_ge(s_ct, 1)
                dve.tensor_copy(combT[:, :], PS[0:CROWS, 1:3, :].bitcast(bf16).rearrange("p b t -> p (b t)"))
        s2.close()

        s3 = ExitStack()
        sb = make_sb(s3)
        wf_hi = sb("wf_hi", [128, 2, 768], f32r)
        wf_lo = sb("wf_lo", [128, 2, 768], f32r)
        sl = sb("sl", [128, 2, UT], fp32)
        hm = sb("hm", [128, 2, UT], fp32)
        hc = sb("hc", [128, 2, UT], fp32)
        h_hi = sb("h_hi", [128, CHUNKS, UT], f32r)
        h_lo = sb("h_lo", [128, CHUNKS, UT], f32r)
        f1_done, f2_done, p_done = sem("fc1_done"), sem("fc2_done"), sem("moe_proj_done")
        sl_done, hhi_done, wfh_done = sem("fc1_silu_done"), sem("h_hi_done"), sem("moe_w_hi_done")
        hm_done, hc_done, fa_done = sem("h_done"), sem("h_scaled"), sem("moe_proj_added")
        hlo_done, wfl_done = sem("h_lo_done"), sem("moe_w_lo_done")

        def hidden_tiles(eng, body):
            body(0, 0, 0, False)
            with eng.Fori(0, (FT - 3) // 2) as i:
                body(2 * i + 1, i, 1, False)
                body(2 * i + 2, i + 1, 0, False)
            body(FT - 2, (FT - 2) // 2, 1, False)
            body(FT - 1, (FT - 1) // 2, 0, True)

        with nc.Block() as block:
            @block.sync
            def _(sp):
                def body(f, pair, par, last):
                    if last or (isinstance(f, int) and f == FT - 2):
                        return
                    sp.wait_ge(wfl_done, f + 1)
                    sp.dma_start(wf_raw[:, par, :], wf_d[f + 2, :, :]).then_inc(s_f[par], 16)
                hidden_tiles(sp, body)

            @block.tensor
            def _(pe):
                def hidden(f, par, c, which, bank, s):
                    n = 0
                    for whl, xhl in ((wf_hi, xnT_hi), (wf_hi, xnT_lo), (wf_lo, xnT_hi)):
                        for k in range(KH):
                            w0 = 256 * k + 128 * which
                            mm = pe.matmul(PS[:, bank, :], whl[:, par, w0:w0 + 128], xhl[:, k, UT * c:UT * c + UT],
                                           start=(n == 0), stop=(n == 3 * KH - 1))
                            n += 1
                    if s is not None:
                        mm.then_inc(s, 1)

                def project(j, par, c):
                    pe.wait_ge(hlo_done, j + 1)
                    need(pe, fa_done, j)
                    for m in range(KH):
                        w0 = 512 + 128 * m
                        for n, (whl, hhl) in enumerate(((wf_hi, h_hi), (wf_hi, h_lo), (wf_lo, h_hi))):
                            mm = pe.matmul(PS[:, 6 + m, :], whl[:, par, w0:w0 + 128], hhl[:, c, :],
                                           start=(n == 0), stop=(n == 2))
                    mm.then_inc(p_done, 1)

                def body(f, pair, par, last):
                    pe.wait_ge(wfl_done, f + 1)
                    for c in range(CHUNKS):
                        j = CHUNKS * f + c
                        need(pe, hc_done, j - 1)
                        hidden(f, par, c, 0, c % 2, f1_done)
                        hidden(f, par, c, 1, 2 + c % 2, None)
                        if isinstance(f, int):
                            hot = f_hot[:, 128 * f:128 * f + 128]
                        else:
                            hot = f_hot[:, bass.ds(128 * f, 128)]
                        pe.matmul(PS[:, 4 + c % 2, :], hot, combT[:, UT * c:UT * c + UT],
                                  start=True, stop=True).then_inc(f2_done, 1)
                        if not (isinstance(j, int) and j < 2):
                            project(j - 2, par if c >= 2 else 1 - par, (c - 2) % CHUNKS)
                hidden_tiles(pe, body)
                end = CHUNKS * FT
                project(end - 2, 0, CHUNKS - 2)
                project(end - 1, 0, CHUNKS - 1)

            @block.scalar
            def _(act):
                def split(f, pair, par):
                    act.wait_ge(s_f[par], 16 * (pair + 1))
                    need(act, p_done, CHUNKS * (f - 1))
                    act.activation(wf_hi[:, par, :], wf_raw[:, par, :], ACT.Copy).then_inc(wfh_done, 1)

                split(0, 0, 0)

                def high(j, c):
                    act.wait_ge(hc_done, j + 1)
                    need(act, p_done, j - 3)
                    act.activation(h_hi[:, c, :], hc[:, c % 2, :], ACT.Copy).then_inc(hhi_done, 1)

                def body(f, pair, par, last):
                    for c in range(CHUNKS):
                        j = CHUNKS * f + c
                        act.wait_ge(f1_done, j + 1)
                        need(act, hm_done, j - 1)
                        act.activation(sl[:, c % 2, :], PS[:, c % 2, :], ACT.Silu).then_inc(sl_done, 1)
                        high(j, c)
                        if c == 2 and not last:
                            split(f + 1, pair + par, 1 - par)
                hidden_tiles(act, body)

            @block.vector
            def _(dve):
                def add_up(j, c):
                    dve.wait_ge(p_done, j + 1)
                    o = outT[:, :, UT * c:UT * c + UT]
                    dve.tensor_tensor(o, PS[:, 6:8, :], o, ALU.add).then_inc(fa_done, 1)

                def body(f, pair, par, last):
                    for c in range(CHUNKS):
                        j = CHUNKS * f + c
                        dve.wait_ge(sl_done, j + 1)
                        dve.wait_ge(f2_done, j + 1)
                        dve.tensor_tensor(hm[:, c % 2, :], PS[:, 2 + c % 2, :], sl[:, c % 2, :], ALU.mult).then_inc(hm_done, 1)
                        dve.wait_ge(hm_done, j + 1)
                        need(dve, hlo_done, j - 1)
                        dve.tensor_tensor(hc[:, c % 2, :], PS[:, 4 + c % 2, :], hm[:, c % 2, :], ALU.mult).then_inc(hc_done, 1)
                        if not (isinstance(j, int) and j < 2):
                            add_up(j - 2, (c - 2) % CHUNKS)
                hidden_tiles(dve, body)
                end = CHUNKS * FT
                add_up(end - 2, CHUNKS - 2)
                add_up(end - 1, CHUNKS - 1)

            @block.gpsimd
            def _(pool):
                def split(f, pair, par):
                    pool.wait_ge(wfh_done, f + 1)
                    pool.tensor_tensor(wf_lo[:, par, :], wf_raw[:, par, :], wf_hi[:, par, :].bitcast(fp32),
                                       ALU.subtract).then_inc(wfl_done, 1)

                split(0, 0, 0)

                def body(f, pair, par, last):
                    for c in range(CHUNKS):
                        j = CHUNKS * f + c
                        pool.wait_ge(hhi_done, j + 1)
                        pool.tensor_tensor(h_lo[:, c, :], hc[:, c % 2, :], h_hi[:, c, :].bitcast(fp32),
                                           ALU.subtract).then_inc(hlo_done, 1)
                        if c == 2 and not last:
                            split(f + 1, pair + par, 1 - par)
                hidden_tiles(pool, body)
        s3.close()

        sb = make_sb(outer)
        res = sb("res", [128, TILES, HID], fp32)
        s_tr4, s_d4, s_a4, s_o4, s_out = sem("s4_turned"), sem("s4_dve"), sem("s4_act"), sem("s4_sum"), sem("s4_out")
        s_sc4 = sem("s4_scaled")
        out_v = out_d.rearrange("(t p) c -> p t c", p=128)

        with nc.Block() as block:
            @block.tensor
            def _(pe):
                for t in range(TILES):
                    for k in range(KH):
                        mm = pe.transpose(PS[:, t // 2, HID * (t % 2) + 128 * k:HID * (t % 2) + 128 * k + 128],
                                          outT[:, k, 128 * t:128 * t + 128], ident[:, :])
                    if t % 2:
                        mm.then_inc(s_tr4, 1)

            @block.vector
            def _(dve):
                for i in range(4):
                    a, b = QT * i, QT * i + QT
                    for t in range(a, b):
                        dve.wait_ge(s_tr4, t // 2 + 1)
                        ins = dve.bn_stats(st[:, t, :], tile_ps(t))
                    ins.then_inc(s_d4, 1)
                    dve.wait_ge(s_d4, 4 * i + 1)
                    for t in range(a, b):
                        ins = dve.bn_aggr(mv[:, t, :], st[:, t, :])
                    ins.then_inc(s_d4, 1)
                    dve.wait_ge(s_a4, i + 1)
                    dve.reciprocal(rstd[:, a:b], std[:, a:b]).then_inc(s_d4, 1)
                    dve.wait_ge(s_d4, 4 * i + 3)
                    dve.scalar_tensor_tensor(shf[:, a:b], mv[:, a:b, 0], -1.0, rstd[:, a:b], ALU.mult,
                                             ALU.mult).then_inc(s_d4, 1)
                    dve.wait_ge(s_sc4, b)
                    dve.tensor_tensor(res[:, a:b, :], res[:, a:b, :], x1[:, a:b, :], ALU.add).then_inc(s_o4, 1)

            @block.scalar
            def _(act):
                for i in range(4):
                    a, b = QT * i, QT * i + QT
                    act.wait_ge(s_d4, 4 * i + 2)
                    act.activation(std[:, a:b], mv[:, a:b, 1], ACT.Sqrt, bias=epsc[:, 0:1]).then_inc(s_a4, 1)
                    act.wait_ge(s_d4, 4 * i + 4)
                    for t in range(a, b):
                        act.activation(res[:, t, :], tile_ps(t), ACT.Identity, scale=rstd[:, t:t + 1],
                                       bias=shf[:, t:t + 1]).then_inc(s_sc4, 1)

            @block.sync
            def _(sp):
                for i in range(4):
                    a, b = QT * i, QT * i + QT
                    sp.wait_ge(s_o4, i + 1)
                    sp.dma_start(out_v[:, a:b, :], res[:, a:b, :]).then_inc(s_out, 16)
                sp.wait_ge(s_out, 16 * 4)


def kernel(L0_attn_hidden_states, L0_attn_in_proj_w, L0_attn_conv_w, L0_attn_conv_b, L0_attn_dt_bias,
           L0_attn_A_log, L0_attn_D, L0_attn_norm_w, L0_attn_out_proj_w, L0_ffn_gate_w, L0_ffn_expert_fc1,
           L0_ffn_expert_fc2, L0_ffn_expert_proj, L0_ffn_shared_fc1, L0_ffn_shared_fc2, L0_ffn_shared_proj,
           L0_ffn_shared_gate_w):
    import numpy as np
    import concourse.bacc as bacc
    from concourse import mybir as mb
    from concourse.bass_utils import run_bass_kernel_spmd

    G, CT, HID, INTER, GN, H = 8, 4, 256, 4096, 1024, 64
    E, F, FS, FT = 8, 176, 704, 17
    a = np.asarray
    x = a(L0_attn_hidden_states).reshape(-1, HID)
    w = a(L0_attn_in_proj_w)
    wz, wx, wB, wC, wdt = (w[i:j] for i, j in ((0, INTER), (INTER, 2 * INTER), (2 * INTER, 2 * INTER + GN),
                                               (2 * INTER + GN, 2 * INTER + 2 * GN), (2 * INTER + 2 * GN, w.shape[0])))

    def by_group(bcx, *rest):
        B, C, X = bcx
        return np.concatenate([v.reshape(G, -1, *rest) for v in (B, C, X)], axis=1)

    def k_major(v):
        n = v.shape[1]
        return v.transpose(0, 2, 1).reshape(v.shape[0], 2, 128, n).transpose(0, 2, 1, 3).reshape(v.shape[0], 128, 2 * n)

    cw, cb = a(L0_attn_conv_w), a(L0_attn_conv_b)
    bcx = lambda v: (v[INTER:INTER + GN], v[INTER + GN:], v[:INTER])
    tiles = lambda v, n: v.reshape(G, n, 128, -1).transpose(0, 2, 1, 3).reshape(G, 128, -1)
    par = np.concatenate([tiles(by_group(bcx(cw), 4), CT + 2), tiles(by_group(bcx(cb)), CT + 2),
                          tiles(np.repeat(a(L0_attn_D), INTER // H), CT), tiles(a(L0_attn_norm_w), CT)], axis=2)
    wo = a(L0_attn_out_proj_w).T.reshape(G, CT, 128, HID).transpose(0, 2, 1, 3).reshape(G, 128, CT * HID)
    pad = np.zeros((FT * 128 - E * F - FS, HID), np.float32)
    fc = [np.concatenate([a(e).reshape(E * F, HID), a(s), pad]).reshape(FT, 128, 2, 128) for e, s in
          ((L0_ffn_expert_fc1, L0_ffn_shared_fc1), (L0_ffn_expert_fc2, L0_ffn_shared_fc2))]
    w12 = np.stack(fc, axis=3).transpose(0, 4, 2, 3, 1).reshape(FT, 128, 512)
    wp = np.concatenate([a(L0_ffn_expert_proj).transpose(0, 2, 1).reshape(E * F, HID), a(L0_ffn_shared_proj).T, pad])
    wf = np.concatenate([w12, wp.reshape(FT, 128, HID)], axis=2)
    wg = np.concatenate([a(L0_ffn_gate_w), a(L0_ffn_shared_gate_w), np.zeros((1, HID), np.float32)])

    one = lambda v: np.asarray(v, np.float32)
    i, j = np.arange(128)[None, :], np.arange(128)[:, None]
    upper = one(j <= i)
    squares = np.concatenate([one(i == j), upper, -one(j > i)], axis=1)
    mask = np.concatenate([upper, np.ones((128, 128), np.float32), upper], axis=1)
    tie = np.tile(one(np.arange(E)[None, :] < np.arange(E)[:, None]).reshape(1, -1), (128, 1))
    after = one(np.arange(128)[None, None, :] > 64 * np.arange(2)[None, :, None] + np.arange(64)[:, None, None])
    after = np.stack([after, 0 * after, after], axis=2)
    l_const = np.concatenate([np.zeros((24, 768), np.float32), np.ones((3, 768), np.float32), after.reshape(64, -1)])
    r_const = np.concatenate([np.repeat(np.tile(-np.eye(8, dtype=np.float32), (3, 1)), 64, axis=1),
                              np.zeros((3, 512), np.float32),
                              np.tile(np.eye(64, dtype=np.float32) * np.float32(-2.0 ** 120), (1, 8))])
    route = np.concatenate([np.repeat(np.arange(E), F), np.full(FT * 128 - E * F, E)])
    f_hot = np.tile(one(np.arange(E + 1)[:, None] == route[None, :]), (3, 1))

    ins = dict(x=x, wx=k_major(by_group(bcx(np.concatenate([wx, wB, wC])), HID)), wz=k_major(wz.reshape(G, -1, HID)),
               wo=wo, par=par, wdt=k_major(wdt[None])[0], dtb=np.tile(a(L0_attn_dt_bias), (128, 1)),
               alog=np.tile(a(L0_attn_A_log), (128, 1)), wf=wf, wg=k_major(wg[None])[0], squares=squares, mask=mask,
               tie=tie, l_const=l_const, r_const=r_const, f_hot=f_hot)
    nc = bacc.Bacc("TRN2", target_bir_lowering=False, num_devices=1)
    arrays, aps = {}, []
    for name, v in ins.items():
        v = np.ascontiguousarray(v)
        arrays[f"in_{name}"] = v
        aps.append(nc.dram_tensor(f"in_{name}", v.shape, mb.dt.from_np(v.dtype), kind="ExternalInput").ap())
    aps.append(nc.dram_tensor("out", x.shape, mb.dt.float32, kind="ExternalOutput").ap())
    mamba_moe_sandwich_kernel(nc, *aps)
    r = run_bass_kernel_spmd(nc, [arrays], core_ids=[0])
    return r.results[0]["out"].reshape(a(L0_attn_hidden_states).shape)
```

```python
import concourse.bass as bass
from concourse import mybir
from contextlib import ExitStack


def mamba_moe_sandwich_kernel(nc, x_d, wx_d, wz_d, wo_d, par_d, wdt_d, dtb_d, alog_d,
                              wf_d, wg_d, sq_const_d, mask_d, tie_d, l_const_d, r_const_d, f_hot_d, out_d):
    fp32, f32r, bf16 = mybir.dt.float32, mybir.dt.float32r, mybir.dt.bfloat16
    ALU = mybir.AluOpType
    ACT = mybir.ActivationFunctionType
    AX = mybir.AxisListType

    NBATCH, SEQ, HID = 8, 256, 256
    TOK = NBATCH * SEQ
    TILES = TOK // 128
    KH = HID // 128
    GROUPS, HPG, P = 8, 8, 64
    HEADS = GROUPS * HPG
    CT = HPG * P // 128
    CONVT = CT + 2
    TAPS = 4
    PAIRS = NBATCH // 2
    UT = 2 * SEQ
    PARTS = 3
    LROWS = PARTS * HPG
    SUMS = LROWS + PARTS
    DROWS = SUMS + 64
    INTER = HEADS * P
    E, ROUTES = 8, 9
    FT = 17
    CROWS = PARTS * ROUTES
    CHUNKS = TOK // UT
    EPS = 1e-5
    NPAR = CONVT * TAPS + CONVT + CT + CT
    PA = CONVT * TAPS + CONVT
    XBANK = (0, 1, 0, 7, 0, 1)
    ZBANK = (7, 1, 7, 1)
    BLK = 3
    BORDER = (0, 2, 1)

    outer = ExitStack()
    with outer:
        def sem(name):
            return outer.enter_context(nc.semaphore(name))

        def need(eng, s, value):
            if isinstance(value, int) and value <= 0:
                return
            eng.wait_ge(s, value)

        cs_parts = nc.dram_tensor("cs_parts", (GROUPS, LROWS, NBATCH * BLK * 128), bf16, kind="Internal").ap()

        def make_sb(stack):
            return lambda name, shape, dt: stack.enter_context(nc.sbuf_tensor(name, shape, dt))

        sb = make_sb(outer)
        PS = outer.enter_context(nc.psum_tensor("PS", [128, 8, 512], fp32))

        xnT_hi = sb("xnT_hi", [128, KH, TOK], f32r)
        xnT_lo = sb("xnT_lo", [128, KH, TOK], f32r)
        outT = sb("outT", [128, KH, TOK], fp32)
        ident = sb("ident", [128, 128], fp32)
        ssq = sb("ssq", [128, TOK], fp32)
        epsc = sb("epsc", [128, 1], fp32)
        ones = sb("ones", [128, 1], fp32)
        XWORDS, MWORDS = CT * UT, BLK * HPG * 128
        shared = sb("shared", [128, XWORDS + MWORDS], fp32)
        x1 = shared[:, 0:TILES * HID].rearrange("p (t c) -> p t c", c=HID)
        acc = sb("acc", [128, 3, UT], fp32)
        acc_flat = acc[:, :, :].rearrange("p s t -> p (s t)")
        taken = [0]

        def stat(n):
            taken[0] += TILES * n
            v = acc_flat[:, taken[0] - TILES * n:taken[0]]
            return v.rearrange("p (t n) -> p t n", n=n) if n > 1 else v

        st, mv = [stat(6), stat(6)], [stat(2), stat(2)]
        std, rstd = [stat(1), stat(1)], [stat(1), stat(1)]
        rn, rn2, v2, scl = stat(1), stat(1), stat(1), stat(1)
        shf = [stat(1) for i in range(3)]

        mamba = ExitStack()
        sb = make_sb(mamba)
        dt_sb = sb("dt_sb", [128, TILES, GROUPS, HPG], fp32)
        wraw = sb("wraw", [128, KH * CONVT * 128], fp32)
        praw = sb("praw", [128, NPAR], fp32)
        wx_hi = sb("wx_hi", [128, KH, CONVT * 128], f32r)
        wx_lo = sb("wx_lo", [128, KH, CONVT * 128], f32r)
        wz_hi = sb("wz_hi", [128, KH, CT * 128], f32r)
        wz_lo = sb("wz_lo", [128, KH, CT * 128], f32r)
        wo_hi = sb("wo_hi", [128, CT, HID], f32r)
        wo_lo = sb("wo_lo", [128, CT, HID], f32r)
        par_a = sb("par_a", [128, PA], fp32)
        xT = [shared[:, 0:XWORDS].rearrange("p (c t) -> p c t", c=CT), sb("xT", [128, CT, UT], fp32)]
        BC = sb("BC", [128, 2, 2, UT], fp32)
        mask = sb("mask", [128, BLK * 128], fp32)
        L = sb("L", [DROWS, 2, 2, BLK * 128], bf16)
        R = sb("R", [DROWS, 2, 2, 2, HPG, 64], bf16)
        wraw_x = wraw[:, :].rearrange("p (k n) -> p k n", k=KH)
        wraw_z = wraw[:, 0:KH * CT * 128].rearrange("p (k n) -> p k n", k=KH)
        wraw_o = wraw[:, 0:CT * HID].rearrange("p (c n) -> p c n", c=CT)

        s0 = ExitStack()
        sb = make_sb(s0)
        umask = sb("umask", [128, 128], fp32)
        sufmask = sb("sufmask", [128, 128], fp32)
        wdt_raw = sb("wdt_raw", [128, KH, HEADS], fp32)
        wdt_hi = sb("wdt_hi", [128, KH, HEADS], f32r)
        wdt_lo = sb("wdt_lo", [128, KH, HEADS], f32r)
        dtb = sb("dtb", [128, HEADS], fp32)
        alog = sb("alog", [128, HEADS], fp32)
        expA = sb("expA", [128, HEADS], fp32)
        st0 = sb("st0", [128, TILES, 6], fp32)
        mv0 = sb("mv0", [128, TILES, 2], fp32)
        std0 = sb("std0", [128, TILES], fp32)
        rstd0 = sb("rstd0", [128, TILES], fp32)
        xn = sb("xn", [128, TILES, HID], fp32)
        xn_flat = xn[:, :, :].rearrange("p t c -> p (t c)")
        dt_v, dt_e, dt_w, dt_l = (xn_flat[:, TILES * HEADS * i:TILES * HEADS * (i + 1)] for i in range(4))
        dt_r = sb("dt_r", [128, TILES * HEADS], fp32)
        dtT = sb("dtT", [HEADS, TOK], fp32)
        CSN = NBATCH // 2 * BLK * 128
        csr = [shared[:, XWORDS + CSN * i:XWORDS + CSN * i + CSN] for i in range(2)]
        l_const = sb("l_const", [DROWS, 2 * BLK * 128], fp32)
        r_const = sb("r_const", [DROWS, HPG * 64], fp32)
        csp = [sb(f"csp{i}", [128, CSN], bf16) for i in range(PARTS)]
        x_v = outT[:, :, :].rearrange("p k t -> p (k t)").rearrange("p (t c) -> p t c", c=HID)
        xd_v = x_d.rearrange("(t p) c -> p t c", p=128)

        s_x0 = [sem(f"s0_x{i}") for i in range(4)]
        s_c0 = sem("s0_const_in")
        s_id = sem("s0_ident_in")
        s_par = sem("params_in")
        s_raw = sem("weights_in")
        s_stat = sem("s0_stat")
        s_sqrt = sem("s0_sqrt")
        s_rstd = sem("s0_rstd")
        s_xn = sem("s0_xn")
        s_xt = sem("s0_xt")
        s_hi0 = sem("s0_hi")
        s_lo0 = sem("s0_lo")
        s_wdt = sem("s0_wdt")
        s_dtp = sem("s0_dt_psum")
        s_v = sem("s0_softplus_dve")
        s_a = sem("s0_softplus_act")
        s_cs = sem("s0_cs_psum")
        s_p = sem("s0_parts_act")
        s_r = sem("s0_rest_dve")
        s_scr = sem("s0_scratch_out")
        s_ms = sem("s0_memset")
        s_dtT = sem("s0_dt_copied")
        s_dtt = sem("s0_dt_turned")
        QT = TILES // 4

        a_done, z_done, t_done, cb_done = sem("a_done"), sem("z_done"), sem("t_done"), sem("cb_done")
        d_done, yt_done, o_done = sem("decay_done"), sem("yT_done"), sem("proj_done")
        t0_done, xs_done, zs_done = sem("tap3_done"), sem("conv_silu_done"), sem("z_silu_done")
        exp_done = sem("exp_done")
        sq_done, hi_done = sem("y_squared"), sem("g_hi_done")
        wx_hi_done, wz_hi_done, wo_hi_done, wo_scaled = sem("wx_hi_done"), sem("wz_hi_done"), sem("wo_hi_done"), sem("wo_scaled")
        cbm_done, conv_done, tap_link, m_done = sem("cb_masked"), sem("conv_done"), sem("tap_link"), sem("m_done")
        y_done, xdt_done, oacc_done = sem("y_done"), sem("xdt_done"), sem("proj_added")
        pa_done, pd_done = sem("conv_params_ready"), sem("skip_params_ready")
        ssq_link, gy_done, lo_done = sem("squares_added"), sem("gated_done"), sem("g_lo_done")
        wx_lo_done, wz_lo_done, wo_lo_done = sem("wx_lo_done"), sem("wz_lo_done"), sem("wo_lo_done")
        l_in = [sem(f"l_in{b}") for b in range(2)]
        r_in = [sem(f"r_in{b}") for b in range(2)]

        s_var, s_tr, s_rn = sem("s2_var_psum"), sem("s2_outT_turned"), sem("s2_std")
        s_x1in = [sem(f"s2_x{i}_in") for i in range(CHUNKS)]
        s_link, s_v2, s_sd = sem("s2_dve_link"), sem("s2_variance"), sem("s2_row_std")
        s_x1 = sem("s2_residual")
        BANK1 = (2, 0, 4, 2)
        BANKV = (5, 5, 5, 7)

        def quarter(i):
            return slice(QT * i, QT * i + QT)

        links = [0]

        def linked(dve, ins):
            links[0] += 1
            ins.then_inc(s_link, 1)
            dve.wait_ge(s_link, links[0])

        def norms(act, n, a, b):
            act.wait_ge(s_var, b // QT)
            act.activation(rn[:, a:b], PS[:, BANKV[a // QT], a:b], ACT.Sqrt, scale=1.0 / INTER,
                           bias=epsc[:, 0:1]).then_inc(s_rn, 1)

        def inverse_norms(dve, n, a, b):
            dve.wait_ge(s_rn, n + 1)
            linked(dve, dve.reciprocal(rn[:, a:b], rn[:, a:b]))
            linked(dve, dve.tensor_tensor(rn2[:, a:b], rn[:, a:b], rn[:, a:b], ALU.mult))

        def stats(dve, i):
            dve.wait_ge(s_tr, i + 1)
            for t in range(QT):
                ins = dve.bn_stats(st[0][:, QT * i + t, :], rows_ps(BANK1[i], t))
            linked(dve, ins)
            for t in range(QT):
                ins = dve.bn_aggr(mv[0][:, QT * i + t, :], st[0][:, QT * i + t, :])
            linked(dve, ins)

        def variance(dve, i):
            dve.tensor_tensor(v2[:, quarter(i)], rn2[:, quarter(i)], mv[0][:, quarter(i), 1], ALU.mult).then_inc(s_v2, 1)

        def row_std(act, i):
            act.wait_ge(s_v2, i + 1)
            act.activation(std[0][:, quarter(i)], v2[:, quarter(i)], ACT.Sqrt, bias=epsc[:, 0:1]).then_inc(s_sd, 1)

        def scales(dve, i):
            q = quarter(i)
            dve.wait_ge(s_sd, i + 1)
            linked(dve, dve.reciprocal(rstd[0][:, q], std[0][:, q]))
            linked(dve, dve.tensor_tensor(scl[:, q], rstd[0][:, q], rn[:, q], ALU.mult))
            dve.scalar_tensor_tensor(shf[0][:, q], mv[0][:, q, 0], -1.0, scl[:, q], ALU.mult, ALU.mult)

        def residual(dve, i):
            dve.wait_ge(s_x1in[i], 16)
            for t in range(QT):
                n = QT * i + t
                dve.scalar_tensor_tensor(x1[:, n, :], rows_ps(BANK1[i], t), scl[:, n:n + 1], x1[:, n, :],
                                         ALU.mult, ALU.add).then_inc(s_x1, 1)

        def rows_ps(bank, i):
            return PS[:, bank + i // 2, HID * (i % 2):HID * (i % 2) + HID]

        def turn_out(pe, i):
            for t in range(QT):
                for k in range(KH):
                    mm = pe.transpose(rows_ps(BANK1[i], t)[:, 128 * k:128 * k + 128],
                                      outT[:, k, UT * i + 128 * t:UT * i + 128 * t + 128], ident[:, :])
            mm.then_inc(s_tr, 1)

        def sum_squares(pe, i):
            for t in range(QT * i, QT * i + QT):
                mm = pe.matmul(PS[:, BANKV[i], t:t + 1], ssq[:, 128 * t:128 * t + 128], ones[:, :], start=True, stop=True)
            mm.then_inc(s_var, 1)

        LASTO = (6, 7)
        PT = PS[:, 4, :]
        PO = PS[:, 6, :]
        PY = PS[:, 5, :].rearrange("p (c t) -> p c t", c=2)
        PD = PS[:, 2:4, :]

        def load_lr(sp, g, q, b, bt):
            need(sp, d_done, BLK * (bt - 2) + BLK)
            n = 2 * q + b
            src = cs_parts[g, :, BLK * 128 * n:BLK * 128 * n + BLK * 128]
            sp.dma_start(L[0:LROWS, b, :, :], src.unsqueeze(1).to_broadcast([LROWS, 2, BLK * 128])).then_inc(l_in[b], 16)
            rows = src.rearrange("(p h) t -> p h t", h=HPG)
            for c in range(2):
                for s in range(2):
                    t = 256 * c + 64 * s
                    sp.dma_start(R[LROWS:SUMS, b, c, s, :, :], rows[:, :, t:t + 64]).then_inc(r_in[b], 16)

        def in_proj(pe, bank, whi, wlo, c0, q, s):
            n = 0
            for lhs, rhs in ((whi, xnT_hi), (whi, xnT_lo), (wlo, xnT_hi)):
                for k in range(KH):
                    mm = pe.matmul(PS[:, bank, :], lhs[:, k, c0:c0 + 128], rhs[:, k, UT * q:UT * q + UT],
                                   start=(n == 0), stop=(n == 3 * KH - 1))
                    n += 1
            mm.then_inc(s, 1)

        def conv_in(pe, g, q, v, k, free):
            need(pe, *free)
            pe.wait_ge(wx_lo_done, CONVT * g + k + 1)
            in_proj(pe, XBANK[k], wx_hi, wx_lo, 128 * k, q, a_done)

        def tap3(act, g, v, k):
            n = CONVT * v + k
            act.wait_ge(a_done, n + 1)
            act.wait_ge(pa_done, g + 1)
            need(act, xs_done, n - 2)
            act.activation(acc[:, k % 3, :], PS[:, XBANK[k], :], ACT.Identity,
                           scale=par_a[:, TAPS * k + TAPS - 1:TAPS * k + TAPS],
                           bias=par_a[:, TAPS * CONVT + k:TAPS * CONVT + k + 1]).then_inc(t0_done, 1)

        def conv_silu(act, vp, v, k):
            act.wait_ge(conv_done, CONVT * v + k + 1)
            if k < 2:
                need(act, cb_done, 2 * v - 2)
                dst = BC[:, vp, k, :]
            else:
                need(act, y_done, 4 * v - 5 + (k - 2) // 2)
                dst = xT[vp][:, k - 2, :]
            act.activation(dst, acc[:, k % 3, :], ACT.Silu).then_inc(xs_done, 1)

        def split_x_hi(act, g, k):
            act.wait_ge(s_raw, 48 * g + 16)
            need(act, a_done, CONVT * PAIRS * g - CONVT + k + 1)
            act.activation(wx_hi[:, :, 128 * k:128 * k + 128], wraw_x[:, :, 128 * k:128 * k + 128],
                           ACT.Copy).then_inc(wx_hi_done, 1)

        def split_z_hi(act, g, ct):
            act.wait_ge(s_raw, 48 * g + 32)
            need(act, z_done, CT * PAIRS * g - CT + ct + 1)
            act.activation(wz_hi[:, :, 128 * ct:128 * ct + 128], wraw_z[:, :, 128 * ct:128 * ct + 128],
                           ACT.Copy).then_inc(wz_hi_done, 1)

        def conv(dve, g, v, k, s):
            n = CONVT * v + k
            if s == 1:
                dve.wait_ge(t0_done, n + 1)
                dve.wait_ge(pa_done, g + 1)
            else:
                dve.wait_ge(tap_link, 2 * n + s - 1)
            src = PS[:, XBANK[k], :].rearrange("p (b t) -> p b t", b=2)
            dst = acc[:, k % 3, :].rearrange("p (b t) -> p b t", b=2)
            dve.scalar_tensor_tensor(dst[:, :, s:SEQ], src[:, :, 0:SEQ - s],
                                     par_a[:, TAPS * k + TAPS - 1 - s:TAPS * k + TAPS - s],
                                     dst[:, :, s:SEQ], ALU.mult, ALU.add)\
               .then_inc(conv_done if s == TAPS - 1 else tap_link, 1)

        def conv_params(dve, g):
            dve.wait_ge(s_par, 16 * g + 16)
            need(dve, t0_done, CONVT * PAIRS * g)
            need(dve, conv_done, CONVT * PAIRS * g)
            dve.tensor_copy(par_a[:, :], praw[:, 0:PA]).then_inc(pa_done, 1)

        def split_x_lo(pool, g, k):
            pool.wait_ge(wx_hi_done, CONVT * g + k + 1)
            n = slice(128 * k, 128 * k + 128)
            pool.tensor_tensor(wx_lo[:, :, n], wraw_x[:, :, n], wx_hi[:, :, n].bitcast(fp32),
                               ALU.subtract).then_inc(wx_lo_done, 1)

        def split_z_lo(pool, g, ct):
            pool.wait_ge(wz_hi_done, CT * g + ct + 1)
            n = slice(128 * ct, 128 * ct + 128)
            pool.tensor_tensor(wz_lo[:, :, n], wraw_z[:, :, n], wz_hi[:, :, n].bitcast(fp32),
                               ALU.subtract).then_inc(wz_lo_done, 1)

        with nc.Block() as block:
            @block.sync
            def _(sp):
                for i in range(4):
                    sp.dma_start(x_v[:, QT * i:QT * i + QT, :], xd_v[:, QT * i:QT * i + QT, :]).then_inc(s_x0[i], 16)
                    if i == 0:
                        sp.dma_start(ident[:, :], sq_const_d[:, 0:128]).then_inc(s_id, 16)
                for dst, src in ((umask, sq_const_d[:, 128:256]),
                                 (sufmask, sq_const_d[:, 256:384]), (mask, mask_d), (dtb, dtb_d),
                                 (alog, alog_d), (l_const, l_const_d), (r_const, r_const_d)):
                    sp.dma_start(dst[:, :], src).then_inc(s_c0, 16)
                sp.dma_start(wdt_raw[:, :, :], wdt_d.rearrange("p (k n) -> p k n", k=KH)).then_inc(s_c0, 16)
                sp.dma_start(praw[:, :], par_d[0, :, :]).then_inc(s_par, 16)
                sp.dma_start(wraw[:, :], wx_d[0, :, :]).then_inc(s_raw, 16)
                sp.wait_ge(wx_lo_done, CONVT)
                sp.dma_start(wraw[:, 0:KH * CT * 128], wz_d[0, :, :]).then_inc(s_raw, 16)
                for i in range(PARTS):
                    sp.wait_ge(s_p, i + 1)
                    for hf in range(2):
                        sp.dma_start(cs_parts[:, HPG * i:HPG * i + HPG, CSN * hf:CSN * hf + CSN],
                                     csp[i][HEADS * hf:HEADS * hf + HEADS, :]).then_inc(s_scr, 16)

            @block.gpsimd
            def _(pool):
                pool.memset(epsc[:, :], EPS).then_inc(s_ms, 1)
                pool.memset(ones[:, :], 1.0).then_inc(s_ms, 1)
                pool.memset(ssq[:, :], 0.0).then_inc(s_ms, 1)
                pool.wait_ge(s_c0, 16 * 8)

                def constant_rows(b):
                    pool.tensor_copy(L[:, b, :, :], l_const[:, :].rearrange("p (s n) -> p s n", s=2)).then_inc(s_ms, 1)
                    for c in range(2):
                        pool.tensor_copy(R[:, b, c, :, :, :].rearrange("p s h i -> p s (h i)"),
                                         r_const[:, :].unsqueeze(1).to_broadcast([DROWS, 2, HPG * 64])).then_inc(s_ms, 1)

                constant_rows(0)
                for k in range(CONVT):
                    split_x_lo(pool, 0, k)
                constant_rows(1)
                for ct in range(CT):
                    split_z_lo(pool, 0, ct)
                pool.wait_ge(s_xn, 4)
                pool.memset(outT[:, :, :], 0.0).then_inc(s_ms, 1)

            @block.vector
            def _(dve):
                def stats(i):
                    a, b = QT * i, QT * i + QT
                    dve.wait_ge(s_x0[i], 16)
                    for t in range(a, b):
                        ins = dve.bn_stats(st0[:, t, :], x_v[:, t, :])
                    ins.then_inc(s_stat, 1)
                    dve.wait_ge(s_stat, 2 * i + 1)
                    for t in range(a, b):
                        ins = dve.bn_aggr(mv0[:, t, :], st0[:, t, :])
                    ins.then_inc(s_stat, 1)

                def normalise(i):
                    a, b = QT * i, QT * i + QT
                    dve.wait_ge(s_sqrt, i + 1)
                    dve.reciprocal(rstd0[:, a:b], std0[:, a:b]).then_inc(s_rstd, 1)
                    dve.wait_ge(s_rstd, i + 1)
                    for t in range(a, b):
                        ins = dve.tensor_scalar(xn[:, t, :], x_v[:, t, :], mv0[:, t, 0:1], rstd0[:, t:t + 1],
                                                ALU.subtract, ALU.mult)
                    ins.then_inc(s_xn, 1)

                def low(i):
                    for k in range(KH):
                        n = KH * i + k
                        dve.wait_ge(s_hi0, n + 1)
                        dve.tensor_tensor(xnT_lo[:, k, 512 * i:512 * i + 512], PS[:, n, :],
                                          xnT_hi[:, k, 512 * i:512 * i + 512].bitcast(fp32),
                                          ALU.subtract).then_inc(s_lo0, 1)

                stats(0)
                stats(1)
                normalise(0)
                stats(2)
                normalise(1)
                stats(3)
                normalise(2)
                low(0)
                normalise(3)
                dve.wait_ge(s_wdt, 1)
                dve.tensor_tensor(wdt_lo[:, :, :], wdt_raw[:, :, :], wdt_hi[:, :, :].bitcast(fp32),
                                  ALU.subtract).then_inc(s_wdt, 1)
                for i in range(1, 4):
                    low(i)
                conv_params(dve, 0)
                per_head = lambda v: v.rearrange("p (t h) -> p t h", h=HEADS)
                dve.wait_ge(s_dtt, 1)
                dve.tensor_tensor(per_head(dt_v), PS[:, 2:4, :].rearrange("p b (t h) -> p (b t) h", h=HEADS),
                                  dtb[:, :].unsqueeze(1).to_broadcast([128, TILES, HEADS]), ALU.add).then_inc(s_v, 1)
                dve.wait_ge(s_a, 3)
                dve.tensor_scalar(dt_w, dt_e, 1.0, None, ALU.add).then_inc(s_v, 1)
                dve.wait_ge(s_v, 2)
                dve.scalar_tensor_tensor(dt_r[:, :], dt_w, -1.0, dt_e, ALU.add, ALU.subtract).then_inc(s_v, 1)
                for s in range(1, TAPS):
                    conv(dve, 0, 0, 0, s)
                dve.wait_ge(s_a, 5)
                dve.wait_ge(s_v, 3)
                dve.tensor_tensor(dt_r[:, :], dt_r[:, :], dt_e, ALU.mult).then_inc(s_v, 1)
                dve.wait_ge(s_v, 4)
                dve.tensor_tensor(dt_l, dt_l, dt_r[:, :], ALU.subtract).then_inc(s_v, 1)
                dve.wait_ge(s_v, 5)
                dt_flat = dt_sb[:, :, :, :].rearrange("p t g h -> p (t g h)")
                dve.scalar_tensor_tensor(dt_flat, dt_v, 0.0, dt_l, ALU.max, ALU.add).then_inc(s_v, 1)
                dve.wait_ge(s_v, 6)
                dve.scalar_tensor_tensor(per_head(dt_r[:, :]), per_head(dt_flat), -1.0,
                                         expA[:, :].unsqueeze(1).to_broadcast([128, TILES, HEADS]),
                                         ALU.mult, ALU.mult).then_inc(s_v, 1)
                by_seq = lambda v: v[:, :].rearrange("p (b n) -> p b n", n=BLK * 128)
                for k in range(1, CONVT):
                    if 3 <= k < 2 + PARTS:
                        i = k - 3
                        src = PS[:, 2:6, 0:BLK * 128] if i == 0 else by_seq(csr[0])
                        dve.wait_ge(s_p, i + 1)
                        dve.tensor_tensor(by_seq(csr[i]), src, by_seq(csp[i]), ALU.subtract).then_inc(s_r, 1)
                    for s in range(1, TAPS):
                        conv(dve, 0, 0, k, s)

            @block.scalar
            def _(act):
                act.wait_ge(s_ms, 1)
                for i in range(4):
                    act.wait_ge(s_stat, 2 * i + 2)
                    act.activation(std0[:, QT * i:QT * i + QT], mv0[:, QT * i:QT * i + QT, 1], ACT.Sqrt,
                                   bias=epsc[:, 0:1]).then_inc(s_sqrt, 1)
                act.wait_ge(s_c0, 16 * 8)
                act.activation(wdt_hi[:, :, :], wdt_raw[:, :, :], ACT.Copy).then_inc(s_wdt, 1)
                for n in range(4 * KH):
                    i, k = n // KH, n % KH
                    act.wait_ge(s_xt, n + 1)
                    act.activation(xnT_hi[:, k, 512 * i:512 * i + 512], PS[:, n, :], ACT.Copy).then_inc(s_hi0, 1)
                act.activation(expA[:, :], alog[:, :], ACT.Exp).then_inc(s_a, 1)
                for i in range(4):
                    act.wait_ge(s_dtp, i + 1)
                    act.activation(dtT[:, 512 * i:512 * i + 512], PS[0:HEADS, 2 + i, :], ACT.Copy).then_inc(s_dtT, 1)
                for k in range(CONVT):
                    split_x_hi(act, 0, k)
                act.wait_ge(s_v, 1)
                act.activation(dt_e, dt_v, ACT.Abs).then_inc(s_a, 1)
                act.wait_ge(s_a, 2)
                act.activation(dt_e, dt_e, ACT.Exp, scale=-1.0).then_inc(s_a, 1)
                tap3(act, 0, 0, 0)
                act.wait_ge(s_v, 2)
                act.activation(dt_l, dt_w, ACT.Ln).then_inc(s_a, 1)
                act.wait_ge(s_a, 4)
                act.wait_ge(s_v, 3)
                act.activation(dt_e, dt_l, ACT.Exp, scale=-1.0).then_inc(s_a, 1)
                tap3(act, 0, 0, 1)
                for ct in range(CT):
                    split_z_hi(act, 0, ct)
                tap3(act, 0, 0, 2)

                def part(i):
                    if i == 0:
                        act.wait_ge(s_cs, 1)
                        act.activation(csp[0][:, :].rearrange("p (b n) -> p b n", n=BLK * 128),
                                       PS[:, 2:6, 0:BLK * 128], ACT.Copy).then_inc(s_p, 1)
                    else:
                        act.wait_ge(s_r, i)
                        act.activation(csp[i][:, :], csr[i - 1][:, :], ACT.Copy).then_inc(s_p, 1)

                conv_silu(act, 0, 0, 0)
                conv_silu(act, 0, 0, 1)
                part(0)
                tap3(act, 0, 0, 3)
                conv_silu(act, 0, 0, 2)
                part(1)
                tap3(act, 0, 0, 4)
                conv_silu(act, 0, 0, 3)
                part(2)
                tap3(act, 0, 0, 5)
                conv_silu(act, 0, 0, 4)
                conv_silu(act, 0, 0, 5)

            @block.tensor
            def _(pe):
                XFREE = (0, 0, 1, 0, 3, 2)
                pe.wait_ge(s_id, 16)
                for i in range(4):
                    pe.wait_ge(s_xn, i + 1)
                    for k in range(KH):
                        for t in range(QT):
                            mm = pe.transpose(PS[:, KH * i + k, 128 * t:128 * t + 128],
                                              xn[:, QT * i + t, 128 * k:128 * k + 128], ident[:, :])
                        mm.then_inc(s_xt, 1)
                pe.wait_ge(s_wdt, 2)
                for i in range(4):
                    pe.wait_ge(s_lo0, max(KH * i + 2, i + 3))
                    n = 0
                    for lhs, rhs in ((wdt_hi, xnT_hi), (wdt_lo, xnT_hi), (wdt_hi, xnT_lo)):
                        for k in range(KH):
                            mm = pe.matmul(PS[0:HEADS, 2 + i, :], lhs[:, k, :], rhs[:, k, 512 * i:512 * i + 512],
                                           start=(n == 0), stop=(n == 3 * KH - 1))
                            n += 1
                    mm.then_inc(s_dtp, 1)
                for t in range(TILES):
                    if t % QT == 0:
                        pe.wait_ge(s_dtT, max(t // QT + 1, 2))
                    mm = pe.transpose(PS[:, 2 + t // 8, HEADS * (t % 8):HEADS * (t % 8) + HEADS],
                                      dtT[:, 128 * t:128 * t + 128], ident[0:HEADS, 0:HEADS])
                mm.then_inc(s_dtt, 1)
                for k in range(4):
                    conv_in(pe, 0, 0, 0, k, (conv_done, XFREE[k]))
                pe.wait_ge(s_v, 7)
                for b in range(NBATCH):
                    hf, bb = b // 4, b % 4
                    for blk, (c, m) in enumerate(((0, umask), (0, sufmask), (1, umask))):
                        t = 2 * b + c
                        mm = pe.matmul(PS[HEADS * hf:HEADS * hf + HEADS, 2 + bb, 128 * blk:128 * blk + 128],
                                       dt_r[:, HEADS * t:HEADS * t + HEADS], m[:, :], start=True, stop=True)
                mm.then_inc(s_cs, 1)
                for k in range(4, CONVT):
                    conv_in(pe, 0, 0, 0, k, (conv_done, XFREE[k]))
        s0.close()

        sb = make_sb(mamba)
        par_d_sb = sb("par_d_sb", [128, CT], fp32)
        xdt = sb("xdt", [128, 2, 2, HPG, P], fp32)
        M = [shared[:, XWORDS:].rearrange("p (k h i) -> p k h i", k=BLK, h=HPG),
             sb("M", [128, BLK, HPG, 128], fp32)]
        cbm = sb("cbm", [128, BLK * 128], fp32)
        sz = sb("sz", [128, CT, UT], fp32)
        y = sb("y", [128, 2, 2, SEQ], fp32)
        y2 = sb("y2", [128, 2, 2, SEQ], fp32)
        gy = sb("gy", [128, 2, 2, SEQ], fp32)
        g_hi = sb("g_hi", [128, CT, UT], f32r)
        g_lo = sb("g_lo", [128, CT, UT], f32r)

        def groups(eng, body):
            body(0, False)
            with eng.Fori(1, GROUPS - 1) as g:
                body(g, False)
            body(GROUPS - 1, True)

        with nc.Block() as block:
            @block.sync
            def _(sp):
                sp.wait_ge(s_scr, 16 * PARTS * 2)
                sp.wait_ge(s_ms, 9)
                load_lr(sp, 0, 0, 0, 0)
                load_lr(sp, 0, 0, 1, 1)

                def body(g, last):
                    for q in range(PAIRS):
                        u = PAIRS * g + q
                        if q == 0:
                            sp.wait_ge(wz_lo_done, CT * g + CT)
                            sp.dma_start(wraw[:, 0:CT * HID], wo_d[g, :, :]).then_inc(s_raw, 16)
                        for b in range(2):
                            if not (last and q == PAIRS - 1):
                                nq = (q + 1) % PAIRS
                                load_lr(sp, g + 1 if q == PAIRS - 1 else g, nq, b, 2 * u + b + 2)
                            if last:
                                continue
                            if q == 1 and b == 0:
                                sp.wait_ge(wo_lo_done, CT * (g + 1))
                                sp.wait_ge(pd_done, g + 1)
                                sp.dma_start(praw[:, :], par_d[g + 1, :, :]).then_inc(s_par, 16)
                                sp.dma_start(wraw[:, :], wx_d[g + 1, :, :]).then_inc(s_raw, 16)
                            if q == 3 and b == 0:
                                sp.wait_ge(wx_lo_done, CONVT * (g + 2))
                                sp.dma_start(wraw[:, 0:KH * CT * 128], wz_d[g + 1, :, :]).then_inc(s_raw, 16)
                groups(sp, body)
                end = 2 * PAIRS * GROUPS
                sp.wait_ge(t_done, 2 * (end - 2))
                sp.wait_ge(y_done, 2 * (end - 2))
                for i in range(CHUNKS):
                    if i == 2:
                        sp.wait_ge(yt_done, 2 * (end - 1))
                    sp.dma_start(x1[:, quarter(i), :], xd_v[:, quarter(i), :]).then_inc(s_x1in[i], 16)

            @block.tensor
            def _(pe):
                def z_in(g, q, u, ct, free):
                    need(pe, *free)
                    pe.wait_ge(wz_lo_done, CT * g + ct + 1)
                    in_proj(pe, ZBANK[ct], wz_hi, wz_lo, 128 * ct, q, z_done)

                def c_by_b(u, up, b, bt):
                    pe.wait_ge(xs_done, CONVT * u + 2)
                    if b == 0:
                        need(pe, oacc_done, KH * (u - 1))
                    else:
                        pe.wait_ge(cbm_done, bt)
                    t = SEQ * b
                    pe.matmul(PO[:, 0:256], BC[:, up, 0, t:t + 128], BC[:, up, 1, t:t + 256],
                              start=True, stop=True)
                    pe.matmul(PO[:, 256:384], BC[:, up, 0, t + 128:t + 256], BC[:, up, 1, t + 128:t + 256],
                              start=True, stop=True).then_inc(cb_done, 1)

                def decay(u, b, bt, n):
                    if n == 0:
                        pe.wait_ge(l_in[b], 16 * (u + 1))
                        pe.wait_ge(r_in[b], 64 * (u + 1))
                    need(pe, exp_done, BLK * bt + n)
                    blk = BORDER[n]
                    for s in range(2):
                        mm = pe.matmul(PS[:, 2 + s, :], L[:, b, s, 128 * blk:128 * blk + 128],
                                       R[:, b, min(blk, 1), s, :, :], start=True, stop=True)
                    mm.then_inc(d_done, 1)

                def turn_x(u, up, b, bt, c):
                    if c == 0:
                        pe.wait_ge(xs_done, CONVT * u + CONVT)
                    need(pe, xdt_done, 2 * bt + c)
                    t = SEQ * b + 128 * c
                    for ct in range(CT):
                        mm = pe.transpose(PT[:, 128 * ct:128 * ct + 128], xT[up][:, ct, t:t + 128], ident[:, :])
                    mm.then_inc(t_done, 1)

                def y_t(par, bt, half):
                    if half == 0:
                        pe.wait_ge(m_done, BLK * bt + BLK)
                        pe.wait_ge(xdt_done, 2 * bt + 2)
                    need(pe, y_done, 2 * bt + half)
                    for cc in range(2):
                        ct = 2 * half + cc
                        for c in range(2):
                            for s in range(2):
                                h = 2 * ct + s
                                lhs = xdt[:, par, c, h, :]
                                o = PS[P * s:P * s + P, 5, SEQ * cc + 128 * c:SEQ * cc + SEQ]
                                rhs = M[par][:, 0:2, h, :] if c == 0 else M[par][:, 2, h, :]
                                mm = pe.matmul(o, lhs, rhs, start=(c == 0), stop=(c == 1))
                    mm.then_inc(yt_done, 1)

                def project(g, u, m):
                    if m == 0:
                        pe.wait_ge(lo_done, 4 * u + 4)
                        pe.wait_ge(wo_lo_done, CT * g + CT)
                        pe.wait_ge(cbm_done, min(2 * u + 4, 2 * PAIRS * GROUPS) if isinstance(u, int) else 2 * u + 4)
                    else:
                        pe.wait_ge(oacc_done, KH * u + m)
                    project_part(m, 6, range(CT))

                def project_part(m, bank, cts):
                    for ct in cts:
                        for n, (lhs, rhs) in enumerate(((wo_hi, g_hi), (wo_hi, g_lo), (wo_lo, g_hi))):
                            mm = pe.matmul(PS[:, bank, :], lhs[:, ct, 128 * m:128 * m + 128], rhs[:, ct, :],
                                           start=(ct == 0 and n == 0), stop=(ct == CT - 1 and n == 2))
                    if cts[-1] == CT - 1:
                        mm.then_inc(o_done, 1)

                def last_unit(g, gu, q, u, up, zdone):
                    bt = 2 * u
                    y_t(1, bt - 1, 0)
                    z_in(g, q, u, 0, zdone(u - 1, 2))
                    decay(u, 0, bt, 1)
                    turn_x(u, up, 0, bt, 0)
                    z_in(g, q, u, 1, zdone(u - 1, 3))
                    decay(u, 0, bt, 2)
                    y_t(1, bt - 1, 1)
                    decay(u, 1, bt + 1, 0)
                    turn_x(u, up, 0, bt, 1)
                    c_by_b(u, up, 1, bt + 1)
                    decay(u, 1, bt + 1, 1)
                    y_t(0, bt, 0)
                    decay(u, 1, bt + 1, 2)
                    project(gu, u - 1, 0)
                    turn_x(u, up, 1, bt + 1, 0)
                    y_t(0, bt, 1)
                    project(gu, u - 1, 1)
                    z_in(g, q, u, 2, zdone(u, 0))
                    turn_x(u, up, 1, bt + 1, 1)
                    z_in(g, q, u, 3, zdone(u, 1))

                def body(g, last):
                    for q in range(PAIRS):
                        u = PAIRS * g + q
                        first = isinstance(u, int) and u == 0
                        ahead = not (last and q == PAIRS - 1)
                        gv, qv, v = (g + 1 if q == PAIRS - 1 else g), (q + 1) % PAIRS, u + 1
                        gu = g if q else g - 1
                        up = q % 2
                        bt = 2 * u
                        done = lambda w, k: (conv_done, CONVT * w + k + 1)
                        zdone = lambda w, ct: (zs_done, CT * w + ct + 1)
                        if not ahead:
                            last_unit(g, gu, q, u, up, zdone)
                            continue
                        conv_in(pe, gv, qv, v, 0, done(u, 4))
                        if first:
                            conv_in(pe, gv, qv, v, 1, done(u, 5))
                            decay(u, 0, bt, 0)
                            z_in(g, q, u, 0, done(u, 3))
                            decay(u, 0, bt, 1)
                            turn_x(u, up, 0, bt, 0)
                            decay(u, 0, bt, 2)
                        else:
                            y_t(1, bt - 1, 0)
                            decay(u, 0, bt, 1)
                            conv_in(pe, gv, qv, v, 1, zdone(u - 1, 3))
                            decay(u, 0, bt, 2)
                            turn_x(u, up, 0, bt, 0)
                            z_in(g, q, u, 0, zdone(u - 1, 2))
                            y_t(1, bt - 1, 1)
                        conv_in(pe, gv, qv, v, 2, done(v, 0))
                        decay(u, 1, bt + 1, 0)
                        turn_x(u, up, 0, bt, 1)
                        z_in(g, q, u, 1, done(v, 1))
                        c_by_b(u, up, 1, bt + 1)
                        bt = 2 * u + 1
                        conv_in(pe, gv, qv, v, 3, zdone(u, 0))
                        conv_in(pe, gv, qv, v, 4, done(v, 2))
                        decay(u, 1, bt, 1)
                        y_t(0, bt - 1, 0)
                        if not first:
                            project(gu, u - 1, 0)
                        decay(u, 1, bt, 2)
                        conv_in(pe, gv, qv, v, 5, zdone(u, 1))
                        if not first:
                            project(gu, u - 1, 1)
                        turn_x(u, up, 1, bt, 0)
                        y_t(0, bt - 1, 1)
                        z_in(g, q, u, 2, done(v, 3))
                        decay(v, 0, 2 * v, 0)
                        turn_x(u, up, 1, bt, 1)
                        z_in(g, q, u, 3, done(v, 5))
                        c_by_b(v, 1 - up, 0, 2 * v)

                c_by_b(0, 0, 0, 0)
                groups(pe, body)
                end = 2 * PAIRS * GROUPS
                u = PAIRS * GROUPS - 1
                y_t(1, end - 1, 0)
                pe.wait_ge(exp_done, BLK * end)
                pe.wait_ge(oacc_done, KH * (PAIRS * (GROUPS - 1) + 1))
                turn_out(pe, 0)
                y_t(1, end - 1, 1)
                pe.wait_ge(zs_done, CT * PAIRS * GROUPS)
                pe.wait_ge(conv_done, CONVT * PAIRS * GROUPS)
                pe.wait_ge(oacc_done, KH * (PAIRS * (GROUPS - 1) + 2))
                turn_out(pe, 1)
                pe.wait_ge(y_done, 2 * end)
                for i in range(CHUNKS - 1):
                    pe.wait_ge(ssq_link, 8 * (PAIRS * (GROUPS - 1) + i + 1))
                    sum_squares(pe, i)
                for half in range(2):
                    pe.wait_ge(lo_done, 4 * u + 3 + half)
                    for m in range(KH):
                        project_part(m, LASTO[m], range(2 * half, 2 * half + 2))

            @block.scalar
            def _(act):
                def z_silu(u, ct):
                    act.wait_ge(z_done, CT * u + ct + 1)
                    need(act, gy_done, 4 * u - 1 + ct // 2)
                    act.activation(sz[:, ct, :], PS[:, ZBANK[ct], :], ACT.Silu).then_inc(zs_done, 1)

                def decay_exp(par, bt, n):
                    act.wait_ge(d_done, BLK * bt + n + 1)
                    need(act, yt_done, 2 * bt - 2)
                    act.activation(M[par][:, BORDER[n], :, :].rearrange("p h (s i) -> p s h i", s=2),
                                   PD.rearrange("p s (h i) -> p s h i", i=64), ACT.Exp).then_inc(exp_done, 1)

                def square(bt, half):
                    n = 2 * bt + half
                    act.wait_ge(y_done, n + 1)
                    need(act, ssq_link, 2 * n - 2)
                    act.activation(y2[:, half, :, :], y[:, half, :, :], ACT.Square).then_inc(sq_done, 1)

                def gated_hi(u, b, bt, half):
                    n = 2 * bt + half
                    act.wait_ge(gy_done, n + 1)
                    need(act, o_done, KH * u)
                    act.activation(g_hi[:, 2 * half:2 * half + 2, SEQ * b:SEQ * b + SEQ], gy[:, half, :, :],
                                   ACT.Copy).then_inc(hi_done, 1)

                def split_o(g, ct):
                    act.wait_ge(wo_scaled, CT * g + ct + 1)
                    need(act, o_done, KH * PAIRS * g)
                    act.activation(wo_hi[:, ct, :], wraw_o[:, ct, :], ACT.Copy).then_inc(wo_hi_done, 1)

                def last_unit(u):
                    bt = 2 * u
                    decay_exp(0, bt, 0)
                    decay_exp(0, bt, 1)
                    gated_hi(u - 1, 0, bt - 2, 1)
                    square(bt - 2, 1)
                    decay_exp(0, bt, 2)
                    gated_hi(u - 1, 1, bt - 1, 0)
                    decay_exp(1, bt + 1, 0)
                    gated_hi(u - 1, 1, bt - 1, 1)
                    decay_exp(1, bt + 1, 1)
                    square(bt - 1, 0)
                    square(bt - 1, 1)
                    decay_exp(1, bt + 1, 2)
                    z_silu(u, 0)
                    z_silu(u, 1)
                    square(bt, 0)
                    gated_hi(u, 0, bt, 0)
                    z_silu(u, 2)
                    z_silu(u, 3)

                def body(g, last):
                    for q in range(PAIRS):
                        u = PAIRS * g + q
                        first = isinstance(u, int) and u == 0
                        ahead = not (last and q == PAIRS - 1)
                        gv, v, vp = (g + 1 if q == PAIRS - 1 else g), u + 1, (q + 1) % 2
                        bt = 2 * u
                        if not ahead:
                            last_unit(u)
                            continue
                        if q == 0 and not first:
                            for ct in (0, 1):
                                split_z_hi(act, g, ct)
                        if first:
                            tap3(act, gv, v, 0)
                        decay_exp(0, bt, 0)
                        if not first:
                            tap3(act, gv, v, 0)
                        if q == 0 and not first:
                            for ct in (2, 3):
                                split_z_hi(act, g, ct)
                        decay_exp(0, bt, 1)
                        if not first:
                            gated_hi(u - 1, 0, bt - 2, 1)
                        tap3(act, gv, v, 1)
                        if not first:
                            square(bt - 2, 1)
                        if q == 1:
                            for ct in (2, 3):
                                split_o(g, ct)
                        decay_exp(0, bt, 2)
                        z_silu(u, 0)
                        tap3(act, gv, v, 2)
                        conv_silu(act, vp, v, 0)
                        if not first:
                            gated_hi(u - 1, 1, bt - 1, 0)
                        conv_silu(act, vp, v, 1)
                        z_silu(u, 1)
                        bt = 2 * u + 1
                        decay_exp(1, bt, 0)
                        if not first:
                            gated_hi(u - 1, 1, bt - 2, 1)
                            square(bt - 2, 0)
                        tap3(act, gv, v, 3)
                        decay_exp(1, bt, 1)
                        tap3(act, gv, v, 4)
                        if not first:
                            square(bt - 2, 1)
                        decay_exp(1, bt, 2)
                        if q == 2 and not last:
                            for k in range(3):
                                split_x_hi(act, g + 1, k)
                        conv_silu(act, vp, v, 2)
                        tap3(act, gv, v, 5)
                        conv_silu(act, vp, v, 3)
                        square(bt - 1, 0)
                        conv_silu(act, vp, v, 4)
                        gated_hi(u, 0, bt - 1, 0)
                        if q == 0:
                            for ct in (0, 1):
                                split_o(g, ct)
                        z_silu(u, 2)
                        conv_silu(act, vp, v, 5)
                        if q == 2 and not last:
                            for k in range(3, CONVT):
                                split_x_hi(act, g + 1, k)
                        z_silu(u, 3)
                groups(act, body)
                end = 2 * PAIRS * GROUPS
                gated_hi(PAIRS * GROUPS - 1, 0, end - 2, 1)
                square(end - 2, 1)
                act.activation(std[1][:, 0:1], epsc[:, 0:1], ACT.Sqrt)
                gated_hi(PAIRS * GROUPS - 1, 1, end - 1, 0)
                norms(act, 0, 0, TILES - QT)
                gated_hi(PAIRS * GROUPS - 1, 1, end - 1, 1)
                square(end - 1, 0)
                row_std(act, 0)
                row_std(act, 1)
                square(end - 1, 1)

            @block.vector
            def _(dve):
                def mask_cb(bt):
                    dve.wait_ge(cb_done, bt + 1)
                    need(dve, m_done, BLK * bt)
                    dve.tensor_tensor(cbm[:, :], PO[:, 0:BLK * 128], mask[:, :], ALU.mult).then_inc(cbm_done, 1)

                def decay_cb(par, bt, n):
                    if n == 0:
                        dve.wait_ge(cbm_done, bt + 1)
                    dve.wait_ge(exp_done, BLK * bt + n + 1)
                    blk = BORDER[n]
                    dve.scalar_tensor_tensor(M[par][:, blk, :, :], M[par][:, blk, :, :], 1.0,
                                             cbm[:, 128 * blk:128 * blk + 128].unsqueeze(1).to_broadcast([128, HPG, 128]),
                                             ALU.min, ALU.mult).then_inc(m_done, 1)

                def add_skip(g, up, b, bt, half):
                    n = 2 * bt + half
                    dve.wait_ge(yt_done, n + 1)
                    dve.wait_ge(pd_done, g + 1)
                    need(dve, sq_done, n - 1)
                    need(dve, gy_done, n - 1)
                    for cc in range(2):
                        ct = 2 * half + cc
                        ins = dve.scalar_tensor_tensor(y[:, half, cc, :], xT[up][:, ct, SEQ * b:SEQ * b + SEQ],
                                                       par_d_sb[:, ct:ct + 1], PY[:, cc, :], ALU.mult, ALU.add)
                    ins.then_inc(y_done, 1)

                def scale_x(g, q, par, b, bt, c):
                    dve.wait_ge(t_done, 2 * bt + c + 1)
                    need(dve, yt_done, 2 * bt - 2)
                    t = 4 * q + 2 * b + c
                    dve.tensor_tensor(xdt[:, par, c, :, :], PT.rearrange("p (h e) -> p h e", h=HPG),
                                      dt_sb[:, t, g, :].unsqueeze(2).to_broadcast([128, HPG, P]),
                                      ALU.mult).then_inc(xdt_done, 1)

                def add_proj(q, u, m, bank=6):
                    dve.wait_ge(o_done, KH * u + m + 1)
                    o = outT[:, m, UT * q:UT * q + UT]
                    dve.tensor_tensor(o, PS[:, bank, :], o, ALU.add).then_inc(oacc_done, 1)

                def skip_params(g):
                    dve.wait_ge(s_par, 16 * g + 16)
                    need(dve, y_done, 4 * PAIRS * g)
                    dve.tensor_copy(par_d_sb[:, :], praw[:, PA:PA + CT]).then_inc(pd_done, 1)

                def body(g, last):
                    for q in range(PAIRS):
                        u = PAIRS * g + q
                        first = isinstance(u, int) and u == 0
                        ahead = not (last and q == PAIRS - 1)
                        gv, v = (g + 1 if q == PAIRS - 1 else g), u + 1
                        up = q % 2
                        gy_, upy = (g if q else g - 1), 1 - up
                        bt = 2 * u
                        if q == PAIRS - 1 and ahead:
                            conv_params(dve, g + 1)
                        if not first:
                            scale_x(gy_, (q - 1) % PAIRS, 1, 1, bt - 1, 1)
                        mask_cb(bt)
                        if first:
                            for s in range(1, TAPS):
                                conv(dve, gv, v, 0, s)
                        decay_cb(0, bt, 0)
                        if ahead and not first:
                            conv(dve, gv, v, 0, 1)
                        if not first:
                            add_skip(gy_, upy, 1, bt - 1, 0)
                        if ahead and not first:
                            conv(dve, gv, v, 0, 2)
                        decay_cb(0, bt, 1)
                        if ahead and not first:
                            conv(dve, gv, v, 0, 3)
                        if ahead:
                            conv(dve, gv, v, 1, 1)
                        scale_x(g, q, 0, 0, bt, 0)
                        if ahead:
                            conv(dve, gv, v, 1, 2)
                            conv(dve, gv, v, 1, 3)
                        if not first:
                            add_skip(gy_, upy, 1, bt - 1, 1)
                        if ahead:
                            conv(dve, gv, v, 2, 1)
                        scale_x(g, q, 0, 0, bt, 1)
                        if ahead:
                            conv(dve, gv, v, 2, 2)
                            conv(dve, gv, v, 2, 3)
                        decay_cb(0, bt, 2)
                        bt = 2 * u + 1
                        if q == 0:
                            skip_params(g)
                        mask_cb(bt)
                        decay_cb(1, bt, 0)
                        if ahead:
                            conv(dve, gv, v, 3, 1)
                        decay_cb(1, bt, 1)
                        if ahead:
                            conv(dve, gv, v, 3, 2)
                        add_skip(g, up, 0, bt - 1, 0)
                        if ahead:
                            conv(dve, gv, v, 3, 3)
                        if not first:
                            add_proj((q - 1) % PAIRS, u - 1, 0)
                        if ahead:
                            conv(dve, gv, v, 4, 1)
                            conv(dve, gv, v, 4, 2)
                        if ahead:
                            conv(dve, gv, v, 4, 3)
                            conv(dve, gv, v, 5, 1)
                        if not first:
                            add_proj((q - 1) % PAIRS, u - 1, 1)
                        if ahead:
                            conv(dve, gv, v, 5, 2)
                        scale_x(g, q, 1, 1, bt, 0)
                        if ahead:
                            conv(dve, gv, v, 5, 3)
                        add_skip(g, up, 0, bt - 1, 1)
                        decay_cb(1, bt, 2)
                groups(dve, body)
                end = 2 * PAIRS * GROUPS
                scale_x(GROUPS - 1, PAIRS - 1, 1, 1, end - 1, 1)
                add_skip(GROUPS - 1, 1, 1, end - 1, 0)
                add_skip(GROUPS - 1, 1, 1, end - 1, 1)
                dve.wait_ge(xs_done, CONVT * PAIRS * GROUPS)
                stats(dve, 0)
                stats(dve, 1)
                inverse_norms(dve, 0, 0, TILES - QT)
                variance(dve, 0)
                variance(dve, 1)
                scales(dve, 0)
                residual(dve, 0)
                scales(dve, 1)
                add_proj(PAIRS - 1, PAIRS * GROUPS - 1, 0, LASTO[0])
                add_proj(PAIRS - 1, PAIRS * GROUPS - 1, 1, LASTO[1])
                residual(dve, 1)

            @block.gpsimd
            def _(pool):
                def gate(u, b, bt, half):
                    n = 2 * bt + half
                    pool.wait_ge(y_done, n + 1)
                    pool.wait_ge(zs_done, CT * u + 2 * half + 2)
                    need(pool, hi_done, n - 1)
                    need(pool, lo_done, n - 1)
                    pool.tensor_tensor(gy[:, half, :, :], y[:, half, :, :],
                                       sz[:, 2 * half:2 * half + 2, SEQ * b:SEQ * b + SEQ], ALU.mult).then_inc(gy_done, 1)

                def gated_lo(b, bt, half):
                    cts, ts = slice(2 * half, 2 * half + 2), slice(SEQ * b, SEQ * b + SEQ)
                    pool.wait_ge(hi_done, 2 * bt + half + 1)
                    pool.tensor_tensor(g_lo[:, cts, ts], gy[:, half, :, :], g_hi[:, cts, ts].bitcast(fp32),
                                       ALU.subtract).then_inc(lo_done, 1)

                def add_squares(q, b, bt, half):
                    n = 2 * bt + half
                    pool.wait_ge(sq_done, n + 1)
                    tok = ssq[:, UT * q + SEQ * b:UT * q + SEQ * b + SEQ]
                    for cc in range(2):
                        need(pool, ssq_link, 2 * n + cc)
                        pool.tensor_tensor(tok, tok, y2[:, half, cc, :], ALU.add).then_inc(ssq_link, 1)

                def scale_o(g):
                    pool.wait_ge(s_raw, 48 * g + 48)
                    pool.wait_ge(s_par, 16 * g + 16)
                    for ct in range(CT):
                        pool.tensor_tensor(wraw_o[:, ct, :], wraw_o[:, ct, :],
                                           praw[:, PA + CT + ct:PA + CT + ct + 1].to_broadcast([128, HID]),
                                           ALU.mult).then_inc(wo_scaled, 1)

                def split_o(g, cts):
                    for ct in cts:
                        pool.wait_ge(wo_hi_done, CT * g + ct + 1)
                        pool.tensor_tensor(wo_lo[:, ct, :], wraw_o[:, ct, :], wo_hi[:, ct, :].bitcast(fp32),
                                           ALU.subtract).then_inc(wo_lo_done, 1)

                def body(g, last):
                    for q in range(PAIRS):
                        u = PAIRS * g + q
                        first = isinstance(u, int) and u == 0
                        bt, pq = 2 * u, (q - 1) % PAIRS
                        if q == 0 and not first:
                            for ct in range(CT):
                                split_z_lo(pool, g, ct)
                        if not first:
                            gated_lo(0, bt - 2, 1)
                        if not first:
                            gate(u - 1, 1, bt - 1, 0)
                            add_squares(pq, 0, bt - 2, 1)
                            gate(u - 1, 1, bt - 1, 1)
                            gated_lo(1, bt - 1, 0)
                        if q == 1:
                            split_o(g, (2, 3))
                        if not first:
                            gated_lo(1, bt - 1, 1)
                            add_squares(pq, 1, bt - 1, 0)
                            add_squares(pq, 1, bt - 1, 1)
                        if q == 2 and not last:
                            for k in range(3):
                                split_x_lo(pool, g + 1, k)
                        if q == 0:
                            scale_o(g)
                        gate(u, 0, bt, 0)
                        gated_lo(0, bt, 0)
                        if q == 0:
                            split_o(g, (0, 1))
                        add_squares(q, 0, bt, 0)
                        if q == 2 and not last:
                            for k in range(3, CONVT):
                                split_x_lo(pool, g + 1, k)
                        gate(u, 0, bt, 1)
                groups(pool, body)
                u, q = PAIRS * GROUPS - 1, PAIRS - 1
                gated_lo(0, 2 * u, 1)
                gate(u, 1, 2 * u + 1, 0)
                gated_lo(1, 2 * u + 1, 0)
                gate(u, 1, 2 * u + 1, 1)
                gated_lo(1, 2 * u + 1, 1)
                add_squares(q, 0, 2 * u, 1)
                add_squares(q, 1, 2 * u + 1, 0)
                add_squares(q, 1, 2 * u + 1, 1)

        mamba.close()

        sb = make_sb(outer)
        AHEAD = 3
        END = CHUNKS * FT
        EARLY = CHUNKS * AHEAD
        PSTEPS = [(c, f) for c in range(CHUNKS) for f in range(AHEAD)]
        BUF = (2, 3, 0)
        xo = sb("xo", [128, TILES, HID], fp32)
        wf_raw = sb("wf_raw", [128, 2, 768], fp32)
        wf_hi = sb("wf_hi", [128, AHEAD + 1, 768], f32r)
        wf_lo = sb("wf_lo", [128, AHEAD + 1, 768], f32r)
        combT = sb("combT", [CROWS, TOK], bf16)
        f_hot = sb("f_hot", [CROWS, FT * 128], bf16)
        NLG = ROUTES + 1
        wg_raw = sb("wg_raw", [128, KH, NLG], fp32)
        wg_hi = sb("wg_hi", [128, KH, NLG], f32r)
        wg_lo = sb("wg_lo", [128, KH, NLG], f32r)
        tie = sb("tie", [128, E * E], fp32)
        ident_b = sb("ident_b", [128, 128], bf16)
        lgT = sb("lgT", [NLG, TOK], fp32)
        lg = sb("lg", [128, TILES, NLG], fp32)
        mx = sb("mx", [128, TILES], fp32)
        pr = sb("pr", [128, TILES, E], fp32)
        sm = sb("sm", [128, TILES], fp32)
        gts = shared[:, TILES * HID:TILES * (HID + E * E)].rearrange("p (t e o) -> p t e o", t=TILES, e=E)
        eqs = sb("eqs", [128, TILES, E, E], fp32)
        rank = sb("rank", [128, TILES, E], fp32)
        comb = sb("comb", [128, TILES, ROUTES], fp32)
        comb_r = sb("comb_r", [128, TILES, ROUTES], fp32)
        cparts = sb("cparts", [128, TILES, PARTS, ROUTES], bf16)
        sl = sb("sl", [128, 2, UT], fp32)
        hm = sb("hm", [128, EARLY, UT], fp32)
        hot_raw = hm[0:CROWS, 7:EARLY, :].rearrange("p s t -> p (s t)")[:, 0:FT * 128]
        hc = sb("hc", [128, 2, UT], fp32)
        h_hi = sb("h_hi", [128, CHUNKS, UT], f32r)
        h_lo = sb("h_lo", [128, CHUNKS, UT], f32r)

        s_in = sem("s2_const_in")
        s_f = [sem(f"moe_weights_in{i}") for i in range(2)]
        s_ag2, s_sd2, s_f2, s_n = sem("s2_stats2"), sem("s2_row_std2"), sem("s2_scales2"), sem("s2_normed")
        s_t2, s_h2, s_l2 = sem("s2_xT"), sem("s2_hi"), sem("s2_lo")
        s_gh, s_gl, s_lg, s_lc, s_lt = sem("s2_gate_w_hi"), sem("s2_gate_w_lo"), sem("s2_logits"), sem("s2_logits_copied"), sem("s2_logits_turned")
        s_q, s_e, s_cp = sem("s2_shifted_logits"), sem("s2_exp"), sem("s2_route_parts")
        s_ct, s_cc = sem("s2_combT"), sem("s2_combT_copied")
        f1_done, f2_done, g_done, p_done = sem("fc1_done"), sem("fc2_done"), sem("route_weight_done"), sem("moe_proj_done")
        sl_done, hhi_done, wfh_done = sem("fc1_silu_done"), sem("h_hi_done"), sem("moe_w_hi_done")
        hm_done, hc_done, fa_done = sem("h_done"), sem("h_scaled"), sem("moe_proj_added")
        hlo_done, wfl_done = sem("h_lo_done"), sem("moe_w_lo_done")
        s_tr4, s_ag4, s_sd4, s_f4 = sem("s4_turned"), sem("s4_stats"), sem("s4_row_std"), sem("s4_scales")
        s_sc4, s_o4, s_out = sem("s4_scaled"), sem("s4_sum"), sem("s4_out")
        s_o4_last = sem("s4_last_sum")
        out_v = out_d.rearrange("(t p) c -> p t c", p=128)
        BANK2 = (6, 0, 2, 0)
        LBANK = (2, 3, 0, 1)
        BANK4 = (4, 6, 0, 2)

        def pair_loop(eng, body):
            body(AHEAD, 1, 1, BUF[AHEAD - 1], False)
            body(AHEAD + 1, 2, 0, 1, False)
            with eng.Fori(1, (FT - AHEAD) // 2 - 1) as i:
                body(2 * i + AHEAD, i + 1, 1, 0, False)
                body(2 * i + AHEAD + 1, i + 2, 0, 1, False)
            body(FT - 2, FT // 2 - 1, 1, 0, True)
            body(FT - 1, FT // 2, 0, 1, True)

        SUMB = (2, 6, 4, 2)
        ADDS = CHUNKS - EARLY

        with nc.Block() as block:
            @block.sync
            def _(sp):
                for f in range(2):
                    sp.dma_start(wf_raw[:, f, :], wf_d[f, :, :]).then_inc(s_f[f], 16)
                for dst, src in ((wg_raw[:, :, :], wg_d.rearrange("p (k n) -> p k n", k=KH)),
                                 (tie[:, :], tie_d), (hot_raw, f_hot_d)):
                    sp.dma_start(dst, src).then_inc(s_in, 16)

                def reload(f, par):
                    sp.wait_ge(wfl_done, f + 1)
                    sp.dma_start(wf_raw[:, par, :], wf_d[f + 2, :, :]).then_inc(s_f[par], 16)

                for f in range(AHEAD):
                    reload(f, f % 2)

                def body(f, filled, par, before, last):
                    if not last:
                        reload(f, par)
                pair_loop(sp, body)
                for i in range(CHUNKS):
                    if i < CHUNKS - 1:
                        sp.wait_ge(s_o4, i + 1)
                    else:
                        sp.wait_ge(s_sc4, TILES)
                    sp.dma_start(out_v[:, quarter(i), :], xo[:, quarter(i), :]).then_inc(s_out, 16)
                sp.wait_ge(s_out, 16 * CHUNKS)

            @block.tensor
            def _(pe):
                def turn_normed(i):
                    pe.wait_ge(s_n, QT * i + QT)
                    if i == 0:
                        pe.wait_ge(s_rn, 2)
                    elif i == 3:
                        pe.wait_ge(s_l2, KH * 2)
                    else:
                        pe.wait_ge(s_x1, QT * (2 if i == 1 else 4))
                    for k in range(KH):
                        for t in range(QT):
                            mm = pe.transpose(PS[:, BANK2[i] + k, 128 * t:128 * t + 128],
                                              xo[:, QT * i + t, 128 * k:128 * k + 128], ident[:, :])
                        mm.then_inc(s_t2, 1)

                def hidden(j, par, c):
                    need(pe, hm_done, j - 1)
                    if isinstance(j, int) and j == 0:
                        pe.wait_ge(s_x1, QT * 3)
                    for which in range(2):
                        n = 0
                        for whl, xhl in ((wf_hi, xnT_hi), (wf_hi, xnT_lo), (wf_lo, xnT_hi)):
                            for k in range(KH):
                                w0 = 256 * k + 128 * which
                                mm = pe.matmul(PS[:, 4 + 2 * which + j_parity(j, c), :], whl[:, par, w0:w0 + 128],
                                               xhl[:, k, UT * c:UT * c + UT],
                                               start=(n == 0), stop=(n == 3 * KH - 1))
                                n += 1
                        mm.then_inc(f2_done if which else f1_done, 1)

                def j_parity(j, c):
                    return j % 2 if isinstance(j, int) else c % 2

                def early(p):
                    c, f = PSTEPS[p]
                    pe.wait_ge(wfl_done, f + 1)
                    pe.wait_ge(s_l2, KH * c + KH)
                    hidden(p, BUF[f], c)

                def logits(i):
                    pe.wait_ge(s_gl, 1)
                    pe.wait_ge(s_l2, KH * 3 if i < 2 else KH * CHUNKS)
                    n = 0
                    for lhs, rhs in ((wg_hi, xnT_hi), (wg_lo, xnT_hi), (wg_hi, xnT_lo)):
                        for k in range(KH):
                            mm = pe.matmul(PS[0:NLG, LBANK[i], :], lhs[:, k, :], rhs[:, k, UT * i:UT * i + UT],
                                           start=(n == 0), stop=(n == 3 * KH - 1))
                            n += 1
                    mm.then_inc(s_lg, 1)

                def route_weight(f, c, bank):
                    hot = f_hot[:, 128 * f:128 * f + 128] if isinstance(f, int) else f_hot[:, bass.ds(128 * f, 128)]
                    pe.matmul(PS[:, bank, :], hot, combT[:, UT * c:UT * c + UT], start=True, stop=True).then_inc(g_done, 1)

                def project(j, par, c):
                    pe.wait_ge(hlo_done, j + 1)
                    need(pe, fa_done, j + ADDS)
                    shares(2, par, c, True, True)

                def shares(bank, par, slot, first, last):
                    for m in range(KH):
                        w0 = 512 + 128 * m
                        for n, (whl, hhl) in enumerate(((wf_hi, h_hi), (wf_hi, h_lo), (wf_lo, h_hi))):
                            mm = pe.matmul(PS[:, bank + m, :], whl[:, par, w0:w0 + 128], hhl[:, slot, :],
                                           start=(first and n == 0), stop=(last and n == 2))
                    mm.then_inc(p_done, 1)

                def project_early(p):
                    c, f = PSTEPS[p]
                    pe.wait_ge(hlo_done, p + 1)
                    if c == 1 and f == 0:
                        pe.wait_ge(hm_done, EARLY)
                    if c == 3 and f == 0:
                        pe.wait_ge(fa_done, 1)
                    shares(SUMB[c], BUF[f], p % CHUNKS, f == 0, f == AHEAD - 1)

                def turn_sum(i):
                    pe.wait_ge(fa_done, END + ADDS - CHUNKS + i + 1)
                    if i < 2:
                        pe.wait_ge(hm_done, END)
                    else:
                        pe.wait_ge(hc_done, END)
                    for t in range(QT):
                        for k in range(KH):
                            mm = pe.transpose(rows_ps(BANK4[i], t)[:, 128 * k:128 * k + 128],
                                              outT[:, k, UT * i + 128 * t:UT * i + 128 * t + 128], ident[:, :])
                    mm.then_inc(s_tr4, 1)

                sum_squares(pe, CHUNKS - 1)
                turn_out(pe, 2)
                pe.wait_ge(s_x1, QT)
                turn_out(pe, 3)
                turn_normed(0)
                early(0)
                turn_normed(1)
                early(1)
                early(2)
                turn_normed(2)
                early(3)
                turn_normed(3)
                logits(0)
                logits(1)
                early(4)
                logits(2)
                logits(3)
                early(5)
                pe.wait_ge(s_lc, CHUNKS)
                for t in range(TILES):
                    mm = pe.transpose(PS[:, 0, NLG * t:NLG * t + NLG], lgT[:, 128 * t:128 * t + 128], ident[0:NLG, 0:NLG])
                mm.then_inc(s_lt, 1)
                for p in range(6, EARLY - 1):
                    early(p)
                pe.wait_ge(s_cp, PARTS)
                cps = PS[0:CROWS, 2:4, :].bitcast(bf16).rearrange("p b t -> p (b t)")
                for t in range(TILES):
                    mm = pe.transpose(cps[:, 128 * t:128 * t + 128],
                                      cparts[:, t, :, :].rearrange("p a r -> p (a r)"), ident_b[:, :])
                mm.then_inc(s_ct, 1)
                pe.wait_ge(s_cc, 1)
                for p, (c, f) in enumerate(PSTEPS):
                    need(pe, hc_done, p - 1)
                    route_weight(f, c, p % 2)
                    if p == 1:
                        early(EARLY - 1)
                    if p >= 2:
                        project_early(p - 2)
                pe.wait_ge(fa_done, CHUNKS - 1)

                def body(f, filled, par, before, last):
                    pe.wait_ge(wfl_done, f + 1)
                    for c in range(CHUNKS):
                        j = CHUNKS * f + c
                        pe.wait_ge(hc_done, j - 1)
                        hidden(j, par, c)
                        route_weight(f, c, c % 2)
                        if isinstance(j, int) and j - 2 < EARLY:
                            project_early(j - 2)
                        else:
                            project(j - 2, par if c >= 2 else before, (c - 2) % CHUNKS)
                pair_loop(pe, body)
                turn_sum(0)
                project(END - 2, 0, CHUNKS - 2)
                turn_sum(1)
                project(END - 1, 0, CHUNKS - 1)
                turn_sum(2)
                turn_sum(3)

            @block.scalar
            def _(act):
                def split(f, filled, par, buf):
                    act.wait_ge(s_f[par], 16 * (filled + 1))
                    if not (isinstance(f, int) and f <= AHEAD):
                        act.wait_ge(p_done, CHUNKS * (f - 1))
                    act.activation(wf_hi[:, buf, :], wf_raw[:, par, :], ACT.Copy).then_inc(wfh_done, 1)

                def row_std2(i):
                    act.wait_ge(s_ag2, 2 * i + 2)
                    act.activation(std[1][:, quarter(i)], mv[1][:, quarter(i), 1], ACT.Sqrt, bias=epsc[:, 0:1]).then_inc(s_sd2, 1)

                def normed(i):
                    act.wait_ge(s_f2, i + 1)
                    for t in range(QT):
                        n = QT * i + t
                        act.activation(xo[:, n, :], x1[:, n, :], ACT.Identity, scale=rstd[1][:, n:n + 1],
                                       bias=shf[1][:, n:n + 1]).then_inc(s_n, 1)

                def high_x(i):
                    for k in range(KH):
                        act.wait_ge(s_t2, KH * i + k + 1)
                        act.activation(xnT_hi[:, k, UT * i:UT * i + UT], PS[:, BANK2[i] + k, :], ACT.Copy).then_inc(s_h2, 1)

                def silu(j, par):
                    act.wait_ge(f1_done, j + 1)
                    need(act, hm_done, j - 1)
                    act.activation(sl[:, par, :], PS[:, 4 + par, :], ACT.Silu).then_inc(sl_done, 1)

                def copy_logits(i):
                    act.wait_ge(s_lg, i + 1)
                    act.activation(lgT[:, UT * i:UT * i + UT], PS[0:NLG, LBANK[i], :], ACT.Copy).then_inc(s_lc, 1)

                def high(j, c):
                    act.wait_ge(hc_done, j + 1)
                    need(act, p_done, j - 3)
                    act.activation(h_hi[:, c, :], hc[:, c % 2, :], ACT.Copy).then_inc(hhi_done, 1)

                row_std2(0)
                norms(act, 1, TILES - QT, TILES)
                normed(0)
                row_std(act, 2)
                split(0, 0, 0, BUF[0])
                high_x(0)
                split(1, 0, 1, BUF[1])
                row_std2(1)
                normed(1)
                row_std(act, 3)
                split(2, 1, 0, BUF[2])
                silu(0, 0)
                high_x(1)
                act.wait_ge(s_in, 16 * 3)
                act.activation(wg_hi[:, :, :], wg_raw[:, :, :], ACT.Copy).then_inc(s_gh, 1)
                silu(1, 1)
                row_std2(2)
                row_std2(3)
                normed(2)
                normed(3)
                silu(2, 0)
                high_x(2)
                silu(3, 1)
                high_x(3)
                split(AHEAD, 1, 1, 1)
                for i in range(CHUNKS):
                    copy_logits(i)
                for p in range(4, 7):
                    silu(p, p % 2)
                act.wait_ge(s_q, 1)
                act.activation(pr[:, :, :], pr[:, :, :], ACT.Exp).then_inc(s_e, 1)
                act.activation(sm[:, :], lg[:, :, E], ACT.Exp, scale=-1.0).then_inc(s_e, 1)
                for p in range(7, EARLY - 1):
                    silu(p, p % 2)
                for p in range(EARLY):
                    high(p, p % CHUNKS)
                    if p == 1:
                        silu(EARLY - 1, (EARLY - 1) % 2)

                def body(f, filled, par, before, last):
                    for c in range(CHUNKS):
                        j = CHUNKS * f + c
                        silu(j, c % 2)
                        high(j, c)
                        if c == 2 and not (isinstance(f, int) and f == FT - 1):
                            split(f + 1, filled + par, 1 - par, 1 - par)
                pair_loop(act, body)
                for i in range(CHUNKS):
                    act.wait_ge(s_ag4, 2 * i + 2)
                    act.activation(std[0][:, quarter(i)], mv[0][:, quarter(i), 1], ACT.Sqrt, bias=epsc[:, 0:1]).then_inc(s_sd4, 1)
                    act.wait_ge(s_f4, i + 1)
                    for t in range(QT):
                        n = QT * i + t
                        if i == CHUNKS - 1:
                            act.wait_ge(s_o4_last, t + 1)
                            act.activation(xo[:, n, :], xo[:, n, :], ACT.Identity,
                                           bias=shf[2][:, n:n + 1]).then_inc(s_sc4, 1)
                            continue
                        act.activation(xo[:, n, :], rows_ps(BANK4[i], t), ACT.Identity, scale=rstd[0][:, n:n + 1],
                                       bias=shf[2][:, n:n + 1]).then_inc(s_sc4, 1)

            @block.vector
            def _(dve):
                def stats2(i):
                    dve.wait_ge(s_x1, QT * i + QT)
                    for t in range(QT):
                        ins = dve.bn_stats(st[1][:, QT * i + t, :], x1[:, QT * i + t, :])
                    ins.then_inc(s_ag2, 1)
                    dve.wait_ge(s_ag2, 2 * i + 1)
                    for t in range(QT):
                        ins = dve.bn_aggr(mv[1][:, QT * i + t, :], st[1][:, QT * i + t, :])
                    ins.then_inc(s_ag2, 1)

                def scales2(i):
                    q = quarter(i)
                    dve.wait_ge(s_sd2, i + 1)
                    linked(dve, dve.reciprocal(rstd[1][:, q], std[1][:, q]))
                    dve.scalar_tensor_tensor(shf[1][:, q], mv[1][:, q, 0], -1.0, rstd[1][:, q], ALU.mult, ALU.mult).then_inc(s_f2, 1)

                def low_x(i):
                    for k in range(KH):
                        dve.wait_ge(s_h2, KH * i + k + 1)
                        dve.tensor_tensor(xnT_lo[:, k, UT * i:UT * i + UT], PS[:, BANK2[i] + k, :],
                                          xnT_hi[:, k, UT * i:UT * i + UT].bitcast(fp32), ALU.subtract).then_inc(s_l2, 1)

                def gated(j, par, slot):
                    dve.wait_ge(sl_done, j + 1)
                    dve.wait_ge(f2_done, j + 1)
                    dve.tensor_tensor(hm[:, slot, :], PS[:, 6 + par, :], sl[:, par, :], ALU.mult).then_inc(hm_done, 1)

                def early(p):
                    gated(p, p % 2, p)

                def routed(j, par, slot):
                    dve.wait_ge(g_done, j + 1)
                    need(dve, hlo_done, j - 1)
                    dve.tensor_tensor(hc[:, par, :], PS[:, par, :], hm[:, slot, :], ALU.mult).then_inc(hc_done, 1)

                def add_up(j, c):
                    dve.wait_ge(p_done, j + 1)
                    o = outT[:, :, UT * c:UT * c + UT]
                    dve.tensor_tensor(o, PS[:, 2:2 + KH, :], o, ALU.add).then_inc(fa_done, 1)

                def first_sum(c):
                    dve.wait_ge(p_done, AHEAD * (c + 1))
                    dve.tensor_copy(outT[:, :, UT * c:UT * c + UT], PS[:, SUMB[c]:SUMB[c] + KH, :]).then_inc(fa_done, 1)

                dve.tensor_copy(ident_b[:, :], ident[:, :])
                stats2(0)
                scales2(0)
                stats(dve, 2)
                variance(dve, 2)
                scales(dve, 2)
                residual(dve, 2)
                low_x(0)
                stats2(1)
                scales2(1)
                inverse_norms(dve, 1, TILES - QT, TILES)
                stats(dve, 3)
                variance(dve, 3)
                scales(dve, 3)
                residual(dve, 3)
                early(0)
                stats2(2)
                stats2(3)
                scales2(2)
                low_x(1)
                scales2(3)
                early(1)
                dve.wait_ge(s_gh, 1)
                dve.tensor_tensor(wg_lo[:, :, :], wg_raw[:, :, :], wg_hi[:, :, :].bitcast(fp32), ALU.subtract).then_inc(s_gl, 1)
                early(2)
                low_x(2)
                low_x(3)
                early(3)
                dve.tensor_copy(f_hot[:, :], hot_raw)
                early(4)
                dve.wait_ge(s_lt, 1)
                linked(dve, dve.tensor_copy(lg[:, :, :], PS[:, 0, 0:TILES * NLG].rearrange("p (t r) -> p t r", t=TILES)))
                linked(dve, dve.tensor_reduce(mx[:, :], lg[:, :, 0:E], AX.X, ALU.max))
                dve.tensor_tensor(pr[:, :, :], lg[:, :, 0:E], mx[:, :].unsqueeze(2).to_broadcast([128, TILES, E]),
                                  ALU.subtract).then_inc(s_q, 1)
                early(5)
                early(6)
                dve.wait_ge(s_e, 1)
                dve.tensor_reduce(mx[:, :], pr[:, :, :], AX.X, ALU.add)
                dve.wait_ge(s_e, 2)
                linked(dve, dve.tensor_scalar(sm[:, :], sm[:, :], 1.0, None, ALU.add))
                dve.reciprocal(mx[:, :], mx[:, :])
                linked(dve, dve.reciprocal(comb[:, :, E], sm[:, :]))
                linked(dve, dve.tensor_tensor(pr[:, :, :], pr[:, :, :], mx[:, :].unsqueeze(2).to_broadcast([128, TILES, E]),
                                         ALU.mult))
                full = [128, TILES, E, E]
                other = pr[:, :, :].unsqueeze(2).to_broadcast(full)
                own = pr[:, :, :].unsqueeze(3).to_broadcast(full)
                first = tie[:, :].rearrange("p (e o) -> p e o", e=E).unsqueeze(1).to_broadcast(full)
                dve.tensor_tensor(gts[:, :, :, :], other, own, ALU.is_gt)
                linked(dve, dve.tensor_tensor(eqs[:, :, :, :], other, own, ALU.is_equal))
                early(7)
                linked(dve, dve.tensor_tensor(eqs[:, :, :, :], eqs[:, :, :, :], first, ALU.mult))
                early(8)
                linked(dve, dve.tensor_tensor(gts[:, :, :, :], gts[:, :, :, :], eqs[:, :, :, :], ALU.add))
                linked(dve, dve.tensor_reduce(rank[:, :, :], gts[:, :, :, :], AX.X, ALU.add))
                early(9)
                linked(dve, dve.scalar_tensor_tensor(comb[:, :, 0:E], rank[:, :, :], 2.0, pr[:, :, :], ALU.is_lt, ALU.mult))
                src = comb
                for i in range(PARTS):
                    dve.tensor_copy(cparts[:, :, i, :], src[:, :, :]).then_inc(s_cp, 1)
                    if i < PARTS - 1:
                        dve.wait_ge(s_cp, i + 1)
                        linked(dve, dve.tensor_tensor(comb_r[:, :, :], src[:, :, :], cparts[:, :, i, :], ALU.subtract))
                        src = comb_r
                early(10)
                dve.wait_ge(s_ct, 1)
                dve.tensor_copy(combT[:, :], PS[0:CROWS, 2:4, :].bitcast(bf16).rearrange("p b t -> p (b t)")).then_inc(s_cc, 1)
                for p, (c, f) in enumerate(PSTEPS):
                    if p == 0:
                        dve.wait_ge(hm_done, EARLY - 1)
                    routed(p, p % 2, p)
                    if p == 1:
                        early(EARLY - 1)
                        dve.wait_ge(hm_done, EARLY)
                    if p >= 2 and PSTEPS[p - 2][1] == AHEAD - 1:
                        first_sum(PSTEPS[p - 2][0])

                def body(f, filled, par, before, last):
                    for c in range(CHUNKS):
                        j = CHUNKS * f + c
                        gated(j, c % 2, c % 2)
                        dve.wait_ge(hm_done, j + 1)
                        routed(j, c % 2, c % 2)
                        if not (isinstance(j, int) and j - 2 < EARLY):
                            add_up(j - 2, (c - 2) % CHUNKS)
                        elif PSTEPS[j - 2][1] == AHEAD - 1:
                            first_sum(PSTEPS[j - 2][0])
                pair_loop(dve, body)
                def stats4(i):
                    dve.wait_ge(s_tr4, i + 1)
                    for t in range(QT):
                        ins = dve.bn_stats(st[0][:, QT * i + t, :], rows_ps(BANK4[i], t))
                    ins.then_inc(s_ag4, 1)
                    dve.wait_ge(s_ag4, 2 * i + 1)
                    for t in range(QT):
                        ins = dve.bn_aggr(mv[0][:, QT * i + t, :], st[0][:, QT * i + t, :])
                    ins.then_inc(s_ag4, 1)

                def scales4(i):
                    q = quarter(i)
                    dve.wait_ge(s_sd4, i + 1)
                    linked(dve, dve.reciprocal(rstd[0][:, q], std[0][:, q]))
                    linked(dve, dve.scalar_tensor_tensor(shf[2][:, q], mv[0][:, q, 0], -1.0, rstd[0][:, q],
                                                         ALU.mult, ALU.mult))
                    dve.tensor_tensor(shf[2][:, q], shf[2][:, q], shf[0][:, q], ALU.add).then_inc(s_f4, 1)

                stats4(0)
                add_up(END - 2, CHUNKS - 2)
                scales4(0)
                stats4(1)
                add_up(END - 1, CHUNKS - 1)
                scales4(1)
                stats4(2)
                scales4(2)
                stats4(3)
                scales4(3)
                for n in range(TILES - QT, TILES):
                    dve.scalar_tensor_tensor(xo[:, n, :], rows_ps(BANK4[CHUNKS - 1], n % QT), rstd[0][:, n:n + 1],
                                             x1[:, n, :], ALU.mult, ALU.add).then_inc(s_o4_last, 1)

            @block.gpsimd
            def _(pool):
                def split(f, buf, par):
                    pool.wait_ge(wfh_done, f + 1)
                    pool.tensor_tensor(wf_lo[:, buf, :], wf_raw[:, par, :], wf_hi[:, buf, :].bitcast(fp32),
                                       ALU.subtract).then_inc(wfl_done, 1)

                def low(j, c):
                    pool.wait_ge(hhi_done, j + 1)
                    pool.tensor_tensor(h_lo[:, c, :], hc[:, c % 2, :], h_hi[:, c, :].bitcast(fp32),
                                       ALU.subtract).then_inc(hlo_done, 1)

                split(0, BUF[0], 0)
                split(1, BUF[1], 1)
                split(2, BUF[2], 0)
                split(AHEAD, 1, 1)
                for p in range(EARLY):
                    low(p, p % CHUNKS)

                def body(f, filled, par, before, last):
                    for c in range(CHUNKS):
                        low(CHUNKS * f + c, c)
                        if c == 2 and not (isinstance(f, int) and f == FT - 1):
                            split(f + 1, 1 - par, 1 - par)
                pair_loop(pool, body)

                for i in range(CHUNKS - 1):
                    pool.wait_ge(s_sc4, QT * i + QT)
                    pool.tensor_tensor(xo[:, quarter(i), :], xo[:, quarter(i), :], x1[:, quarter(i), :], ALU.add).then_inc(s_o4, 1)


def kernel(L0_attn_hidden_states, L0_attn_in_proj_w, L0_attn_conv_w, L0_attn_conv_b, L0_attn_dt_bias,
           L0_attn_A_log, L0_attn_D, L0_attn_norm_w, L0_attn_out_proj_w, L0_ffn_gate_w, L0_ffn_expert_fc1,
           L0_ffn_expert_fc2, L0_ffn_expert_proj, L0_ffn_shared_fc1, L0_ffn_shared_fc2, L0_ffn_shared_proj,
           L0_ffn_shared_gate_w):
    import numpy as np
    import concourse.bacc as bacc
    from concourse import mybir as mb
    from concourse.bass_utils import run_bass_kernel_spmd

    G, CT, HID, INTER, GN, H = 8, 4, 256, 4096, 1024, 64
    E, F, FS, FT = 8, 176, 704, 17
    a = np.asarray
    x = a(L0_attn_hidden_states).reshape(-1, HID)
    w = a(L0_attn_in_proj_w)
    wz, wx, wB, wC, wdt = (w[i:j] for i, j in ((0, INTER), (INTER, 2 * INTER), (2 * INTER, 2 * INTER + GN),
                                               (2 * INTER + GN, 2 * INTER + 2 * GN), (2 * INTER + 2 * GN, w.shape[0])))

    def by_group(bcx, *rest):
        B, C, X = bcx
        return np.concatenate([v.reshape(G, -1, *rest) for v in (B, C, X)], axis=1)

    def k_major(v):
        n = v.shape[1]
        return v.transpose(0, 2, 1).reshape(v.shape[0], 2, 128, n).transpose(0, 2, 1, 3).reshape(v.shape[0], 128, 2 * n)

    cw, cb = a(L0_attn_conv_w), a(L0_attn_conv_b)
    bcx = lambda v: (v[INTER:INTER + GN], v[INTER + GN:], v[:INTER])
    tiles = lambda v, n: v.reshape(G, n, 128, -1).transpose(0, 2, 1, 3).reshape(G, 128, -1)
    par = np.concatenate([tiles(by_group(bcx(cw), 4), CT + 2), tiles(by_group(bcx(cb)), CT + 2),
                          tiles(np.repeat(a(L0_attn_D), INTER // H), CT), tiles(a(L0_attn_norm_w), CT)], axis=2)
    wo = a(L0_attn_out_proj_w).T.reshape(G, CT, 128, HID).transpose(0, 2, 1, 3).reshape(G, 128, CT * HID)
    pad = np.zeros((FT * 128 - E * F - FS, HID), np.float32)
    fc = [np.concatenate([a(e).reshape(E * F, HID), a(s), pad]).reshape(FT, 128, 2, 128) for e, s in
          ((L0_ffn_expert_fc1, L0_ffn_shared_fc1), (L0_ffn_expert_fc2, L0_ffn_shared_fc2))]
    w12 = np.stack(fc, axis=3).transpose(0, 4, 2, 3, 1).reshape(FT, 128, 512)
    wp = np.concatenate([a(L0_ffn_expert_proj).transpose(0, 2, 1).reshape(E * F, HID), a(L0_ffn_shared_proj).T, pad])
    wf = np.concatenate([w12, wp.reshape(FT, 128, HID)], axis=2)
    wg = np.concatenate([a(L0_ffn_gate_w), a(L0_ffn_shared_gate_w), np.zeros((1, HID), np.float32)])

    one = lambda v: np.asarray(v, np.float32)
    i, j = np.arange(128)[None, :], np.arange(128)[:, None]
    upper = one(j <= i)
    squares = np.concatenate([one(i == j), upper, -one(j > i)], axis=1)
    mask = np.concatenate([upper, np.ones((128, 128), np.float32), upper], axis=1)
    tie = np.tile(one(np.arange(E)[None, :] < np.arange(E)[:, None]).reshape(1, -1), (128, 1))
    after = one(np.arange(128)[None, None, :] > 64 * np.arange(2)[None, :, None] + np.arange(64)[:, None, None])
    after = np.stack([after, 0 * after, after], axis=2)
    l_const = np.concatenate([np.zeros((24, 768), np.float32), np.ones((3, 768), np.float32), after.reshape(64, -1)])
    r_const = np.concatenate([np.repeat(np.tile(-np.eye(8, dtype=np.float32), (3, 1)), 64, axis=1),
                              np.zeros((3, 512), np.float32),
                              np.tile(np.eye(64, dtype=np.float32) * np.float32(-2.0 ** 120), (1, 8))])
    route = np.concatenate([np.repeat(np.arange(E), F), np.full(FT * 128 - E * F, E)])
    f_hot = np.tile(one(np.arange(E + 1)[:, None] == route[None, :]), (3, 1))

    ins = dict(x=x, wx=k_major(by_group(bcx(np.concatenate([wx, wB, wC])), HID)), wz=k_major(wz.reshape(G, -1, HID)),
               wo=wo, par=par, wdt=k_major(wdt[None])[0], dtb=np.tile(a(L0_attn_dt_bias), (128, 1)),
               alog=np.tile(a(L0_attn_A_log), (128, 1)), wf=wf, wg=k_major(wg[None])[0], squares=squares, mask=mask,
               tie=tie, l_const=l_const, r_const=r_const, f_hot=f_hot)
    nc = bacc.Bacc("TRN2", target_bir_lowering=False, num_devices=1)
    arrays, aps = {}, []
    for name, v in ins.items():
        v = np.ascontiguousarray(v)
        arrays[f"in_{name}"] = v
        aps.append(nc.dram_tensor(f"in_{name}", v.shape, mb.dt.from_np(v.dtype), kind="ExternalInput").ap())
    aps.append(nc.dram_tensor("out", x.shape, mb.dt.float32, kind="ExternalOutput").ap())
    mamba_moe_sandwich_kernel(nc, *aps)
    r = run_bass_kernel_spmd(nc, [arrays], core_ids=[0])
    return r.results[0]["out"].reshape(a(L0_attn_hidden_states).shape)
```
